# Optimizing a Trainium2 kernel written in Bass

```python
import numpy as np
import jax
import jax.numpy as jnp

def _softmax(x, axis=-1):
    return jax.nn.softmax(x, axis=axis)

def _gelu(x):
    return jax.nn.gelu(x, approximate=True)

def _silu(x):
    return jax.nn.silu(x)

def _sigmoid(x):
    return jax.nn.sigmoid(x)

def _layernorm(x, axis=-1, eps=1e-05):
    m = jnp.mean(x, axis=axis, keepdims=True)
    v = jnp.var(x, axis=axis, keepdims=True)
    return (x - m) / jnp.sqrt(v + eps)

def _scatter_add(tgt, idx, src, axis=0):
    return tgt.at[idx].add(src)

def _segment_sum(src, seg, n):
    return jax.ops.segment_sum(src, seg, n)
kernel_name = 'mk_flamingo_gated_d1_seqx_r4_d47246'

def setup_inputs(seed: int=0):
    np.random.seed(seed)
    _w = jnp.asarray

    def _rec_inputs():
        import jax
        import jax.numpy as jnp
        _rk = jax.random.key(seed)
        x = -9.806e-05 + 1 * jax.random.normal(jax.random.fold_in(_rk, 1), (4, 1024, 256), jnp.float32)
        _lenS = 1024 - jax.random.randint(jax.random.fold_in(_rk, 7), (4,), 0, max(1, 1024 // 4) + 1, jnp.int32)
        _lenS2 = 64 - jax.random.randint(jax.random.fold_in(_rk, 8), (4,), 0, max(1, 64 // 4) + 1, jnp.int32)
        _ctx_1024P = jax.random.normal(jax.random.fold_in(_rk, 11), (4, 16, 256), jnp.float32)
        _ctx_1024c = jax.random.dirichlet(jax.random.fold_in(_rk, 511), 0.3 * jnp.ones((16,), jnp.float32), (4, 64))
        _ctx_1024t = jnp.einsum('bsk,bkd->bsd', _ctx_1024c, _ctx_1024P)
        _ctx_1024t = _ctx_1024t * jax.lax.rsqrt(jnp.mean(jnp.square(_ctx_1024t)) + 1e-12) * 0.953939
        ctx_1024 = -1.52775e-05 + 0.999936 * (_ctx_1024t + 0.3 * jax.random.normal(jax.random.fold_in(_rk, 611), (4, 64, 256), jnp.float32))
        _g = jax.random.normal(jax.random.fold_in(_rk, 9001), (2, 1), jnp.float32)
        _g = jnp.sign(_g) * jnp.maximum(jnp.abs(_g), 1.0) + (_g == 0) * 1.0
        g_xattn = _g[0]
        g_ffn = _g[1]
        return (x, ctx_1024, g_xattn, g_ffn)
    x, ctx_1024, g_xattn, g_ffn = _rec_inputs()

    def _L0_xattn_setup():
        import jax, jax.numpy as jnp
        import numpy as np
        D = 256
        NUM_ITERS = 3
        EPS = 1e-06
        SCALE = D ** (-0.5)

        def rmsnorm(x, w, eps=EPS):
            return x * jax.lax.rsqrt(jnp.mean(x * x, axis=-1, keepdims=True) + eps) * w

        def gru_cell(x, h, wih, whh, bih, bhh):
            gx = x @ wih.T + bih
            gh = h @ whh.T + bhh
            xr, xz, xn = jnp.split(gx, 3, axis=-1)
            hr, hz, hn = jnp.split(gh, 3, axis=-1)
            r = jax.nn.sigmoid(xr + hr)
            z = jax.nn.sigmoid(xz + hz)
            n = jnp.tanh(xn + r * hn)
            return (1.0 - z) * n + z * h
        key = jax.random.key(seed)
        ks = jax.random.split(key, 8)
        B, K, M, d = (8, 64, 1024, D)
        w_std = d ** (-0.5)
        return {'slots': jax.random.normal(ks[0], (B, K, d), jnp.float32), 'P': jax.random.normal(ks[1], (B, M, d), jnp.float32), 'Wq': jax.random.normal(ks[2], (d, d), jnp.float32) * w_std, 'Wk': jax.random.normal(ks[3], (d, d), jnp.float32) * w_std, 'Wv': jax.random.normal(ks[4], (d, d), jnp.float32) * w_std, 'gru_wih': jax.random.normal(ks[5], (3 * d, d), jnp.float32) * w_std, 'gru_whh': jax.random.normal(ks[6], (3 * d, d), jnp.float32) * w_std, 'gru_bih': jnp.zeros((3 * d,), jnp.float32), 'gru_bhh': jnp.zeros((3 * d,), jnp.float32), 'slot_norm_w': jnp.ones((d,), jnp.float32), 'input_norm_w': jnp.ones((d,), jnp.float32)}
    _L0_xattn_all = _L0_xattn_setup()
    _L0_xattn_in = {k: v for k, v in _L0_xattn_all.items() if k in ('Wq', 'Wk', 'Wv', 'gru_wih', 'gru_whh', 'gru_bih', 'gru_bhh', 'slot_norm_w', 'input_norm_w')}
    del _L0_xattn_all

    def _L0_ffn_setup():
        import jax, jax.numpy as jnp
        import numpy as np
        import math
        E = 16
        TOP_K = 2
        D = 256
        F = 1024
        SH = 512
        key = jax.random.key(seed)
        ks = jax.random.split(key, 10)
        s = lambda k, shape, fan: jax.random.normal(k, shape, jnp.float32) / np.sqrt(fan)
        return {'x': jax.random.normal(ks[0], (32, 64, D), jnp.float32), 'gate_w': s(ks[1], (E, D), D), 'up_w': s(ks[2], (E, F, D), D), 'up_b': s(ks[3], (E, F), D), 'gw': s(ks[4], (E, F, D), D), 'gb': s(ks[5], (E, F), D), 'down_w': s(ks[6], (E, D, F), F), 'down_b': s(ks[7], (E, D), F), 'sh_gate_w': s(ks[8], (SH, D), D), 'sh_up_w': s(ks[9], (SH, D), D), 'sh_down_w': s(jax.random.fold_in(key, 11), (D, SH), SH)}
    _L0_ffn_all = _L0_ffn_setup()
    _L0_ffn_in = {k: v for k, v in _L0_ffn_all.items() if k in ('gate_w', 'up_w', 'up_b', 'gw', 'gb', 'down_w', 'down_b', 'sh_gate_w', 'sh_up_w', 'sh_down_w')}
    del _L0_ffn_all
    return {'x': x, 'ctx_1024': ctx_1024, 'g_xattn': g_xattn, 'g_ffn': g_ffn, 'L0_xattn_Wq': _L0_xattn_in['Wq'], 'L0_xattn_Wk': _L0_xattn_in['Wk'], 'L0_xattn_Wv': _L0_xattn_in['Wv'], 'L0_xattn_gru_wih': _L0_xattn_in['gru_wih'], 'L0_xattn_gru_whh': _L0_xattn_in['gru_whh'], 'L0_xattn_gru_bih': _L0_xattn_in['gru_bih'], 'L0_xattn_gru_bhh': _L0_xattn_in['gru_bhh'], 'L0_xattn_slot_norm_w': _L0_xattn_in['slot_norm_w'], 'L0_xattn_input_norm_w': _L0_xattn_in['input_norm_w'], 'L0_ffn_gate_w': _L0_ffn_in['gate_w'], 'L0_ffn_up_w': _L0_ffn_in['up_w'], 'L0_ffn_up_b': _L0_ffn_in['up_b'], 'L0_ffn_gw': _L0_ffn_in['gw'], 'L0_ffn_gb': _L0_ffn_in['gb'], 'L0_ffn_down_w': _L0_ffn_in['down_w'], 'L0_ffn_down_b': _L0_ffn_in['down_b'], 'L0_ffn_sh_gate_w': _L0_ffn_in['sh_gate_w'], 'L0_ffn_sh_up_w': _L0_ffn_in['sh_up_w'], 'L0_ffn_sh_down_w': _L0_ffn_in['sh_down_w']}

def reference(x, ctx_1024, g_xattn, g_ffn, L0_xattn_Wq, L0_xattn_Wk, L0_xattn_Wv, L0_xattn_gru_wih, L0_xattn_gru_whh, L0_xattn_gru_bih, L0_xattn_gru_bhh, L0_xattn_slot_norm_w, L0_xattn_input_norm_w, L0_ffn_gate_w, L0_ffn_up_w, L0_ffn_up_b, L0_ffn_gw, L0_ffn_gb, L0_ffn_down_w, L0_ffn_down_b, L0_ffn_sh_gate_w, L0_ffn_sh_up_w, L0_ffn_sh_down_w):
    import jax
    import jax.numpy as jnp

    def _L0_xattn_ref(slots, P, Wq, Wk, Wv, gru_wih, gru_whh, gru_bih, gru_bhh, slot_norm_w, input_norm_w):
        import jax, jax.numpy as jnp
        import numpy as np
        D = 256
        NUM_ITERS = 3
        EPS = 1e-06
        SCALE = D ** (-0.5)

        def rmsnorm(x, w, eps=EPS):
            return x * jax.lax.rsqrt(jnp.mean(x * x, axis=-1, keepdims=True) + eps) * w

        def gru_cell(x, h, wih, whh, bih, bhh):
            gx = x @ wih.T + bih
            gh = h @ whh.T + bhh
            xr, xz, xn = jnp.split(gx, 3, axis=-1)
            hr, hz, hn = jnp.split(gh, 3, axis=-1)
            r = jax.nn.sigmoid(xr + hr)
            z = jax.nn.sigmoid(xz + hz)
            n = jnp.tanh(xn + r * hn)
            return (1.0 - z) * n + z * h
        Pn = rmsnorm(P, input_norm_w)
        k_proj = Pn @ Wk.T
        v_proj = Pn @ Wv.T
        for _ in range(NUM_ITERS):
            sn = rmsnorm(slots, slot_norm_w)
            q_proj = sn @ Wq.T
            scores = jnp.einsum('bkd,bmd->bkm', q_proj, k_proj) * SCALE
            attn = jax.nn.softmax(scores, axis=-2)
            attn = attn / (jnp.sum(attn, axis=-1, keepdims=True) + EPS)
            updates = jnp.einsum('bkm,bmd->bkd', attn, v_proj)
            slots = gru_cell(updates, slots, gru_wih, gru_whh, gru_bih, gru_bhh)
        return slots

    def _L0_ffn_ref(x, gate_w, up_w, up_b, gw, gb, down_w, down_b, sh_gate_w, sh_up_w, sh_down_w):
        import jax, jax.numpy as jnp
        import numpy as np
        import math
        E = 16
        TOP_K = 2
        D = 256
        F = 1024
        SH = 512
        B, S, Dm = x.shape
        h = x.reshape(-1, Dm)
        T = h.shape[0]
        scores = jax.nn.sigmoid(h @ gate_w.T)
        cap = math.ceil(T / E * TOP_K)
        topk_score, topk_ids = jax.lax.top_k(scores.T, cap)
        xin = h[topk_ids]
        up = jnp.einsum('ecd,efd->ecf', xin, up_w) + up_b[:, None, :]
        g = jnp.einsum('ecd,efd->ecf', xin, gw) + gb[:, None, :]
        eo = jax.nn.silu(g) * up
        eo = jnp.einsum('ecf,edf->ecd', eo, down_w) + down_b[:, None, :]
        flat = (eo * topk_score[..., None]).reshape(-1, Dm)
        out = jnp.zeros_like(h).at[topk_ids.reshape(-1)].add(flat)
        out = out.reshape(B, S, Dm)
        shared = jax.nn.silu(jnp.einsum('bsd,fd->bsf', x, sh_gate_w)) * jnp.einsum('bsd,fd->bsf', x, sh_up_w)
        shared = jnp.einsum('bsf,df->bsd', shared, sh_down_w)
        return out + shared
    x = x + jnp.tanh(g_xattn[0]) * _L0_xattn_ref(_layernorm(x, axis=-1), ctx_1024, L0_xattn_Wq, L0_xattn_Wk, L0_xattn_Wv, L0_xattn_gru_wih, L0_xattn_gru_whh, L0_xattn_gru_bih, L0_xattn_gru_bhh, L0_xattn_slot_norm_w, L0_xattn_input_norm_w)
    x = x + jnp.tanh(g_ffn[0]) * _L0_ffn_ref(_layernorm(x, axis=-1), L0_ffn_gate_w, L0_ffn_up_w, L0_ffn_up_b, L0_ffn_gw, L0_ffn_gb, L0_ffn_down_w, L0_ffn_down_b, L0_ffn_sh_gate_w, L0_ffn_sh_up_w, L0_ffn_sh_down_w)
    return x

_drawn_inputs = setup_inputs


def setup_inputs(seed=0):
    import zlib

    import numpy as np

    out = dict(_drawn_inputs(seed))
    spreads = {'L0_xattn_gru_bih': (0.0, 0.1),
     'L0_xattn_gru_bhh': (0.0, 0.1),
     'L0_xattn_slot_norm_w': (1.0, 0.2),
     'L0_xattn_input_norm_w': (1.0, 0.2)}
    factors = {}
    for name, (base, spread) in spreads.items():
        noise = np.random.default_rng([zlib.crc32(name.encode()), seed]).standard_normal(out[name].shape)
        drawn = base * np.exp(spread * noise) if base else spread * noise
        out[name] = jnp.asarray(drawn.astype(out[name].dtype))
    for name, factor in factors.items():
        out[name] = (out[name] * factor).astype(out[name].dtype)
    return out
```

```python
import concourse.bass as bass
from concourse import mybir
from contextlib import ExitStack

F32 = mybir.dt.float32
F32R = mybir.dt.float32r
F16 = mybir.dt.float16
I32 = mybir.dt.int32
U32 = mybir.dt.uint32
ALU = mybir.AluOpType
ACT = mybir.ActivationFunctionType
AX = mybir.AxisListType.X

P = 128
GROUP = 512
BLK = GROUP // P
RSQRT_MAGIC = 0x5F3759DF


class Steps:

    def __init__(self, eng, sem, done=0):
        self.eng, self.sem, self.n = eng, sem, done

    def add(self, ins):
        ins.then_inc(self.sem, 1)
        self.n += 1

    def wait(self):
        self.eng.wait_ge(self.sem, self.n)

    def do(self, ins):
        self.add(ins)
        self.wait()


def rsqrt_steps(dve, do, y, v, t):
    do(dve.tensor_scalar(t.bitcast(I32), v.bitcast(I32), 1, None, ALU.logical_shift_right))
    do(dve.tensor_scalar(y.bitcast(I32), t.bitcast(I32), -1.0, float(RSQRT_MAGIC), ALU.mult, ALU.add))
    for _ in range(3):
        do(dve.scalar_tensor_tensor(t, y, -0.5, y, ALU.mult, ALU.mult))
        do(dve.tensor_tensor(t, t, v, ALU.mult))
        do(dve.scalar_tensor_tensor(y, t, 1.5, y, ALU.add, ALU.mult))


def flamingo_kernel(nc, x, ctx_tok, g_xattn, g_ffn, wq, wk_t, wv_t, wih_t, whh_t, bih, bhh, slot_w, input_w,
                    gate_t, w_expert, gate_b, up_b, down_b, w_shared, out):
    T, D = x.shape
    M = ctx_tok.shape[0]
    B = 4
    MB = M // B
    KC = D // P
    G = T // GROUP
    NT = T // P
    PAIRS = B // 2
    GPP = G // PAIRS
    ITERS = 3
    SCALE = float(D) ** -0.5
    RMS_EPS, LN_EPS, ATTN_EPS = 1e-6, 1e-5, 1e-6
    assert KC == 2 and MB == 64 and T // B == 2 * GROUP and GPP == 4

    with ExitStack() as whole:
        def tensors(stack):
            def sb(name, shape, dt=F32):
                return stack.enter_context(nc.sbuf_tensor(name, shape, dt))

            def ps(name, shape, dt=F32):
                return stack.enter_context(nc.psum_tensor(name, shape, dt))
            return sb, ps

        def sem(name):
            return whole.enter_context(nc.semaphore(name))

        sb, ps = tensors(whole)
        ident = sb("ident", [P, P])
        tanh_g = sb("tanh_g", [P, 2])

        state = ExitStack()
        ssb, _ = tensors(state)
        slots = ssb("slots", [P, KC, T])
        slots_hi = ssb("slots_hi", [P, KC, T], F32R)
        slots_lo = ssb("slots_lo", [P, KC, T], F32R)
        attention = ExitStack()
        asb, aps = tensors(attention)
        whh_hi = asb("whh_hi", [P, KC, 3 * D], F32R)
        whh_lo = asb("whh_lo", [P, KC, 3 * D], F32R)
        vw_hi = asb("vw_hi", [P, PAIRS, 3 * D], F32R)
        vw_lo = asb("vw_lo", [P, PAIRS, 3 * D], F32R)
        kq_hi = asb("kq_hi", [P, KC, B, P], F32R)
        kq_lo = asb("kq_lo", [P, KC, B, P], F32R)
        square = asb("square", [P, 2, KC, GROUP])
        ones_half = asb("ones_half", [P, 2, P])
        half_mask = asb("half_mask", [P, P])
        ones_col = asb("ones_col", [P, 1])
        attn_eps = asb("attn_eps", [P, 1])
        half_b_rz = asb("half_b_rz", [P, 4])
        b_xn = asb("b_xn", [P, 2])
        half_b_hn = asb("half_b_hn", [P, 2])
        ssq = aps("ssq", [P, 512])

        s_hi = sem("s_hi")
        s_lo = sem("s_lo")
        s_sqk = sem("s_sqk")
        s_sq = sem("s_sq")
        s_ss = sem("s_ss")

        def sum_squares(pe, run, pair, g4, wait_read=None):
            pe.wait_ge(s_sq, run + 1)
            if wait_read is not None:
                pe.wait_ge(*wait_read)
            for blk in range(BLK):
                col = (pair * GPP + g4) * BLK + blk
                last = nc.tensor.matmul(ssq[:, col:col + 1], square[:, g4 % 2, 0, blk * P:(blk + 1) * P],
                                        ones_col[:, :], start=True, stop=True)
            last.then_inc(s_ss, 1)

        def squares(pool, g, run):
            sq = square[:, g % 2, :, :]
            sl = slice(g * GROUP, (g + 1) * GROUP)
            nc.gpsimd.tensor_tensor(sq, slots[:, :, sl], slots[:, :, sl], ALU.mult).then_inc(s_sqk, 1)
            pool.wait_ge(s_sqk, run + 1)
            nc.gpsimd.tensor_tensor(sq[:, 0, :], sq[:, 0, :], sq[:, 1, :], ALU.add).then_inc(s_sq, 1)

        with ExitStack() as setup:
            lsb, lps = tensors(setup)
            xs = lsb("xs", [P, NT, D])
            ctx_sb = lsb("ctx_sb", [P, M // P, D])
            ctx_sq = lsb("ctx_sq", [P, M // P, D])
            wq_sb = lsb("wq_sb", [P, KC, D])
            wk_sb = lsb("wk_sb", [P, KC, D])
            wv_sb = lsb("wv_sb", [P, KC, D])
            wih_sb = lsb("wih_sb", [P, KC, 3 * D])
            whh_sb = lsb("whh_sb", [P, KC, 3 * D])
            vecs = lsb("vecs", [P, 16])
            g_in = lsb("g_in", [P, 2])
            pn_t = lsb("pn_t", [P, KC, M])
            kp_t = lsb("kp_t", [P, KC, M])
            vp_t = lsb("vp_t", [P, KC, M])
            kq_f = lsb("kq_f", [P, KC, M])
            vw_f = lsb("vw_f", [P, PAIRS, 3 * D])
            stats = lsb("stats", [P, NT, 6])
            mv = lsb("mv", [P, NT, 2])
            var = lsb("var", [P, NT + 2])
            rstd = lsb("rstd", [P, NT + 2])
            rtmp = lsb("rtmp", [P, NT + 2])
            csum = lsb("csum", [P, 2])
            bank = lps("bank", [P, 3, 512])
            turn = lps("turn", [P, 2, KC, GROUP])

            l_ctx, l_wk, l_wv, l_wq, l_wih, l_whh, l_vec, l_g = (
                sem(f"loaded_{n}") for n in ("ctx", "wk", "wv", "wq", "wih", "whh", "vec", "g"))
            l_x = [sem(f"loaded_x{g}") for g in range(G)]
            c_pool = sem("const_pool")
            c_act = sem("ctx_squares")
            v0 = sem("vector_setup")
            t_pn = sem("t_pn")
            w_pn = sem("w_pn")
            m_w = sem("m_w")
            e_w = sem("e_w")
            n_x = sem("n_x")
            t_x = sem("t_x")
            s_s0 = sem("s_s0")

            block = setup.enter_context(nc.Block())

            @block.sync
            def _(sp):
                sp.dma_start(ctx_sb[:, :, :], ctx_tok.rearrange("(t p) d -> p t d", p=P)).then_inc(l_ctx, 16)
                for dst, src, s in ((wk_sb, wk_t, l_wk), (wv_sb, wv_t, l_wv), (wq_sb, wq, l_wq)):
                    sp.dma_start(dst[:, :, :], src.rearrange("(k p) n -> p k n", p=P)).then_inc(s, 16)
                xv = x.rearrange("(g b p) d -> g p b d", b=BLK, p=P)
                for g in range(0, G, 2):
                    sp.dma_start(xs[:, g * BLK:(g + 1) * BLK, :], xv[g]).then_inc(l_x[g], 16)

            @block.scalar
            def _(act):
                act.dma_start(vecs[:, 0:6], bih).then_inc(l_vec, 16)
                act.dma_start(vecs[:, 6:12], bhh).then_inc(l_vec, 16)
                act.dma_start(vecs[:, 12:14], slot_w).then_inc(l_vec, 16)
                act.dma_start(vecs[:, 14:16], input_w).then_inc(l_vec, 16)
                act.dma_start(g_in[:, 0:1], g_xattn.rearrange("(a n) -> a n", a=1).to_broadcast([P, 1])).then_inc(l_g, 16)
                act.dma_start(g_in[:, 1:2], g_ffn.rearrange("(a n) -> a n", a=1).to_broadcast([P, 1])).then_inc(l_g, 16)
                xv = x.rearrange("(g b p) d -> g p b d", b=BLK, p=P)
                for g in range(1, G, 2):
                    act.dma_start(xs[:, g * BLK:(g + 1) * BLK, :], xv[g]).then_inc(l_x[g], 16)
                act.dma_start(wih_sb[:, :, :], wih_t.rearrange("(k p) n -> p k n", p=P)).then_inc(l_wih, 16)
                act.dma_start(whh_sb[:, :, :], whh_t.rearrange("(k p) n -> p k n", p=P)).then_inc(l_whh, 16)
                act.wait_ge(l_ctx, 16)
                for t in range(M // P):
                    nc.scalar.activation(ctx_sq[:, t, :], ctx_sb[:, t, :], ACT.Square,
                                         accum_out=csum[:, t:t + 1]).then_inc(c_act, 1)
                act.wait_ge(l_g, 32)
                nc.scalar.activation(tanh_g[:, :], g_in[:, :], ACT.Tanh).then_inc(c_act, 1)
                for g in range(G):
                    act.wait_ge(t_x, g + 1)
                    sl = slice(g * GROUP, (g + 1) * GROUP)
                    nc.scalar.activation(slots[:, :, sl], turn[:, g % 2, :, :], ACT.Copy).then_inc(s_s0, 1)
                    nc.scalar.activation(slots_hi[:, :, sl], turn[:, g % 2, :, :], ACT.Copy).then_inc(s_hi, 1)

            @block.gpsimd
            def _(pool):
                nc.gpsimd.memset(ident[:, :], 0.0).then_inc(c_pool, 1)
                nc.gpsimd.memset(ones_half[:, :, :], 0.0).then_inc(c_pool, 1)
                nc.gpsimd.memset(half_mask[:, :], 0.0).then_inc(c_pool, 1)
                nc.gpsimd.memset(kq_hi[:, :, :, :].bitcast(F32), 0.0).then_inc(c_pool, 1)
                nc.gpsimd.memset(kq_lo[:, :, :, :].bitcast(F32), 0.0).then_inc(c_pool, 1)
                pool.wait_ge(c_pool, 5)
                nc.gpsimd.affine_select(out=ident[:, :], in_=ident[:, :], compare_op=ALU.not_equal, fill=1.0,
                                        base=0, pattern=[[-1, P]], channel_multiplier=1).then_inc(c_pool, 1)
                nc.gpsimd.memset(ones_half[:, 0, 0:MB], 1.0).then_inc(c_pool, 1)
                nc.gpsimd.memset(ones_half[:, 1, MB:P], 1.0).then_inc(c_pool, 1)
                nc.gpsimd.memset(half_mask[0:MB, 0:MB], 1.0).then_inc(c_pool, 1)
                nc.gpsimd.memset(ones_col[:, :], 1.0).then_inc(c_pool, 1)
                nc.gpsimd.memset(attn_eps[:, :], ATTN_EPS).then_inc(c_pool, 1)
                pool.wait_ge(c_pool, 11)
                nc.gpsimd.memset(half_mask[MB:P, MB:P], 1.0).then_inc(c_pool, 1)
                pool.wait_ge(c_pool, 12)
                for g in range(G):
                    pool.wait_ge(s_s0, g + 1)
                    if g >= 2:
                        pool.wait_ge(s_ss, g - 1)
                    sl = slice(g * GROUP, (g + 1) * GROUP)
                    squares(pool, g, g)

            @block.tensor
            def _(pe):
                pe.wait_ge(c_pool, 12)
                pe.wait_ge(v0, V_PN)
                for t in range(M // P):
                    for k in range(KC):
                        last = nc.tensor.transpose(bank[:, 0, k * M + t * P:k * M + (t + 1) * P],
                                                   ctx_sb[:, t, k * P:(k + 1) * P], ident[:, :])
                last.then_inc(t_pn, 1)
                pe.wait_ge(w_pn, 1)
                for w, (l, n) in enumerate(((wk_sb, l_wk), (wv_sb, l_wv))):
                    pe.wait_ge(n, 16)
                    for j in range(KC):
                        for k in range(KC):
                            last = nc.tensor.matmul(bank[:, 1 + w, j * M:(j + 1) * M], l[:, k, j * P:(j + 1) * P],
                                                    pn_t[:, k, :], start=(k == 0), stop=(k == KC - 1))
                    last.then_inc(m_w, 1)
                pe.wait_ge(e_w, 1)
                pe.wait_ge(l_wq, 16)
                for j in range(KC):
                    for k in range(KC):
                        last = nc.tensor.matmul(bank[:, 0, j * M:(j + 1) * M], wq_sb[:, k, j * P:(j + 1) * P],
                                                kp_t[:, k, :], start=(k == 0), stop=(k == KC - 1))
                last.then_inc(m_w, 1)
                pe.wait_ge(l_wih, 16)
                W = 3 * D // 2
                for n in range(2 * PAIRS):
                    pe.wait_ge(e_w, 2 + n if n else 2)
                    for k in range(KC):
                        last = nc.tensor.matmul(bank[:, (1, 2, 0, 1)[n], 0:W], vp_t[:, k, (n // 2) * P:(n // 2 + 1) * P],
                                                wih_sb[:, k, (n % 2) * W:(n % 2 + 1) * W],
                                                start=(k == 0), stop=(k == KC - 1))
                    last.then_inc(m_w, 1)
                for g in range(G):
                    pe.wait_ge(n_x, (g + 1) * BLK)
                    if g >= 2:
                        pe.wait_ge(s_hi, g - 1)
                    for blk in range(BLK):
                        for k in range(KC):
                            last = nc.tensor.transpose(turn[:, g % 2, k, blk * P:(blk + 1) * P],
                                                       xs[:, g * BLK + blk, k * P:(k + 1) * P], ident[:, :])
                    last.then_inc(t_x, 1)
                    if g >= 1:
                        sum_squares(pe, g - 1, (g - 1) // GPP, (g - 1) % GPP)

            @block.vector
            def _(dve):
                st = Steps(dve, v0)
                dve.wait_ge(c_act, 2)
                st.do(nc.vector.tensor_scalar(var[:, NT:NT + 2], csum[:, :], 1.0 / D, RMS_EPS, ALU.mult, ALU.add))
                rsqrt_steps(nc.vector, st.do, rstd[:, NT:NT + 2], var[:, NT:NT + 2], rtmp[:, NT:NT + 2])
                for t in range(M // P):
                    st.add(nc.vector.tensor_scalar(ctx_sb[:, t, :], ctx_sb[:, t, :], rstd[:, NT + t:NT + t + 1],
                                                   None, ALU.mult))
                assert st.n == V_PN
                for g in range(G):
                    dve.wait_ge(l_x[g], 16)
                    for t in range(g * BLK, (g + 1) * BLK):
                        st.add(nc.vector.bn_stats(stats[:, t, :], xs[:, t, :]))
                    if g == 0:
                        dve.wait_ge(l_vec, 64)
                        dve.wait_ge(t_pn, 1)
                        for k in range(KC):
                            last = nc.vector.tensor_scalar(pn_t[:, k, :], bank[:, 0, k * M:(k + 1) * M],
                                                           vecs[:, 14 + k:15 + k], None, ALU.mult)
                        last.then_inc(w_pn, 1)
                st.wait()
                for t in range(NT):
                    st.add(nc.vector.bn_aggr(mv[:, t, :], stats[:, t, :]))
                st.wait()
                st.do(nc.vector.tensor_scalar(var[:, 0:NT], mv[:, :, 1], LN_EPS, None, ALU.add))
                rsqrt_steps(nc.vector, st.do, rstd[:, 0:NT], var[:, 0:NT], rtmp[:, 0:NT])

                def normalise(g):
                    for t in range(g * BLK, (g + 1) * BLK):
                        nc.vector.tensor_scalar(xs[:, t, :], xs[:, t, :], mv[:, t, 0:1], rstd[:, t:t + 1],
                                                ALU.subtract, ALU.mult).then_inc(n_x, 1)

                normalise(0)
                dve.wait_ge(m_w, 1)
                nc.vector.tensor_copy(kp_t[:, :, :], bank[:, 1, :]).then_inc(e_w, 1)
                dve.wait_ge(m_w, 2)
                nc.vector.tensor_copy(vp_t[:, :, :], bank[:, 2, :]).then_inc(e_w, 1)
                normalise(1)
                dve.wait_ge(m_w, 3)
                for k in range(KC):
                    last = nc.vector.tensor_scalar(kq_f[:, k, :], bank[:, 0, k * M:(k + 1) * M],
                                                   vecs[:, 12 + k:13 + k], SCALE, ALU.mult, ALU.mult)
                last.then_inc(e_w, 1)
                W = 3 * D // 2
                for n in range(2 * PAIRS):
                    dve.wait_ge(m_w, 4 + n)
                    nc.vector.tensor_copy(vw_f[:, n // 2, (n % 2) * W:(n % 2 + 1) * W],
                                          bank[:, (1, 2, 0, 1)[n], 0:W]).then_inc(e_w, 1)
                dve.wait_ge(e_w, 3 + 2 * PAIRS)
                dve.wait_ge(l_whh, 16)
                dve.wait_ge(c_pool, 12)
                kq_v = kq_f[:, :, :].rearrange("p k (b m) -> p k b m", b=B)
                for b in range(B):
                    lo = (b % 2) * MB
                    st.add(nc.vector.tensor_copy(kq_hi[:, :, b, lo:lo + MB], kq_v[:, :, b, :]))
                st.add(nc.vector.tensor_copy(vw_hi[:, :, :], vw_f[:, :, :]))
                st.add(nc.vector.tensor_copy(whh_hi[:, :, :], whh_sb[:, :, :]))
                st.wait()
                for b in range(B):
                    lo = (b % 2) * MB
                    st.add(nc.vector.tensor_tensor(kq_lo[:, :, b, lo:lo + MB], kq_v[:, :, b, :],
                                                   kq_hi[:, :, b, lo:lo + MB].bitcast(F32), ALU.subtract))
                st.add(nc.vector.tensor_tensor(vw_lo[:, :, :], vw_f[:, :, :], vw_hi[:, :, :].bitcast(F32), ALU.subtract))
                st.add(nc.vector.tensor_tensor(whh_lo[:, :, :], whh_sb[:, :, :], whh_hi[:, :, :].bitcast(F32),
                                               ALU.subtract))
                st.add(nc.vector.tensor_tensor(half_b_rz[:, :], vecs[:, 0:4], vecs[:, 6:10], ALU.add))
                st.add(nc.vector.tensor_copy(b_xn[:, :], vecs[:, 4:6]))
                st.add(nc.vector.tensor_scalar(half_b_hn[:, :], vecs[:, 10:12], 0.5, None, ALU.mult))
                st.wait()
                st.do(nc.vector.tensor_scalar(half_b_rz[:, :], half_b_rz[:, :], 0.5, None, ALU.mult))
                for g in range(G):
                    if g + 2 < G:
                        normalise(g + 2)
                    dve.wait_ge(s_hi, g + 1)
                    sl = slice(g * GROUP, (g + 1) * GROUP)
                    nc.vector.tensor_tensor(slots_lo[:, :, sl], slots[:, :, sl], slots_hi[:, :, sl].bitcast(F32),
                                            ALU.subtract).then_inc(s_lo, 1)
        with ExitStack() as loop:
            lsb, lps = tensors(loop)
            tr = lsb("tr", [P, KC, GROUP])
            tz = lsb("tz", [P, KC, GROUP])
            hb = lsb("hb", [P, KC, GROUP])
            nn = lsb("nn", [P, KC, GROUP])
            pre = lsb("pre", [P, GROUP])
            dif = lsb("dif", [P, GROUP])
            expo = lsb("expo", [P, 2 * GROUP])
            rms_c = lsb("rms_c", [P, 2, GROUP])
            csum_c = lsb("csum_c", [P, 2, GROUP])
            attn_hi = lsb("attn_hi", [P, PAIRS, 2 * GROUP], F32R)
            attn_lo = lsb("attn_lo", [P, PAIRS, 2 * GROUP], F32R)
            diag = lsb("diag", [P, GPP * BLK, P])
            rsum = lsb("rsum", [P, P])
            ms = lsb("ms", [P, GPP * BLK])
            rms = lsb("rms", [P, GPP * BLK])
            rms_t = lsb("rms_t", [P, GPP * BLK])
            top = lsb("top", [P, 1])
            neg_top = lsb("neg_top", [P, 1])
            den = lsb("den", [P, 1])
            rden = lsb("rden", [P, 1])

            gate_r = lps("gate_r", [P, GROUP])
            gate_z = lps("gate_z", [P, GROUP])
            gate_h = lps("gate_h", [P, GROUP])
            gate_x = lps("gate_x", [P, GROUP])
            rms_b = lps("rms_b", [P, GROUP])
            score = lps("score", [P, 2, GROUP])

            m_r, m_z, m_h, m_x = (sem(f"m_{n}") for n in "rzhx")
            a_r, a_z, a_h, a_n = (sem(f"a_{n}") for n in "rzhn")
            v_q = sem("v_q")
            v_pre, v_dif, v_mix, v_new = (sem(f"v_{n}") for n in ("pre", "dif", "mix", "new"))
            v_ms = sem("v_ms")
            v_rms = sem("v_rms")
            v_diag = sem("v_diag")
            m_score, m_rms, m_csum = sem("m_score"), sem("m_rms"), sem("m_csum")
            a_rms, a_csum = sem("a_rms"), sem("a_csum")
            v_mul, v_top, v_neg, a_exp, v_rden, v_rsum = (sem(n) for n in
                                                          ("v_mul", "v_top", "v_neg", "a_exp", "v_rden", "v_rsum"))
            v_rec, v_attn, a_attn, v_alo = sem("v_rec"), sem("v_attn"), sem("a_attn"), sem("v_alo")
            RMS_STEPS = 12
            UNITS = 2 * G

            def tokens(pair, g4):
                g = pair * GPP + g4
                return slice(g * GROUP, (g + 1) * GROUP)

            block = loop.enter_context(nc.Block())

            @block.tensor
            def _(pe):
                def gru_unit(it, pair, g4, c):
                    u = it * UNITS + (pair * GPP + g4) * 2 + c
                    sl = tokens(pair, g4)
                    rows = slice((g4 // 2) * MB, (g4 // 2 + 1) * MB)
                    half = slice((g4 % 2) * GROUP, (g4 % 2 + 1) * GROUP)
                    if c == 0:
                        pe.wait_ge(s_hi, it * G + pair * GPP + g4 + 1)
                        pe.wait_ge(s_lo, it * G + pair * GPP + g4 + 1)

                    def from_slots(out, f, stop):
                        n = 0
                        for k in range(KC):
                            for w, s in ((whh_hi, slots_hi), (whh_hi, slots_lo), (whh_lo, slots_hi)):
                                n += 1
                                last = nc.tensor.matmul(out[:, :], w[:, k, f * P:(f + 1) * P], s[:, k, sl],
                                                        start=(n == 1), stop=(stop and n == 3 * KC))
                        return last

                    def from_attention(out, f, start):
                        for n, (w, a) in enumerate(((vw_hi, attn_hi), (vw_hi, attn_lo), (vw_lo, attn_hi))):
                            last = nc.tensor.matmul(out[:, :], w[rows, pair, f * P:(f + 1) * P],
                                                    a[rows, pair, half], start=(start and n == 0), stop=(n == 2))
                        return last

                    pe.wait_ge(a_r, u + 1)
                    from_slots(gate_r, c, False)
                    if c == 0:
                        pe.wait_ge(a_attn, 4 * it + 2 * pair + g4 % 2 + 1)
                        pe.wait_ge(v_alo, 4 * it + 2 * pair + g4 % 2 + 1)
                    from_attention(gate_r, c, False).then_inc(m_r, 1)
                    pe.wait_ge(a_z, u + 1)
                    from_slots(gate_z, 2 + c, False)
                    from_attention(gate_z, 2 + c, False).then_inc(m_z, 1)
                    pe.wait_ge(a_h, u + 1)
                    from_slots(gate_h, 4 + c, True).then_inc(m_h, 1)
                    pe.wait_ge(v_pre, u + 1)
                    from_attention(gate_x, 4 + c, True).then_inc(m_x, 1)

                def scores(s, pair):
                    for h in range(2):
                        n = 0
                        for b in range(2):
                            sl = tokens(pair, 2 * b + h)
                            for k in range(KC):
                                for w, x_ in ((kq_hi, slots_hi), (kq_hi, slots_lo), (kq_lo, slots_hi)):
                                    n += 1
                                    last = nc.tensor.matmul(score[:, h, :], w[:, k, 2 * pair + b, :], x_[:, k, sl],
                                                            start=(n == 1), stop=(n == 6 * KC))
                        last.then_inc(m_score, 1)

                def spread_rms(s, h):
                    if h == 0:
                        pe.wait_ge(v_diag, s + 1)
                    else:
                        pe.wait_ge(a_rms, 2 * s + 1)
                    for blk in range(BLK):
                        for b in range(2):
                            last = nc.tensor.matmul(rms_b[:, blk * P:(blk + 1) * P], ones_half[:, b, :],
                                                    diag[:, (2 * b + h) * BLK + blk, :], start=(b == 0), stop=(b == 1))
                    last.then_inc(m_rms, 1)

                def column_sums(s):
                    pe.wait_ge(v_rsum, s + 1)
                    for h in range(2):
                        nc.tensor.matmul(score[:, h, :], rsum[:, :], expo[:, h * GROUP:(h + 1) * GROUP],
                                         start=True, stop=True).then_inc(m_csum, 1)

                def half_iteration(it, pair, softmax, more):
                    s = 2 * it + pair + 1
                    first_run = G * it + GPP * pair + G
                    gru_unit(it, pair, 0, 0)
                    gru_unit(it, pair, 0, 1)
                    if softmax:
                        sum_squares(pe, first_run - 1, 1 - pair, GPP - 1, (v_ms, s))
                        pe.wait_ge(s_hi, first_run)
                        pe.wait_ge(s_lo, first_run)
                        scores(s, 1 - pair)
                    gru_unit(it, pair, 1, 0)
                    if softmax:
                        spread_rms(s, 0)
                    gru_unit(it, pair, 1, 1)
                    if softmax:
                        spread_rms(s, 1)
                    if more:
                        sum_squares(pe, first_run, pair, 0, (v_ms, s + 1))
                    gru_unit(it, pair, 2, 0)
                    gru_unit(it, pair, 2, 1)
                    if softmax:
                        column_sums(s)
                    if more:
                        sum_squares(pe, first_run + 1, pair, 1, (v_ms, s + 1))
                    gru_unit(it, pair, 3, 0)
                    gru_unit(it, pair, 3, 1)
                    if more:
                        sum_squares(pe, first_run + 2, pair, 2, (v_ms, s + 1))

                scores(0, 0)
                spread_rms(0, 0)
                spread_rms(0, 1)
                column_sums(0)
                with pe.Fori(0, ITERS - 1) as it:
                    half_iteration(it, 0, True, True)
                    half_iteration(it, 1, True, True)
                half_iteration(ITERS - 1, 0, True, False)
                half_iteration(ITERS - 1, 1, False, False)

            @block.scalar
            def _(act):
                def gru_unit(it, pair, g4, c, meanwhile=None):
                    u = it * UNITS + (pair * GPP + g4) * 2 + c
                    act.wait_ge(v_q, u + 2)
                    act.wait_ge(m_r, u + 1)
                    nc.scalar.activation(tr[:, c, :], gate_r[:, :], ACT.Tanh, bias=half_b_rz[:, c:c + 1],
                                         scale=0.5).then_inc(a_r, 1)
                    act.wait_ge(m_z, u + 1)
                    nc.scalar.activation(tz[:, c, :], gate_z[:, :], ACT.Tanh, bias=half_b_rz[:, 2 + c:3 + c],
                                         scale=0.5).then_inc(a_z, 1)
                    act.wait_ge(m_h, u + 1)
                    nc.scalar.activation(hb[:, c, :], gate_h[:, :], ACT.Identity, bias=half_b_hn[:, c:c + 1],
                                         scale=0.5).then_inc(a_h, 1)
                    if meanwhile is not None:
                        meanwhile()
                    act.wait_ge(v_pre, u + 2)
                    nc.scalar.activation(nn[:, c, :], pre[:, :], ACT.Tanh, bias=b_xn[:, c:c + 1]).then_inc(a_n, 1)

                def slots_high(it, pair, g4):
                    act.wait_ge(v_new, it * UNITS + (pair * GPP + g4) * 2 + 2)
                    sl = tokens(pair, g4)
                    nc.scalar.activation(slots_hi[:, :, sl], slots[:, :, sl], ACT.Copy).then_inc(s_hi, 1)

                def copy_rms(s, h):
                    act.wait_ge(m_rms, 2 * s + h + 1)
                    nc.scalar.activation(rms_c[:, h, :], rms_b[:, :], ACT.Copy).then_inc(a_rms, 1)

                def exponentials(s):
                    act.wait_ge(v_neg, s + 1)
                    nc.scalar.activation(expo[:, :], expo[:, :], ACT.Exp, bias=neg_top[:, :],
                                         accum_out=den[:, :]).then_inc(a_exp, 1)

                def copy_csum(s):
                    for h in range(2):
                        act.wait_ge(m_csum, 2 * s + h + 1)
                        nc.scalar.activation(csum_c[:, h, :], score[:, h, :], ACT.Identity,
                                             bias=attn_eps[:, :]).then_inc(a_csum, 1)

                def attention_hi(s, pair, h):
                    act.wait_ge(v_attn, 2 * s + h + 1)
                    half = slice(h * GROUP, (h + 1) * GROUP)
                    nc.scalar.activation(attn_hi[:, pair, half], expo[:, half], ACT.Copy).then_inc(a_attn, 1)

                def half_iteration(it, pair, softmax, more=True):
                    s = 2 * it + pair + 1

                    def high(p, g4):
                        return (lambda: slots_high(it, p, g4)) if more else None

                    gru_unit(it, pair, 0, 0, high(0, GPP - 1) if pair == 1 else None)
                    attention_hi(s - 1, pair, 1)
                    gru_unit(it, pair, 0, 1)
                    gru_unit(it, pair, 1, 0, high(pair, 0))
                    if softmax:
                        copy_rms(s, 0)
                    gru_unit(it, pair, 1, 1)
                    if softmax:
                        copy_rms(s, 1)
                    gru_unit(it, pair, 2, 0, high(pair, 1))
                    if softmax:
                        exponentials(s)
                    gru_unit(it, pair, 2, 1)
                    if softmax:
                        copy_csum(s)
                    gru_unit(it, pair, 3, 0, high(pair, 2))
                    if softmax:
                        attention_hi(s, 1 - pair, 0)
                    gru_unit(it, pair, 3, 1)
                    if more and pair == 1:
                        slots_high(it, pair, GPP - 1)

                for free in (a_r, a_z, a_h):
                    act.sem_inc(free, 1)
                copy_rms(0, 0)
                copy_rms(0, 1)
                exponentials(0)
                copy_csum(0)
                attention_hi(0, 0, 0)
                with act.Fori(0, ITERS - 1) as it:
                    half_iteration(it, 0, True)
                    half_iteration(it, 1, True)
                half_iteration(ITERS - 1, 0, True, more=False)
                half_iteration(ITERS - 1, 1, False, more=False)

            @block.vector
            def _(dve):
                def gru_unit(it, pair, g4, c, meanwhile=None):
                    u = it * UNITS + (pair * GPP + g4) * 2 + c
                    sl = tokens(pair, g4)
                    dve.wait_ge(a_r, u + 2)
                    dve.wait_ge(a_h, u + 2)
                    nc.vector.scalar_tensor_tensor(pre[:, :], tr[:, c, :], 1.0, hb[:, c, :], ALU.add,
                                                   ALU.mult).then_inc(v_q, 1)
                    dve.wait_ge(v_q, u + 3)
                    dve.wait_ge(m_x, u + 1)
                    nc.vector.tensor_tensor(pre[:, :], pre[:, :], gate_x[:, :], ALU.add).then_inc(v_pre, 1)
                    if meanwhile is not None:
                        meanwhile()
                    dve.wait_ge(a_n, u + 1)
                    nc.vector.tensor_tensor(dif[:, :], slots[:, c, sl], nn[:, c, :], ALU.subtract).then_inc(v_dif, 1)
                    dve.wait_ge(v_dif, u + 1)
                    dve.wait_ge(a_z, u + 2)
                    nc.vector.scalar_tensor_tensor(dif[:, :], tz[:, c, :], 1.0, dif[:, :], ALU.add,
                                                   ALU.mult).then_inc(v_mix, 1)
                    dve.wait_ge(v_mix, u + 1)
                    nc.vector.scalar_tensor_tensor(slots[:, c, sl], dif[:, :], 0.5, nn[:, c, :], ALU.mult,
                                                   ALU.add).then_inc(v_new, 1)

                def token_rms(s, pair):
                    dve.wait_ge(s_ss, GPP * (s + 1))
                    cols = slice(pair * GPP * BLK, (pair + 1) * GPP * BLK)
                    nc.vector.tensor_scalar(ms[:, :], ssq[:, cols], 1.0 / D, RMS_EPS, ALU.mult,
                                            ALU.add).then_inc(v_ms, 1)
                    dve.wait_ge(v_ms, s + 1)
                    n = [0]

                    def do(ins):
                        n[0] += 1
                        ins.then_inc(v_rms, 1)
                        dve.wait_ge(v_rms, s * 11 + n[0])

                    rsqrt_steps(nc.vector, do, rms[:, :], ms[:, :], rms_t[:, :])
                    assert n[0] == 11
                    w = GPP * BLK
                    nc.vector.tensor_tensor(
                        diag[:, :, :], ident[:, :].rearrange("p (a q) -> p a q", a=1).to_broadcast([P, w, P]),
                        rms[:, :].rearrange("p (w a) -> p w a", a=1).to_broadcast([P, w, P]),
                        ALU.mult).then_inc(v_diag, 1)

                def scale_scores(s, h):
                    dve.wait_ge(m_score, 2 * s + h + 1)
                    dve.wait_ge(a_rms, 2 * s + h + 1)
                    nc.vector.tensor_tensor(expo[:, h * GROUP:(h + 1) * GROUP], score[:, h, :], rms_c[:, h, :],
                                            ALU.mult).then_inc(v_mul, 1)

                def maximum(s):
                    dve.wait_ge(v_mul, 2 * s + 2)
                    nc.vector.reduce_max(top[:, :], expo[:, :], AX).then_inc(v_top, 1)
                    dve.wait_ge(v_top, s + 1)
                    nc.vector.tensor_scalar(neg_top[:, :], top[:, :], -1.0, None, ALU.mult).then_inc(v_neg, 1)

                def token_sum(s):
                    dve.wait_ge(a_exp, s + 1)
                    nc.vector.reciprocal(rden[:, :], den[:, :]).then_inc(v_rden, 1)
                    dve.wait_ge(v_rden, s + 1)
                    nc.vector.tensor_scalar(rsum[:, :], half_mask[:, :], rden[:, :], None, ALU.mult).then_inc(v_rsum, 1)

                def half_of(h):
                    return slice(h * GROUP, (h + 1) * GROUP)

                def csum_reciprocal(s, h):
                    dve.wait_ge(a_csum, 2 * s + h + 1)
                    nc.vector.reciprocal(csum_c[:, h, :], csum_c[:, h, :]).then_inc(v_rec, 1)

                def attention_half(s, h):
                    dve.wait_ge(v_rec, 2 * s + h + 1)
                    nc.vector.scalar_tensor_tensor(expo[:, half_of(h)], expo[:, half_of(h)], rden[:, :], csum_c[:, h, :],
                                                   ALU.mult, ALU.mult).then_inc(v_attn, 1)

                def attention_lo(s, pair, h):
                    dve.wait_ge(a_attn, 2 * s + h + 1)
                    nc.vector.tensor_tensor(attn_lo[:, pair, half_of(h)], expo[:, half_of(h)],
                                            attn_hi[:, pair, half_of(h)].bitcast(F32), ALU.subtract).then_inc(v_alo, 1)

                def half_iteration(it, pair, softmax):
                    s = 2 * it + pair + 1
                    gru_unit(it, pair, 0, 0)
                    gru_unit(it, pair, 0, 1, lambda: attention_lo(s - 1, pair, 1))
                    if softmax:
                        token_rms(s, 1 - pair)
                    gru_unit(it, pair, 1, 0)
                    if softmax:
                        scale_scores(s, 0)
                    gru_unit(it, pair, 1, 1)
                    if softmax:
                        scale_scores(s, 1)
                        maximum(s)
                    gru_unit(it, pair, 2, 0)
                    if softmax:
                        token_sum(s)
                    gru_unit(it, pair, 2, 1)
                    if softmax:
                        csum_reciprocal(s, 0)
                    gru_unit(it, pair, 3, 0, (lambda: attention_half(s, 0)) if softmax else None)
                    if softmax:
                        csum_reciprocal(s, 1)
                        attention_lo(s, 1 - pair, 0)
                    gru_unit(it, pair, 3, 1, (lambda: attention_half(s, 1)) if softmax else None)

                dve.sem_inc(v_q, 2)
                dve.sem_inc(v_pre, 1)
                token_rms(0, 0)
                scale_scores(0, 0)
                scale_scores(0, 1)
                maximum(0)
                token_sum(0)
                csum_reciprocal(0, 0)
                attention_half(0, 0)
                csum_reciprocal(0, 1)
                attention_lo(0, 0, 0)
                attention_half(0, 1)
                with dve.Fori(0, ITERS - 1) as it:
                    half_iteration(it, 0, True)
                    half_iteration(it, 1, True)
                half_iteration(ITERS - 1, 0, True)
                half_iteration(ITERS - 1, 1, False)

            @block.gpsimd
            def _(pool):
                with pool.Fori(0, ITERS - 1) as it:
                    for g in range(G):
                        run = it * G + g + G
                        pool.wait_ge(v_new, it * UNITS + 2 * g + 2)
                        pool.wait_ge(s_ss, run - 1)
                        sl = slice(g * GROUP, (g + 1) * GROUP)
                        squares(pool, g, run)
                        pool.wait_ge(s_hi, run + 1)
                        nc.gpsimd.tensor_tensor(slots_lo[:, :, sl], slots[:, :, sl], slots_hi[:, :, sl].bitcast(F32),
                                                ALU.subtract).then_inc(s_lo, 1)
        attention.close()
        E = gate_t.shape[1]
        CAP = -(-T // E) * 2
        WCOL = 6 * P
        FS = w_shared.shape[1]
        BISECT = 4
        ROW = D + E
        BIG = 8192.0
        HALF_T = T // 2
        AW, BW = 32, 16
        assert G * E == P and CAP == AW * BW and BISECT * G >= 30 and E % BLK == 0
        rows = nc.dram_tensor("token_rows", (T, ROW), F32, kind="Internal").ap()
        ids = nc.dram_tensor("token_ids", (E, CAP), U32, kind="Internal").ap()
        s_ids = sem("s_ids")
        s_out = sem("s_out")
        routing = ExitStack()
        rsb, _ = tensors(routing)
        sg = rsb("sg", [P, GROUP])
        thr = rsb("thr", [P, 1], I32)
        same_e = rsb("same_e", [P, P])
        before = rsb("before", [P, P])
        with ExitStack() as dense:
            lsb, lps = tensors(dense)
            xg = lsb("xg", [P, 2, KC, GROUP])
            hg = lsb("hg", [P, 2, KC, GROUP])
            gw_f = lsb("gw_f", [P, KC, E])
            gw_hi = lsb("gw_hi", [P, KC, 2 * P - E], F32R)
            gw_lo = lsb("gw_lo", [P, KC, 2 * P - E], F32R)
            sh_raw = lsb("sh_raw", [P, FS, WCOL])
            sh_hi = lsb("sh_hi", [P, FS, WCOL], F32R)
            sh_lo = lsb("sh_lo", [P, FS, WCOL], F32R)
            silu = lsb("silu", [P, 2, GROUP])
            hid = lsb("hid", [P, 2, GROUP])
            hid_hi = lsb("hid_hi", [P, FS, GROUP], F32R)
            hid_lo = lsb("hid_lo", [P, FS, GROUP], F32R)
            y = lsb("y", [P, BLK, D])
            stats2 = lsb("stats2", [P, BLK, 6])
            mv2 = lsb("mv2", [P, BLK, 2])
            var2 = lsb("var2", [P, BLK])
            rstd2 = lsb("rstd2", [P, BLK])
            rtmp2 = lsb("rtmp2", [P, BLK])
            bit = lsb("bit", [P, 1], I32)
            cand = lsb("cand", [P, 1], I32)
            keep = lsb("keep", [P, 1], I32)
            cnt = lsb("cnt", [P, 1])
            junk = lsb("junk", [P, GROUP])
            wide = lps("wide", [P, 4, 512])
            down = lps("down", [P, 2, 512])
            logit = lps("logit", [P, 512])
            small = lps("small", [P, 512])

            l_sh, l_gw = sem("l_sh"), sem("l_gw")
            l_xg = [sem(f"l_xg{i}") for i in range(2)]
            w_rows = [sem(f"w_rows{i}") for i in range(2)]
            p2 = sem("p2")
            t_tok, t_h = sem("t_tok"), sem("t_h")
            v2 = sem("v2")
            v_x1, v_h = sem("v_x1"), sem("v_h")
            a_hh, v_hl = sem("a_hh"), sem("v_hl")
            v_gw, v_sh, a_sh = sem("v_gw"), sem("v_sh"), sem("a_sh")
            m_log, a_sg = sem("m_log"), sem("a_sg")
            m_g, m_u, a_silu, v_hid, a_hid, v_hlo = (sem(n) for n in ("m_g", "m_u", "a_silu", "v_hid", "a_hid", "v_hlo"))
            m_dn, v_y, w_y = sem("m_dn"), sem("v_y"), sem("w_y")
            v_cnt, m_cnt, v_bis = sem("v_cnt"), sem("m_cnt"), sem("v_bis")

            block = dense.enter_context(nc.Block())
            xrows = x.rearrange("(g b p) (k q) -> g p k b q", b=BLK, p=P, k=KC)
            hrows = rows[:, 0:D].rearrange("(g b p) (k q) -> g p k b q", b=BLK, p=P, k=KC)
            orows = out.rearrange("(g b p) d -> g p b d", b=BLK, p=P)

            @block.sync
            def _(sp):
                sp.dma_start(gw_f[:, :, :], gate_t.rearrange("(k p) e -> p k e", p=P)).then_inc(l_gw, 16)
                for g in range(G):
                    if g >= 2:
                        sp.wait_ge(v_x1, g - 1)
                    for k in range(KC):
                        sp.dma_start(xg[:, g % 2, k, :].rearrange("p (b q) -> p b q", q=P),
                                     xrows[g, :, k]).then_inc(l_xg[g % 2], 16)
                    if g == 0:
                        sp.dma_start(sh_raw[:, :, :], w_shared).then_inc(l_sh, 16)
                    if g >= 1:
                        sp.wait_ge(v_h, g)
                        for k in range(KC):
                            sp.dma_start(hrows[g - 1, :, k], hg[:, (g - 1) % 2, k, :].rearrange("p (b q) -> p b q", q=P))\
                                .then_inc(w_rows[(g - 1) % 2], 16)
                sp.wait_ge(v_h, G)
                for k in range(KC):
                    sp.dma_start(hrows[G - 1, :, k], hg[:, (G - 1) % 2, k, :].rearrange("p (b q) -> p b q", q=P))\
                        .then_inc(w_rows[(G - 1) % 2], 16)
                with sp.Fori(0, G) as g:
                    sp.wait_ge(v_y, g + 1)
                    sp.dma_start(out[bass.ds(g * GROUP, GROUP), :].rearrange("(b p) d -> p b d", p=P),
                                 y[:, :, :]).then_inc(w_y, 16)
                sp.wait_ge(w_y, 16 * G)
                for i in range(2):
                    sp.wait_ge(w_rows[i], 16 * KC * G // 2)

            @block.gpsimd
            def _(pool):
                nc.gpsimd.memset(gw_hi[:, :, :].bitcast(F32), 0.0).then_inc(p2, 1)
                nc.gpsimd.memset(gw_lo[:, :, :].bitcast(F32), 0.0).then_inc(p2, 1)
                nc.gpsimd.memset(same_e[:, :], 0.0).then_inc(p2, 1)
                for n in range(1 - G, G):
                    pool.wait_ge(p2, 3 + n + G - 1)
                    nc.gpsimd.affine_select(out=same_e[:, :], in_=same_e[:, :], compare_op=ALU.not_equal, fill=1.0,
                                            base=-E * n, pattern=[[1, P]], channel_multiplier=-1).then_inc(p2, 1)
                pool.wait_ge(p2, 3 + 2 * G - 1)
                nc.gpsimd.affine_select(out=before[:, :], in_=same_e[:, :], compare_op=ALU.is_ge, fill=0.0,
                                        base=-1, pattern=[[1, P]], channel_multiplier=-1).then_inc(p2, 1)

            def router(pe, g):
                pe.wait_ge(v_hl, g + 1)
                pe.wait_ge(a_hh, g + 1)
                if g == 0:
                    pe.wait_ge(v_gw, 2)
                sl = slice(g * GROUP, (g + 1) * GROUP)
                c0 = P - E - g * E
                n = 0
                for k in range(KC):
                    for w, h in ((gw_hi, slots_hi), (gw_hi, slots_lo), (gw_lo, slots_hi)):
                        n += 1
                        last = nc.tensor.matmul(logit[:, :], w[:, k, c0:c0 + P], h[:, k, sl],
                                                start=(g == 0 and n == 1), stop=(g == G - 1 and n == 3 * KC))
                return last

            @block.tensor
            def _(pe):
                for g in range(G):
                    if g >= 1:
                        pe.wait_ge(v_x1, g)
                    for b in range(BLK):
                        for k in range(KC):
                            c0 = g * GROUP + b * P
                            last = nc.tensor.transpose(wide[:, k, b * P:(b + 1) * P], slots[:, k, c0:c0 + P], ident[:, :])
                    last.then_inc(t_tok, 1)
                    pe.wait_ge(v_h, g + 1)
                    if g >= 1:
                        pe.wait_ge(v_hl, g)
                    for b in range(BLK):
                        for k in range(KC):
                            last = nc.tensor.transpose(wide[:, 2 + k, b * P:(b + 1) * P], hg[:, g % 2, k, b * P:(b + 1) * P],
                                                       ident[:, :])
                    last.then_inc(t_h, 1)
                    if g >= 1:
                        router(pe, g - 1)
                router(pe, G - 1).then_inc(m_log, 1)
                pe.wait_ge(a_sh, 1)
                pe.wait_ge(v_sh, 1)
                pe.wait_ge(p2, 3 + 2 * G)
                with pe.Fori(0, G) as g:
                    sl = bass.ds(g * GROUP, GROUP)
                    for f in range(FS + 1):
                        if f < FS:
                            u = g * FS + f
                            for bank, s_m, s_v, c in ((f % 2, m_g, a_silu, 0), (2 + f % 2, m_u, v_hid, 2)):
                                pe.wait_ge(s_v, u + 1)
                                n = 0
                                for k in range(KC):
                                    cols = slice((c + k) * P, (c + k + 1) * P)
                                    for w, h in ((sh_hi, slots_hi), (sh_hi, slots_lo), (sh_lo, slots_hi)):
                                        n += 1
                                        last = nc.tensor.matmul(wide[:, bank, :], w[:, f, cols], h[:, k, sl],
                                                                start=(n == 1), stop=(n == 3 * KC))
                                last.then_inc(s_m, 1)
                        if f >= 1:
                            d = f - 1
                            u = g * FS + d
                            pe.wait_ge(v_hlo, u + 1)
                            if d == 0:
                                pe.wait_ge(v_y, g)
                            for b in range(BLK):
                                tok = slice(b * P, (b + 1) * P)
                                for n, (h, w) in enumerate(((hid_hi, sh_hi), (hid_lo, sh_hi), (hid_hi, sh_lo))):
                                    last = nc.tensor.matmul(down[:, b // 2, (b % 2) * D:(b % 2 + 1) * D], h[:, d, tok],
                                                            w[:, d, 4 * P:6 * P], start=(d == 0 and n == 0 and b % 2 == 0),
                                                            stop=(d == FS - 1 and n == 2), skip_group_check=True)
                            last.then_inc(m_dn, 1)
                        if f < BISECT:
                            u = g * BISECT + f
                            pe.wait_ge(v_cnt, u + 1)
                            nc.tensor.matmul(small[:, 0:1], same_e[:, :], cnt[:, :], start=True,
                                             stop=True).then_inc(m_cnt, 1)

            @block.scalar
            def _(act):
                act.wait_ge(l_sh, 16)
                nc.scalar.activation(sh_hi[:, :, :], sh_raw[:, :, :], ACT.Copy).then_inc(a_sh, 1)
                for g in range(G):
                    act.wait_ge(t_h, g + 1)
                    nc.scalar.activation(slots_hi[:, :, g * GROUP:(g + 1) * GROUP], wide[:, 2:4, :],
                                         ACT.Copy).then_inc(a_hh, 1)
                act.wait_ge(m_log, 1)
                nc.scalar.activation(sg[:, :], logit[:, :], ACT.Sigmoid).then_inc(a_sg, 1)
                nc.scalar.preload_act_table(ACT.Silu)
                act.sem_inc(a_silu, 2)
                act.sem_inc(a_hid, 1)
                with act.Fori(0, G) as g:
                    for f in range(FS):
                        u = g * FS + f
                        act.wait_ge(m_g, u + 1)
                        act.wait_ge(v_hid, u + 1)
                        nc.scalar.activation(silu[:, f % 2, :], wide[:, f % 2, :], ACT.Silu).then_inc(a_silu, 1)
                        act.wait_ge(v_hid, u + 3)
                        if f == 0:
                            act.wait_ge(m_dn, g * FS)
                        nc.scalar.activation(hid_hi[:, f, :], hid[:, f % 2, :], ACT.Copy).then_inc(a_hid, 1)

            @block.vector
            def _(dve):
                st = Steps(dve, v2)
                dve.wait_ge(l_gw, 16)
                dve.wait_ge(p2, 2)
                nc.vector.tensor_copy(gw_hi[:, :, P - E:P], gw_f[:, :, :]).then_inc(v_gw, 1)
                dve.wait_ge(v_gw, 1)
                nc.vector.tensor_tensor(gw_lo[:, :, P - E:P], gw_f[:, :, :], gw_hi[:, :, P - E:P].bitcast(F32),
                                        ALU.subtract).then_inc(v_gw, 1)
                dve.wait_ge(a_sh, 1)
                nc.vector.tensor_tensor(sh_lo[:, :, :], sh_raw[:, :, :], sh_hi[:, :, :].bitcast(F32),
                                        ALU.subtract).then_inc(v_sh, 1)

                def low_part(g):
                    sl = slice(g * GROUP, (g + 1) * GROUP)
                    dve.wait_ge(a_hh, g + 1)
                    nc.vector.tensor_tensor(slots_lo[:, :, sl], wide[:, 2:4, :], slots_hi[:, :, sl].bitcast(F32),
                                            ALU.subtract).then_inc(v_hl, 1)

                for g in range(G):
                    sl = slice(g * GROUP, (g + 1) * GROUP)
                    dve.wait_ge(t_tok, g + 1)
                    dve.wait_ge(l_xg[g % 2], 16 * KC * (g // 2 + 1))
                    nc.vector.scalar_tensor_tensor(slots[:, :, sl], wide[:, 0:2, :], tanh_g[:, 0:1], xg[:, g % 2, :, :],
                                                   ALU.mult, ALU.add).then_inc(v_x1, 1)
                    dve.wait_ge(v_x1, g + 1)
                    for b in range(BLK):
                        c0 = g * GROUP + b * P
                        st.add(nc.vector.bn_stats(stats2[:, b, :], slots[:, :, c0:c0 + P]))
                    st.wait()
                    for b in range(BLK):
                        st.add(nc.vector.bn_aggr(mv2[:, b, :], stats2[:, b, :]))
                    st.wait()
                    st.do(nc.vector.tensor_scalar(var2[:, :], mv2[:, :, 1], LN_EPS, None, ALU.add))
                    rsqrt_steps(nc.vector, st.do, rstd2[:, :], var2[:, :], rtmp2[:, :])
                    if g >= 2:
                        dve.wait_ge(w_rows[g % 2], 16 * KC * (g // 2))
                        dve.wait_ge(t_h, g - 1)
                    for b in range(BLK):
                        c0 = g * GROUP + b * P
                        last = nc.vector.tensor_scalar(hg[:, g % 2, :, b * P:(b + 1) * P], slots[:, :, c0:c0 + P],
                                                       mv2[:, b, 0:1], rstd2[:, b:b + 1], ALU.subtract, ALU.mult)
                    last.then_inc(v_h, 1)
                    if g >= 1:
                        low_part(g - 1)
                low_part(G - 1)
                st.do(nc.vector.memset(thr[:, :], 0))
                st.do(nc.vector.memset(bit[:, :], 1 << 29))
                dve.sem_inc(v_hid, 2)
                dve.wait_ge(a_sg, 1)

                def bisect_count(u):
                    nc.vector.tensor_scalar(cand[:, :], bit[:, :], thr[:, 0:1], None, ALU.bitwise_or).then_inc(v_bis, 1)
                    dve.wait_ge(v_bis, 3 * u + 1)
                    nc.vector.tensor_scalar(junk[:, :], sg[:, :], cand[:, 0:1].bitcast(F32), 0.0, ALU.is_ge, ALU.add,
                                            accum_out=cnt[:, :]).then_inc(v_cnt, 1)

                def bisect_keep(u):
                    dve.wait_ge(m_cnt, u + 1)
                    nc.vector.tensor_scalar(keep[:, :], small[:, 0:1], float(CAP), -1.0, ALU.is_ge,
                                            ALU.mult).then_inc(v_bis, 1)
                    dve.wait_ge(v_bis, 3 * u + 2)
                    nc.vector.scalar_tensor_tensor(thr[:, :], keep[:, :], bit[:, 0:1], thr[:, :], ALU.bitwise_and,
                                                   ALU.bitwise_or).then_inc(v_bis, 1)
                    dve.wait_ge(v_bis, 3 * u + 3)
                    nc.vector.tensor_scalar(bit[:, :], bit[:, :], 1, None,
                                            ALU.logical_shift_right).then_inc(v2, 1)
                    dve.wait_ge(v2, st.n + u + 1)

                with dve.Fori(0, G) as g:
                    for f in range(FS):
                        u = g * FS + f
                        bisect_count(u)
                        dve.wait_ge(m_u, u + 1)
                        dve.wait_ge(a_silu, u + 3)
                        dve.wait_ge(a_hid, u)
                        nc.vector.tensor_tensor(hid[:, f % 2, :], silu[:, f % 2, :], wide[:, 2 + f % 2, :],
                                                ALU.mult).then_inc(v_hid, 1)
                        dve.wait_ge(a_hid, u + 2)
                        nc.vector.tensor_tensor(hid_lo[:, f, :], hid[:, f % 2, :], hid_hi[:, f, :].bitcast(F32),
                                                ALU.subtract).then_inc(v_hlo, 1)
                        bisect_keep(u)
                    dve.wait_ge(m_dn, (g + 1) * FS)
                    dve.wait_ge(w_y, g * 16)
                    for b in range(BLK):
                        last = nc.vector.scalar_tensor_tensor(
                            y[:, b, :].rearrange("p (k q) -> p k q", k=KC),
                            down[:, b // 2, (b % 2) * D:(b % 2 + 1) * D].rearrange("p (k q) -> p k q", k=KC),
                            tanh_g[:, 1:2], slots[:, :, bass.ds(g * GROUP + b * P, P)], ALU.mult, ALU.add)
                    last.then_inc(v_y, 1)
        with ExitStack() as route:
            lsb, lps = tensors(route)
            ones = lsb("ones", [P, GROUP])
            above = lsb("above", [P, GROUP])
            tie = lsb("tie", [P, GROUP])
            count = lsb("count", [P, GROUP])
            taken = lsb("taken", [P, GROUP])
            slot = lsb("slot", [P, GROUP])
            tots = lsb("tots", [P, 4])
            offs = lsb("offs", [P, 4])
            slot_i = lsb("slot_i", [P, GROUP], I32)
            hi_i = lsb("hi_i", [P, GROUP], I32)
            lo_i = lsb("lo_i", [P, GROUP], I32)
            hi_f = lsb("hi_f", [P, GROUP], F16)
            lo_f = lsb("lo_f", [P, GROUP], F16)
            iota_i = lsb("iota_i", [P, AW], I32)
            iota_f = lsb("iota_f", [P, AW], F16)
            tok_i = lsb("tok_i", [P, BLK * G], I32)
            tok_f = lsb("tok_f", [P, BLK * G])
            hot_a = lsb("hot_a", [P, GROUP, AW], F16)
            hot_b = lsb("hot_b", [P, GROUP, BW], F16)
            score_t = lsb("score_t", [P, GROUP])
            ids_sb = lsb("ids_sb", [P, E // BLK, BW], U32)
            tot = lps("tot", [P, 512])
            slot_p = lps("slot_p", [P, 512])
            score_p = lps("score_p", [P, 512])
            ids_p = lps("ids_p", [P, 512])

            p3, v3, m_tot, t_slot, t_score, a_score = (sem(n) for n in
                                                       ("p3", "v3", "m_tot", "t_slot", "t_score", "a_score"))
            v_tot, v_slot, v_hot, m_ids, v_ids, w_score = (sem(n) for n in
                                                           ("v_tot", "v_slot", "v_hot", "m_ids", "v_ids", "w_score"))
            block = route.enter_context(nc.Block())

            @block.gpsimd
            def _(pool):
                nc.gpsimd.iota(iota_i[:, :], pattern=[[1, AW]], base=0, channel_multiplier=0).then_inc(p3, 1)
                nc.gpsimd.iota(tok_i[:, :], pattern=[[P, BLK], [GROUP, G]], base=-HALF_T,
                               channel_multiplier=1).then_inc(p3, 1)
                pool.wait_ge(p3, 2)
                nc.gpsimd.tensor_copy(iota_f[:, :], iota_i[:, :]).then_inc(p3, 1)
                nc.gpsimd.tensor_copy(tok_f[:, :], tok_i[:, :]).then_inc(p3, 1)

            @block.tensor
            def _(pe):
                for c in range(BLK):
                    last = nc.tensor.transpose(score_p[:, c * P:(c + 1) * P], sg[:, c * P:(c + 1) * P], ident[:, :])
                last.then_inc(t_score, 1)
                pe.wait_ge(v_tot, 1)
                nc.tensor.matmul(tot[:, 0:1], same_e[:, :], tots[:, 0:1], start=True, stop=True)
                nc.tensor.matmul(tot[:, 1:2], before[:, :], tots[:, 1:2], start=True, stop=True).then_inc(m_tot, 1)
                pe.wait_ge(v_tot, 2)
                nc.tensor.matmul(tot[:, 2:3], before[:, :], tots[:, 2:3], start=True, stop=True).then_inc(m_tot, 1)
                pe.wait_ge(v_slot, 1)
                for c in range(BLK):
                    last = nc.tensor.transpose(slot_p[:, c * P:(c + 1) * P], slot[:, c * P:(c + 1) * P], ident[:, :])
                last.then_inc(t_slot, 1)
                hb_ = hot_b[:, :, :].rearrange("p (w e) b -> p w (e b)", e=E)
                ha_ = hot_a[:, :, :].rearrange("p (w e) a -> p w (e a)", e=E)
                pe.wait_ge(v_hot, 1)
                for q in range(E // BLK):
                    for w in range(BLK * G):
                        last = nc.tensor.matmul(ids_p[:, q * BLK * BW:(q + 1) * BLK * BW],
                                                ha_[:, w, q * P:(q + 1) * P], hb_[:, w, q * BLK * BW:(q + 1) * BLK * BW],
                                                start=(w == 0), stop=(w == BLK * G - 1))
                last.then_inc(m_ids, 1)

            @block.scalar
            def _(act):
                act.wait_ge(t_score, 1)
                nc.scalar.activation(score_t[:, :], score_p[:, :], ACT.Copy).then_inc(a_score, 1)

            @block.sync
            def _(sp):
                sp.wait_ge(a_score, 1)
                srows = rows[:, D:ROW].rearrange("(g c p) e -> c p g e", c=BLK, p=P)
                for c in range(BLK):
                    sp.dma_start(srows[c], score_t[:, c * P:(c + 1) * P].rearrange("p (g e) -> p g e", e=E))\
                        .then_inc(w_score, 16)
                sp.wait_ge(v_ids, 1)
                idv = ids.rearrange("(q f) (a b) -> f a q b", f=BLK, b=BW)
                for f in range(BLK):
                    sp.dma_start(idv[f], ids_sb[f * AW:(f + 1) * AW, :, :]).then_inc(s_ids, 16)
                sp.wait_ge(w_score, 16 * BLK)
                sp.wait_ge(s_ids, 16 * BLK)

            @block.vector
            def _(dve):
                st = Steps(dve, v3)
                thr_f = thr[:, 0:1].bitcast(F32)
                st.add(nc.vector.memset(ones[:, :], 1.0))
                st.add(nc.vector.tensor_scalar(above[:, :], sg[:, :], thr_f, 0.0, ALU.is_gt, ALU.add,
                                               accum_out=tots[:, 0:1]))
                st.do(nc.vector.tensor_scalar(tie[:, :], sg[:, :], thr_f, None, ALU.is_equal))
                st.do(nc.vector.tensor_tensor_scan(count[:, :], ones[:, :], tie[:, :], 0.0, ALU.mult, ALU.add))
                st.do(nc.vector.tensor_copy(tots[:, 1:2], count[:, GROUP - 1:GROUP]))
                dve.sem_inc(v_tot, 1)
                dve.wait_ge(m_tot, 1)
                st.add(nc.vector.tensor_scalar(offs[:, 0:1], tot[:, 0:1], -1.0, float(CAP), ALU.mult, ALU.add))
                st.do(nc.vector.tensor_copy(offs[:, 1:2], tot[:, 1:2]))
                st.do(nc.vector.tensor_scalar(taken[:, :], count[:, :], offs[:, 1:2], offs[:, 0:1], ALU.add, ALU.is_le))
                st.do(nc.vector.tensor_tensor(taken[:, :], taken[:, :], tie[:, :], ALU.mult))
                st.do(nc.vector.tensor_tensor(taken[:, :], taken[:, :], above[:, :], ALU.add))
                st.do(nc.vector.tensor_tensor_scan(count[:, :], ones[:, :], taken[:, :], 0.0, ALU.mult, ALU.add))
                st.do(nc.vector.tensor_copy(tots[:, 2:3], count[:, GROUP - 1:GROUP]))
                dve.sem_inc(v_tot, 1)
                dve.wait_ge(m_tot, 2)
                st.do(nc.vector.tensor_scalar(offs[:, 2:3], tot[:, 2:3], -1.0 - BIG, None, ALU.add))
                st.do(nc.vector.scalar_tensor_tensor(slot[:, :], count[:, :], offs[:, 2:3], taken[:, :], ALU.add,
                                                     ALU.mult))
                nc.vector.tensor_scalar(slot[:, :], slot[:, :], BIG, None, ALU.add).then_inc(v_slot, 1)
                dve.wait_ge(t_slot, 1)
                st.do(nc.vector.tensor_copy(slot_i[:, :], slot_p[:, :]))
                st.add(nc.vector.tensor_scalar(hi_i[:, :], slot_i[:, :], 4, None, ALU.logical_shift_right))
                st.do(nc.vector.tensor_scalar(lo_i[:, :], slot_i[:, :], BW - 1, None, ALU.bitwise_and))
                st.add(nc.vector.tensor_copy(hi_f[:, :], hi_i[:, :]))
                st.do(nc.vector.tensor_copy(lo_f[:, :], lo_i[:, :]))
                dve.wait_ge(p3, 4)
                for hot, dig, w in ((hot_b, lo_f, BW), (hot_a, hi_f, AW)):
                    st.add(nc.vector.tensor_tensor(
                        hot[:, :, :], dig[:, :].rearrange("p (t a) -> p t a", a=1).to_broadcast([P, GROUP, w]),
                        iota_f[:, 0:w].rearrange("p (a w) -> p a w", a=1).to_broadcast([P, GROUP, w]), ALU.is_equal))
                st.wait()
                for w in range(BLK * G):
                    part = hot_b[:, w * E:(w + 1) * E, :]
                    last = nc.vector.tensor_scalar(part, part, tok_f[:, w:w + 1], None, ALU.mult)
                last.then_inc(v_hot, 1)
                dve.wait_ge(m_ids, 1)
                for f in range(BLK):
                    pr = slice(f * AW, (f + 1) * AW)
                    last = nc.vector.tensor_scalar(
                        ids_sb[pr, :, :], ids_p[pr, 0:E * BW].rearrange("p (q f b) -> p q f b", f=BLK, b=BW)[:, :, f, :],
                        float(HALF_T), None, ALU.add)
                last.then_inc(v_ids, 1)
        routing.close()
        state.close()
        FE = w_expert.shape[2]
        RING = 4
        LAG = 2
        AHEAD = 5
        HALF_F = FE // 2
        with ExitStack() as experts:
            lsb, lps = tensors(experts)
            raw = lsb("raw", [P, FE, WCOL])
            w_hi = lsb("w_hi", [P, FE, WCOL], F32R)
            w_lo = lsb("w_lo", [P, FE, WCOL], F32R)
            b_gate = lsb("b_gate", [P, E, FE])
            b_up = lsb("b_up", [P, E, FE])
            b_down = lsb("b_down", [P, E, D])
            idx_all = lsb("idx_all", [P, E, BLK], U32)
            idx_in = lsb("idx_in", [P, BLK], U32)
            idx_out = lsb("idx_out", [P, BLK], U32)
            got = lsb("got", [P, BLK, ROW])
            xt_hi = lsb("xt_hi", [P, KC, GROUP], F32R)
            xt_lo = lsb("xt_lo", [P, KC, GROUP], F32R)
            esilu = lsb("esilu", [P, 2, GROUP])
            ehid = lsb("ehid", [P, 2, GROUP])
            eh_hi = lsb("eh_hi", [P, RING, GROUP], F32R)
            eh_lo = lsb("eh_lo", [P, RING, GROUP], F32R)
            weight = lsb("weight", [P, BLK, 1])
            yo = lsb("yo", [P, BLK, D])
            egate = lps("egate", [P, 2, 512])
            eup = lps("eup", [P, 2, 512])
            edown = lps("edown", [P, 2, 512])
            exps = lps("exps", [P, KC, 512])

            l_b, l_idx = sem("l_b"), sem("l_idx")
            l_w = [sem("l_w0"), sem("l_w1")]
            p_idx, p_out, p_step = sem("p_idx"), sem("p_out"), sem("p_step")
            g_in_, g_add = sem("gathered"), sem("scattered")
            t_xt, a_xt, v_xt, v_wt = sem("t_xt"), sem("a_xt"), sem("v_xt"), sem("v_wt")
            a_w, v_w = sem("a_w"), sem("v_w")
            k_g, k_u, k_silu, k_hid, k_hi, k_lo, k_dn = (sem(f"k_{n}") for n in ("g", "u", "silu", "hid", "hi", "lo", "dn"))
            k_out, k_yo = sem("k_out"), sem("k_yo")
            block = experts.enter_context(nc.Block())

            def half_slice(h):
                return slice(h * HALF_F, (h + 1) * HALF_F)

            @block.sync
            def _(sp):
                sp.dma_start(idx_all[:, :, :], ids.rearrange("e (p j) -> p e j", j=BLK)).then_inc(l_idx, 16)
                for h in range(2):
                    sp.dma_start(raw[:, half_slice(h), :], w_expert[0, :, half_slice(h), :]).then_inc(l_w[h], 16)
                sp.dma_start(b_gate[:, :, :], gate_b).then_inc(l_b, 16)
                sp.dma_start(b_up[:, :, :], up_b).then_inc(l_b, 16)
                sp.dma_start(b_down[:, :, :], down_b.rearrange("(a e) d -> a e d", a=1).to_broadcast([P, E, D]))\
                    .then_inc(l_b, 16)
                with sp.Fori(0, E - 1) as e:
                    for h in range(2):
                        sp.wait_ge(a_w, e * FE + (h + 1) * HALF_F)
                        sp.wait_ge(v_w, e * FE + (h + 1) * HALF_F)
                        sp.dma_start(raw[:, half_slice(h), :],
                                     w_expert[bass.ds(e + 1, 1), :, half_slice(h), :].rearrange("a p f n -> p (a f) n"))\
                            .then_inc(l_w[h], 16)

            @block.gpsimd
            def _(pool):
                def gather(e):
                    nc.gpsimd.tensor_copy(idx_in[:, :], idx_all[:, bass.ds(e, 1), :].rearrange("p a j -> p (a j)"))\
                        .then_inc(p_idx, 1)
                    pool.wait_ge(p_idx, e + 1)
                    pool.sem_inc(p_step, 1)
                    for j in range(BLK):
                        pool.indirect_dma_start(got[:, j, :], None, rows,
                                                bass.IndirectOffsetOnAxis(idx_in[:, j:j + 1], 0)).then_inc(g_in_, 16)

                def turn_of(e, more):
                    pool.wait_ge(g_add, 16 * BLK * e)
                    pool.wait_ge(g_in_, 16 * BLK * (e + 1))
                    pool.sem_inc(p_step, 1)
                    nc.gpsimd.tensor_copy(idx_out[:, :], idx_in[:, :]).then_inc(p_out, 1)
                    if more:
                        pool.wait_ge(p_out, e + 1)
                        pool.wait_ge(t_xt, e + 1)
                        pool.wait_ge(v_wt, e + 1)
                        pool.sem_inc(p_step, 1)
                        gather(e + 1)
                    pool.wait_ge(k_yo, e + 1)
                    pool.wait_ge(p_out, e + 1)
                    pool.sem_inc(p_step, 1)
                    for j in range(BLK):
                        pool.indirect_dma_start(out, bass.IndirectOffsetOnAxis(idx_out[:, j:j + 1], 0), yo[:, j, :],
                                                None, compute_op=ALU.add).then_inc(g_add, 16)

                pool.wait_ge(l_idx, 16)
                gather(0)
                with pool.Fori(0, E - 1) as e:
                    turn_of(e, True)
                turn_of(E - 1, False)
                pool.wait_ge(g_add, 16 * BLK * E)

            @block.tensor
            def _(pe):
                def turn_rows(e):
                    pe.wait_ge(g_in_, 16 * BLK * (e + 1))
                    for k in range(KC):
                        for j in range(BLK):
                            last = nc.tensor.transpose(exps[:, k, j * P:(j + 1) * P], got[:, j, k * P:(k + 1) * P],
                                                       ident[:, :])
                    last.then_inc(t_xt, 1)

                def into_hidden(e, f):
                    n = e * FE + f
                    pe.wait_ge(a_w, n + 1)
                    pe.wait_ge(v_w, n + 1)
                    for bank, free, done, c in ((egate, k_silu, k_g, 0), (eup, k_hid, k_u, 2)):
                        pe.wait_ge(free, n + 1)
                        m = 0
                        for k in range(KC):
                            for w, x_ in ((w_hi, xt_hi), (w_hi, xt_lo), (w_lo, xt_hi)):
                                m += 1
                                last = nc.tensor.matmul(bank[:, f % 2, :], w[:, f, (c + k) * P:(c + k + 1) * P], x_[:, k, :],
                                                        start=(m == 1), stop=(m == 3 * KC))
                        last.then_inc(done, 1)

                def out_of_hidden(e, f):
                    n = e * FE + f
                    pe.wait_ge(k_lo, n + 1)
                    if f == 0:
                        pe.wait_ge(k_out, BLK * e)
                    for j in range(BLK):
                        tok = slice(j * P, (j + 1) * P)
                        for m, (h, w) in enumerate(((eh_hi, w_hi), (eh_lo, w_hi), (eh_hi, w_lo))):
                            last = nc.tensor.matmul(edown[:, j // 2, (j % 2) * D:(j % 2 + 1) * D], h[:, f % RING, tok],
                                                    w[:, f, 4 * P:6 * P], start=(f == 0 and m == 0 and j % 2 == 0),
                                                    stop=(f == FE - 1 and m == 2), skip_group_check=True)
                    last.then_inc(k_dn, 1)

                def expert(e, more):
                    pe.wait_ge(a_xt, e + 1)
                    pe.wait_ge(v_xt, e + 1)
                    for f in range(FE):
                        into_hidden(e, f)
                        if f >= LAG:
                            out_of_hidden(e, f - LAG)
                    if more:
                        turn_rows(e + 1)
                    for f in range(FE - LAG, FE):
                        out_of_hidden(e, f)

                pe.sem_inc(k_dn, FE)
                turn_rows(0)
                with pe.Fori(0, E - 1) as e:
                    expert(e, True)
                expert(E - 1, False)

            @block.scalar
            def _(act):
                def split(e, f):
                    if f % HALF_F == 0:
                        act.wait_ge(l_w[f // HALF_F], 16 * (e + 1))
                    act.wait_ge(k_dn, e * FE + f + 1)
                    nc.scalar.activation(w_hi[:, f, :], raw[:, f, :], ACT.Copy).then_inc(a_w, 1)

                def rows_hi(e):
                    act.wait_ge(t_xt, e + 1)
                    nc.scalar.activation(xt_hi[:, :, :], exps[:, :, :], ACT.Copy).then_inc(a_xt, 1)

                def expert(e, more):
                    for f in range(FE):
                        n = e * FE + f
                        act.wait_ge(k_g, n + 1)
                        act.wait_ge(k_hid, n + 1)
                        nc.scalar.activation(esilu[:, f % 2, :], egate[:, f % 2, :], ACT.Silu,
                                             bias=b_gate[:, bass.ds(e, 1), f:f + 1].rearrange("p a b -> p (a b)"))\
                            .then_inc(k_silu, 1)
                        if f < FE - AHEAD:
                            split(e, f + AHEAD)
                        elif more:
                            split(e + 1, f - (FE - AHEAD))
                        act.wait_ge(k_hid, n + 3)
                        act.wait_ge(k_dn, n + 1 + FE - RING)
                        nc.scalar.activation(eh_hi[:, f % RING, :], ehid[:, f % 2, :], ACT.Copy).then_inc(k_hi, 1)
                    if more:
                        rows_hi(e + 1)

                nc.scalar.preload_act_table(ACT.Silu)
                act.sem_inc(k_silu, 2)
                act.sem_inc(k_hi, 1)
                for f in range(AHEAD):
                    split(0, f)
                rows_hi(0)
                act.wait_ge(l_b, 48)
                with act.Fori(0, E - 1) as e:
                    expert(e, True)
                expert(E - 1, False)

            @block.vector
            def _(dve):
                def split(e, f):
                    dve.wait_ge(a_w, e * FE + f + 1)
                    nc.vector.tensor_tensor(w_lo[:, f, :], raw[:, f, :], w_hi[:, f, :].bitcast(F32),
                                            ALU.subtract).then_inc(v_w, 1)

                def rows_lo(e):
                    dve.wait_ge(a_xt, e + 1)
                    nc.vector.tensor_tensor(xt_lo[:, :, :], exps[:, :, :], xt_hi[:, :, :].bitcast(F32),
                                            ALU.subtract).then_inc(v_xt, 1)

                def take_scores(e, first=False):
                    if not first:
                        dve.wait_ge(k_yo, e)
                    nc.vector.tensor_scalar(weight[:, :, :], got[:, :, bass.ds(D + e, 1)], tanh_g[:, 1:2], None,
                                            ALU.mult).then_inc(v_wt, 1)

                def results(e):
                    dve.wait_ge(k_dn, (e + 2) * FE)
                    dve.wait_ge(g_add, 16 * BLK * e)
                    for j in range(BLK):
                        nc.vector.tensor_tensor(yo[:, j, :], edown[:, j // 2, (j % 2) * D:(j % 2 + 1) * D],
                                                b_down[:, bass.ds(e, 1), :].rearrange("p a d -> p (a d)"),
                                                ALU.add).then_inc(k_out, 1)
                    dve.wait_ge(k_out, BLK * (e + 1))
                    dve.wait_ge(v_wt, e + 1)
                    for j in range(BLK):
                        last = nc.vector.tensor_scalar(yo[:, j, :], yo[:, j, :], weight[:, j, :], None, ALU.mult)
                    last.then_inc(k_yo, 1)

                def expert(e, more):
                    for f in range(FE):
                        n = e * FE + f
                        dve.wait_ge(k_u, n + 1)
                        dve.wait_ge(k_silu, n + 3)
                        dve.wait_ge(k_hi, n)
                        nc.vector.scalar_tensor_tensor(
                            ehid[:, f % 2, :], eup[:, f % 2, :], b_up[:, bass.ds(e, 1), f:f + 1].rearrange("p a b -> p (a b)"),
                            esilu[:, f % 2, :], ALU.add, ALU.mult).then_inc(k_hid, 1)
                        if f < FE - AHEAD:
                            split(e, f + AHEAD)
                        elif more:
                            split(e + 1, f - (FE - AHEAD))
                        dve.wait_ge(k_hi, n + 2)
                        nc.vector.tensor_tensor(eh_lo[:, f % RING, :], ehid[:, f % 2, :],
                                                eh_hi[:, f % RING, :].bitcast(F32), ALU.subtract).then_inc(k_lo, 1)
                    if more:
                        rows_lo(e + 1)
                    results(e)
                    if more:
                        take_scores(e + 1)

                dve.sem_inc(k_hid, 2)
                for f in range(AHEAD):
                    split(0, f)
                rows_lo(0)
                take_scores(0, first=True)
                dve.wait_ge(l_b, 48)
                with dve.Fori(0, E - 1) as e:
                    expert(e, True)
                expert(E - 1, False)


V_PN = 1 + 11 + 2


def _columns(v):
    import numpy as _np
    return _np.ascontiguousarray(_np.swapaxes(v.reshape(v.shape[:-1] + (-1, P)), -1, -2))


def _ffn_layout(gate, up, down):
    import numpy as _np
    f, d = gate.shape
    blocks, chunks = f // P, d // P
    into = [w.T.reshape(chunks, P, blocks, P)[k] for w in (gate, up) for k in range(chunks)]
    return _np.concatenate(into + [down.T.reshape(blocks, P, d).transpose(1, 0, 2)], axis=-1)


def kernel(x, ctx_1024, g_xattn, g_ffn, L0_xattn_Wq, L0_xattn_Wk, L0_xattn_Wv, L0_xattn_gru_wih, L0_xattn_gru_whh,
           L0_xattn_gru_bih, L0_xattn_gru_bhh, L0_xattn_slot_norm_w, L0_xattn_input_norm_w, L0_ffn_gate_w, L0_ffn_up_w,
           L0_ffn_up_b, L0_ffn_gw, L0_ffn_gb, L0_ffn_down_w, L0_ffn_down_b, L0_ffn_sh_gate_w, L0_ffn_sh_up_w,
           L0_ffn_sh_down_w):
    import numpy as _np
    import concourse.bacc as _bacc
    from concourse.bass_utils import run_bass_kernel_spmd as _run

    x = _np.asarray(x)
    ctx_1024 = _np.asarray(ctx_1024)
    d = x.shape[-1]
    host = {
        "x": x.reshape(-1, d),
        "ctx_tok": ctx_1024.reshape(-1, d),
        "g_xattn": g_xattn,
        "g_ffn": g_ffn,
        "wq": L0_xattn_Wq,
        "wk_t": _np.asarray(L0_xattn_Wk).T,
        "wv_t": _np.asarray(L0_xattn_Wv).T,
        "wih_t": _np.asarray(L0_xattn_gru_wih).T,
        "whh_t": _np.asarray(L0_xattn_gru_whh).T,
        "bih": _columns(_np.asarray(L0_xattn_gru_bih)),
        "bhh": _columns(_np.asarray(L0_xattn_gru_bhh)),
        "slot_w": _columns(_np.asarray(L0_xattn_slot_norm_w)),
        "input_w": _columns(_np.asarray(L0_xattn_input_norm_w)),
        "gate_t": _np.asarray(L0_ffn_gate_w).T,
        "w_expert": _np.stack([_ffn_layout(*w) for w in zip(_np.asarray(L0_ffn_gw), _np.asarray(L0_ffn_up_w),
                                                            _np.asarray(L0_ffn_down_w))]),
        "gate_b": _columns(_np.asarray(L0_ffn_gb)).transpose(1, 0, 2),
        "up_b": _columns(_np.asarray(L0_ffn_up_b)).transpose(1, 0, 2),
        "down_b": L0_ffn_down_b,
        "w_shared": _ffn_layout(_np.asarray(L0_ffn_sh_gate_w), _np.asarray(L0_ffn_sh_up_w),
                                _np.asarray(L0_ffn_sh_down_w)),
    }
    nc = _bacc.Bacc("TRN2", target_bir_lowering=False, num_devices=1)
    arrays, args = {}, {}
    for name, a in host.items():
        a = _np.ascontiguousarray(a)
        arrays[f"in_{name}"] = a
        args[name] = nc.dram_tensor(f"in_{name}", a.shape, mybir.dt.from_np(a.dtype), kind="ExternalInput").ap()
    out = nc.dram_tensor("out_tokens", host["x"].shape, F32, kind="ExternalOutput").ap()
    flamingo_kernel(nc, **args, out=out)
    r = _run(nc, [arrays], core_ids=[0])
    return r.results[0]["out_tokens"].reshape(x.shape)
```

```python
import concourse.bass as bass
from concourse import mybir
from contextlib import ExitStack

F32 = mybir.dt.float32
F32R = mybir.dt.float32r
F16 = mybir.dt.float16
I32 = mybir.dt.int32
U32 = mybir.dt.uint32
ALU = mybir.AluOpType
ACT = mybir.ActivationFunctionType
AX = mybir.AxisListType.X

P = 128
GROUP = 512
BLK = GROUP // P
RSQRT_MAGIC = 0x5F3759DF


class Steps:

    def __init__(self, eng, sem, done=0):
        self.eng, self.sem, self.n = eng, sem, done

    def add(self, ins):
        ins.then_inc(self.sem, 1)
        self.n += 1

    def wait(self):
        self.eng.wait_ge(self.sem, self.n)

    def do(self, ins):
        self.add(ins)
        self.wait()


def rsqrt_steps(dve, do, y, v, t):
    do(dve.tensor_scalar(t.bitcast(I32), v.bitcast(I32), 1, None, ALU.logical_shift_right))
    do(dve.tensor_scalar(y.bitcast(I32), t.bitcast(I32), -1.0, float(RSQRT_MAGIC), ALU.mult, ALU.add))
    for _ in range(3):
        do(dve.scalar_tensor_tensor(t, y, -0.5, y, ALU.mult, ALU.mult))
        do(dve.tensor_tensor(t, t, v, ALU.mult))
        do(dve.scalar_tensor_tensor(y, t, 1.5, y, ALU.add, ALU.mult))


def flamingo_kernel(nc, x, ctx_tok, tanh_in, wq, wk_t, wv_t, wih_t, whh_t, vectors, gate_t,
                    w_expert, gate_b, up_b, down_b, w_shared, out):
    T, D = x.shape
    M = ctx_tok.shape[0]
    B = 4
    MB = M // B
    KC = D // P
    G = T // GROUP
    PAIRS = B // 2
    GPP = G // PAIRS
    ITERS = 3
    SCALE = float(D) ** -0.5
    RMS_EPS, LN_EPS, ATTN_EPS = 1e-6, 1e-5, 1e-6
    assert KC == 2 and MB == 64 and T // B == 2 * GROUP and GPP == 4

    with ExitStack() as whole:
        def tensors(stack):
            def sb(name, shape, dt=F32):
                return stack.enter_context(nc.sbuf_tensor(name, shape, dt))

            def ps(name, shape, dt=F32):
                return stack.enter_context(nc.psum_tensor(name, shape, dt))
            return sb, ps

        def sem(name):
            return whole.enter_context(nc.semaphore(name))

        sb, ps = tensors(whole)
        ident = sb("ident", [P, P])
        tanh_g = sb("tanh_g", [P, 2])

        state = ExitStack()
        ssb, _ = tensors(state)
        slots = ssb("slots", [P, KC, T])
        slots_hi = ssb("slots_hi", [P, KC, T], F32R)
        slots_lo = ssb("slots_lo", [P, KC, T], F32R)
        attention = ExitStack()
        asb, aps = tensors(attention)
        whh_hi = asb("whh_hi", [P, KC, 3 * D], F32R)
        whh_lo = asb("whh_lo", [P, KC, 3 * D], F32R)
        vw_hi = asb("vw_hi", [P, PAIRS, 3 * D], F32R)
        vw_lo = asb("vw_lo", [P, PAIRS, 3 * D], F32R)
        kq_hi = asb("kq_hi", [P, KC, B, P], F32R)
        kq_lo = asb("kq_lo", [P, KC, B, P], F32R)
        square = asb("square", [P, 2, KC, GROUP])
        ones_half = asb("ones_half", [P, 2, P])
        half_mask = asb("half_mask", [P, P])
        ones_col = asb("ones_col", [P, 1])
        attn_eps = asb("attn_eps", [P, 1])
        half_b_rz = asb("half_b_rz", [P, 4])
        b_xn = asb("b_xn", [P, 2])
        half_b_hn = asb("half_b_hn", [P, 2])
        ssq = aps("ssq", [P, 512])

        s_hi = sem("s_hi")
        s_lo = sem("s_lo")
        s_sqk = sem("s_sqk")
        s_sq = sem("s_sq")
        s_ss = sem("s_ss")

        def sum_squares(pe, run, pair, g4, wait_read=None):
            pe.wait_ge(s_sq, run + 1)
            if wait_read is not None:
                pe.wait_ge(*wait_read)
            for blk in range(BLK):
                col = (pair * GPP + g4) * BLK + blk
                last = nc.tensor.matmul(ssq[:, col:col + 1], square[:, g4 % 2, 0, blk * P:(blk + 1) * P],
                                        ones_col[:, :], start=True, stop=True)
            last.then_inc(s_ss, 1)

        def add_squares(pool, g):
            sq = square[:, g % 2, :, :]
            nc.gpsimd.tensor_tensor(sq[:, 0, :], sq[:, 0, :], sq[:, 1, :], ALU.add).then_inc(s_sq, 1)

        def ln_chain(dve, st, stats, mv, var, rstd, tmp):
            for t in range(mv.shape[1]):
                st.add(nc.vector.bn_aggr(mv[:, t, :], stats[:, t, :]))
            st.wait()
            st.do(nc.vector.tensor_scalar(var, mv[:, :, 1], LN_EPS, None, ALU.add))
            rsqrt_steps(nc.vector, st.do, rstd, var, tmp)

        G1 = GPP
        NT = G1 * BLK
        xv = x.rearrange("(g b p) d -> g p b d", b=BLK, p=P)
        t_x = sem("t_x")
        s_s0 = sem("s_s0")

        def turn_group(tile, banks):
            for blk in range(BLK):
                for k in range(KC):
                    last = nc.tensor.transpose(banks[:, k, blk * P:(blk + 1) * P], tile[:, blk, k * P:(k + 1) * P],
                                               ident[:, :])
            last.then_inc(t_x, 1)

        def first_low(dve, g):
            sl = slice(g * GROUP, (g + 1) * GROUP)
            dve.wait_ge(s_hi, g + 1)
            nc.vector.tensor_tensor(slots_lo[:, :, sl], slots[:, :, sl], slots_hi[:, :, sl].bitcast(F32),
                                    ALU.subtract).then_inc(s_lo, 1)

        with ExitStack() as setup:
            lsb, lps = tensors(setup)
            xs = lsb("xs", [P, NT, D])
            ctx_sb = lsb("ctx_sb", [P, M // P, D])
            ctx_sq = lsb("ctx_sq", [P, M // P, D])
            wq_sb = lsb("wq_sb", [P, KC, D])
            wk_sb = lsb("wk_sb", [P, KC, D])
            wv_sb = lsb("wv_sb", [P, KC, D])
            wih_sb = lsb("wih_sb", [P, KC, 3 * D])
            whh_sb = lsb("whh_sb", [P, KC, 3 * D])
            vecs = lsb("vecs", [P, 16])
            scaled_w = lsb("scaled_w", [P, 2])
            g_in = lsb("g_in", [P, 2])
            pn_t = lsb("pn_t", [P, KC, M])
            kp_t = lsb("kp_t", [P, KC, M])
            vp_t = lsb("vp_t", [P, KC, M])
            kq_f = lsb("kq_f", [P, KC, M])
            vw_f = lsb("vw_f", [P, PAIRS, 3 * D])
            stats = lsb("stats", [P, NT, 6])
            mv = lsb("mv", [P, NT, 2])
            var = lsb("var", [P, NT + 2])
            rstd = lsb("rstd", [P, NT + 2])
            rtmp = lsb("rtmp", [P, NT + 2])
            csum = lsb("csum", [P, 2])
            bank = lps("bank", [P, 3, 512])
            turn = lps("turn", [P, 2, KC, GROUP])
            W = 3 * D // 2
            vw_bank = (1, 2, 0, 1)

            l_ctx, l_wk, l_wv, l_wq, l_wih, l_whh, l_vec, l_g = (
                sem(f"loaded_{n}") for n in ("ctx", "wk", "wv", "wq", "wih", "whh", "vec", "g"))
            l_x = [sem(f"loaded_x{g}") for g in range(G1)]
            c_pool = sem("const_pool")
            c_act = sem("ctx_squares")
            v0 = sem("vector_setup")
            v_vec = sem("v_vec")
            t_pn = sem("t_pn")
            w_pn = sem("w_pn")
            m_w = sem("m_w")
            e_w = sem("e_w")
            a_whi = sem("a_whi")
            p_wlo = sem("p_wlo")
            n_x = sem("n_x")

            block = setup.enter_context(nc.Block())

            @block.sync
            def _(sp):
                sp.dma_start(ctx_sb[:, :, :], ctx_tok.rearrange("(t p) d -> p t d", p=P)).then_inc(l_ctx, 16)
                sp.dma_start(wk_sb[:, :, :], wk_t.rearrange("(k p) n -> p k n", p=P)).then_inc(l_wk, 16)
                sp.dma_start(xs[:, 0:BLK, :], xv[0]).then_inc(l_x[0], 16)
                sp.dma_start(wv_sb[:, :, :], wv_t.rearrange("(k p) n -> p k n", p=P)).then_inc(l_wv, 16)
                sp.dma_start(wq_sb[:, :, :], wq.rearrange("(k p) n -> p k n", p=P)).then_inc(l_wq, 16)
                sp.dma_start(xs[:, 2 * BLK:3 * BLK, :], xv[2]).then_inc(l_x[2], 16)
                sp.dma_start(wih_sb[:, :, :], wih_t.rearrange("(k p) n -> p k n", p=P)).then_inc(l_wih, 16)
                sp.dma_start(g_in[:, :], tanh_in.rearrange("(a n) -> a n", a=1).to_broadcast([P, 2])).then_inc(l_g, 16)

            @block.scalar
            def _(act):
                act.dma_start(vecs[:, :], vectors).then_inc(l_vec, 16)
                for g in range(1, G1, 2):
                    act.dma_start(xs[:, g * BLK:(g + 1) * BLK, :], xv[g]).then_inc(l_x[g], 16)
                act.dma_start(whh_sb[:, :, :], whh_t.rearrange("(k p) n -> p k n", p=P)).then_inc(l_whh, 16)
                act.wait_ge(l_ctx, 16)
                for t in range(M // P):
                    nc.scalar.activation(ctx_sq[:, t, :], ctx_sb[:, t, :], ACT.Square,
                                         accum_out=csum[:, t:t + 1]).then_inc(c_act, 1)
                act.wait_ge(l_whh, 16)
                nc.scalar.activation(whh_hi[:, :, :], whh_sb[:, :, :], ACT.Copy).then_inc(a_whi, 1)
                for i, dst in enumerate((kp_t, vp_t)):
                    act.wait_ge(m_w, i + 1)
                    nc.scalar.activation(dst[:, :, :], bank[:, 1 + i, :], ACT.Copy).then_inc(e_w, 1)
                act.wait_ge(l_g, 16)
                nc.scalar.activation(tanh_g[:, :], g_in[:, :], ACT.Tanh).then_inc(c_act, 1)
                act.wait_ge(m_w, 3)
                act.wait_ge(v_vec, 1)
                for k in range(KC):
                    last = nc.scalar.activation(kq_f[:, k, :], bank[:, 0, k * M:(k + 1) * M], ACT.Copy,
                                                scale=scaled_w[:, k:k + 1])
                last.then_inc(e_w, 1)
                act.wait_ge(e_w, 3)
                act.wait_ge(c_pool, 12)
                for b in range(B):
                    lo = (b % 2) * MB
                    nc.scalar.activation(kq_hi[:, :, b, lo:lo + MB], kq_f[:, :, b * MB:(b + 1) * MB],
                                         ACT.Copy).then_inc(a_whi, 1)
                for n in range(2 * PAIRS):
                    act.wait_ge(m_w, 4 + n)
                    nc.scalar.activation(vw_f[:, n // 2, (n % 2) * W:(n % 2 + 1) * W], bank[:, vw_bank[n], 0:W],
                                         ACT.Copy).then_inc(e_w, 1)
                act.wait_ge(e_w, 3 + 2 * PAIRS)
                nc.scalar.activation(vw_hi[:, :, :], vw_f[:, :, :], ACT.Copy).then_inc(a_whi, 1)
                for g in range(G1):
                    act.wait_ge(s_s0, g + 1)
                    sl = slice(g * GROUP, (g + 1) * GROUP)
                    nc.scalar.activation(slots_hi[:, :, sl], slots[:, :, sl], ACT.Copy).then_inc(s_hi, 1)
                    if g >= 2:
                        act.wait_ge(s_ss, g - 1)
                    nc.scalar.activation(square[:, g % 2, :, :], slots[:, :, sl], ACT.Square).then_inc(s_sqk, 1)

            @block.gpsimd
            def _(pool):
                nc.gpsimd.memset(ident[:, :], 0.0).then_inc(c_pool, 1)
                nc.gpsimd.memset(ones_half[:, :, :], 0.0).then_inc(c_pool, 1)
                nc.gpsimd.memset(half_mask[:, :], 0.0).then_inc(c_pool, 1)
                nc.gpsimd.memset(kq_hi[:, :, :, :].bitcast(F32), 0.0).then_inc(c_pool, 1)
                nc.gpsimd.memset(kq_lo[:, :, :, :].bitcast(F32), 0.0).then_inc(c_pool, 1)
                pool.wait_ge(c_pool, 5)
                nc.gpsimd.affine_select(out=ident[:, :], in_=ident[:, :], compare_op=ALU.not_equal, fill=1.0,
                                        base=0, pattern=[[-1, P]], channel_multiplier=1).then_inc(c_pool, 1)
                nc.gpsimd.memset(ones_half[:, 0, 0:MB], 1.0).then_inc(c_pool, 1)
                nc.gpsimd.memset(ones_half[:, 1, MB:P], 1.0).then_inc(c_pool, 1)
                nc.gpsimd.memset(half_mask[0:MB, 0:MB], 1.0).then_inc(c_pool, 1)
                nc.gpsimd.memset(ones_col[:, :], 1.0).then_inc(c_pool, 1)
                nc.gpsimd.memset(attn_eps[:, :], ATTN_EPS).then_inc(c_pool, 1)
                pool.wait_ge(c_pool, 11)
                nc.gpsimd.memset(half_mask[MB:P, MB:P], 1.0).then_inc(c_pool, 1)
                pool.wait_ge(c_pool, 12)
                pool.wait_ge(a_whi, 1)
                nc.gpsimd.tensor_tensor(whh_lo[:, :, :], whh_sb[:, :, :], whh_hi[:, :, :].bitcast(F32),
                                        ALU.subtract).then_inc(p_wlo, 1)
                for b in range(B):
                    lo = (b % 2) * MB
                    pool.wait_ge(a_whi, 2 + b)
                    nc.gpsimd.tensor_tensor(kq_lo[:, :, b, lo:lo + MB], kq_f[:, :, b * MB:(b + 1) * MB],
                                            kq_hi[:, :, b, lo:lo + MB].bitcast(F32), ALU.subtract).then_inc(p_wlo, 1)
                for g in range(G1):
                    pool.wait_ge(s_sqk, g + 1)
                    add_squares(pool, g)
                    if g == 0:
                        pool.wait_ge(a_whi, 2 + B)
                        nc.gpsimd.tensor_tensor(vw_lo[:, :, :], vw_f[:, :, :], vw_hi[:, :, :].bitcast(F32),
                                                ALU.subtract).then_inc(p_wlo, 1)

            @block.tensor
            def _(pe):
                pe.wait_ge(c_pool, 12)
                pe.wait_ge(v0, V_PN)
                for t in range(M // P):
                    for k in range(KC):
                        last = nc.tensor.transpose(bank[:, 0, k * M + t * P:k * M + (t + 1) * P],
                                                   ctx_sb[:, t, k * P:(k + 1) * P], ident[:, :])
                last.then_inc(t_pn, 1)
                pe.wait_ge(w_pn, 1)
                for w, (l, n) in enumerate(((wk_sb, l_wk), (wv_sb, l_wv))):
                    pe.wait_ge(n, 16)
                    for j in range(KC):
                        for k in range(KC):
                            last = nc.tensor.matmul(bank[:, 1 + w, j * M:(j + 1) * M], l[:, k, j * P:(j + 1) * P],
                                                    pn_t[:, k, :], start=(k == 0), stop=(k == KC - 1))
                    last.then_inc(m_w, 1)
                pe.wait_ge(e_w, 1)
                pe.wait_ge(l_wq, 16)
                for j in range(KC):
                    for k in range(KC):
                        last = nc.tensor.matmul(bank[:, 0, j * M:(j + 1) * M], wq_sb[:, k, j * P:(j + 1) * P],
                                                kp_t[:, k, :], start=(k == 0), stop=(k == KC - 1))
                last.then_inc(m_w, 1)
                pe.wait_ge(l_wih, 16)
                for n in range(2 * PAIRS):
                    pe.wait_ge(e_w, max(2 + n - (n > 0), 2))
                    for k in range(KC):
                        last = nc.tensor.matmul(bank[:, vw_bank[n], 0:W], vp_t[:, k, (n // 2) * P:(n // 2 + 1) * P],
                                                wih_sb[:, k, (n % 2) * W:(n % 2 + 1) * W],
                                                start=(k == 0), stop=(k == KC - 1))
                    last.then_inc(m_w, 1)
                for g in range(G1):
                    pe.wait_ge(n_x, (g + 1) * BLK)
                    if g >= 2:
                        pe.wait_ge(s_s0, g - 1)
                    turn_group(xs[:, g * BLK:(g + 1) * BLK, :], turn[:, g % 2, :, :])
                    if g >= 2:
                        sum_squares(pe, g - 2, 0, g - 2)

            @block.vector
            def _(dve):
                st = Steps(dve, v0)
                dve.wait_ge(c_act, 2)
                st.do(nc.vector.tensor_scalar(var[:, NT:NT + 2], csum[:, :], 1.0 / D, RMS_EPS, ALU.mult, ALU.add))
                rsqrt_steps(nc.vector, st.do, rstd[:, NT:NT + 2], var[:, NT:NT + 2], rtmp[:, NT:NT + 2])
                for t in range(M // P):
                    st.add(nc.vector.tensor_scalar(ctx_sb[:, t, :], ctx_sb[:, t, :], rstd[:, NT + t:NT + t + 1],
                                                   None, ALU.mult))
                assert st.n == V_PN
                dve.wait_ge(l_vec, 16)
                nc.vector.tensor_scalar(scaled_w[:, :], vecs[:, 12:14], SCALE, None, ALU.mult).then_inc(v_vec, 1)
                for g in range(G1):
                    dve.wait_ge(l_x[g], 16)
                    for t in range(g * BLK, (g + 1) * BLK):
                        st.add(nc.vector.bn_stats(stats[:, t, :], xs[:, t, :]))
                    if g == 0:
                        dve.wait_ge(t_pn, 1)
                        for k in range(KC):
                            last = nc.vector.tensor_scalar(pn_t[:, k, :], bank[:, 0, k * M:(k + 1) * M],
                                                           vecs[:, 14 + k:15 + k], None, ALU.mult)
                        last.then_inc(w_pn, 1)
                st.wait()
                ln_chain(dve, st, stats, mv, var[:, 0:NT], rstd[:, 0:NT], rtmp[:, 0:NT])

                def normalise(g):
                    for t in range(g * BLK, (g + 1) * BLK):
                        nc.vector.tensor_scalar(xs[:, t, :], xs[:, t, :], mv[:, t, 0:1], rstd[:, t:t + 1],
                                                ALU.subtract, ALU.mult).then_inc(n_x, 1)

                normalise(0)
                normalise(1)
                st.add(nc.vector.tensor_tensor(half_b_rz[:, :], vecs[:, 0:4], vecs[:, 6:10], ALU.add))
                st.add(nc.vector.tensor_copy(b_xn[:, :], vecs[:, 4:6]))
                st.add(nc.vector.tensor_scalar(half_b_hn[:, :], vecs[:, 10:12], 0.5, None, ALU.mult))
                st.wait()
                st.do(nc.vector.tensor_scalar(half_b_rz[:, :], half_b_rz[:, :], 0.5, None, ALU.mult))
                for g in range(G1):
                    dve.wait_ge(t_x, g + 1)
                    sl = slice(g * GROUP, (g + 1) * GROUP)
                    nc.vector.tensor_copy(slots[:, :, sl], turn[:, g % 2, :, :]).then_inc(s_s0, 1)
                    if g + 2 < G1:
                        normalise(g + 2)
                    first_low(dve, g)
        with ExitStack() as loop:
            lsb, lps = tensors(loop)
            tr = lsb("tr", [P, KC, GROUP])
            tz = lsb("tz", [P, KC, GROUP])
            hb = lsb("hb", [P, KC, GROUP])
            nn = lsb("nn", [P, KC, GROUP])
            pre = lsb("pre", [P, GROUP])
            dif = lsb("dif", [P, GROUP])
            expo = lsb("expo", [P, 2 * GROUP])
            rms_c = lsb("rms_c", [P, 2, GROUP])
            csum_c = lsb("csum_c", [P, 2, GROUP])
            attn_hi = lsb("attn_hi", [P, PAIRS, 2 * GROUP], F32R)
            attn_lo = lsb("attn_lo", [P, PAIRS, 2 * GROUP], F32R)
            diag = lsb("diag", [P, GPP * BLK, P])
            rsum = lsb("rsum", [P, P])
            ms = lsb("ms", [P, GPP * BLK])
            rms = lsb("rms", [P, GPP * BLK])
            rms_t = lsb("rms_t", [P, GPP * BLK])
            stats1 = lsb("stats1", [P, NT, 6])
            mv1 = lsb("mv1", [P, NT, 2])
            var1 = lsb("var1", [P, NT])
            rstd1 = lsb("rstd1", [P, NT])
            shift1 = lsb("shift1", [P, NT])
            rtmp1 = lsb("rtmp1", [P, NT])
            top = lsb("top", [P, 1])
            neg_top = lsb("neg_top", [P, 1])
            den = lsb("den", [P, 1])
            rden = lsb("rden", [P, 1])

            gate_banks = lps("gate_banks", [P, 4, GROUP])
            gate_r, gate_z, gate_h, gate_x = (gate_banks[:, i, :] for i in range(4))
            rms_b = lps("rms_b", [P, GROUP])
            score = lps("score", [P, 2, GROUP])

            m_r, m_z, m_h, m_x = (sem(f"m_{n}") for n in "rzhx")
            a_r, a_z, a_h, a_n = (sem(f"a_{n}") for n in "rzhn")
            v_q = sem("v_q")
            v_pre, v_dif, v_mix, v_new = (sem(f"v_{n}") for n in ("pre", "dif", "mix", "new"))
            v_ms = sem("v_ms")
            v_rms = sem("v_rms")
            v_diag = sem("v_diag")
            m_score, m_rms, m_csum = sem("m_score"), sem("m_rms"), sem("m_csum")
            a_rms, a_csum = sem("a_rms"), sem("a_csum")
            v_mul, v_top, v_neg, a_exp, v_rden, v_rsum = (sem(n) for n in
                                                          ("v_mul", "v_top", "v_neg", "a_exp", "v_rden", "v_rsum"))
            v_rec, v_attn, a_attn, v_alo = sem("v_rec"), sem("v_attn"), sem("a_attn"), sem("v_alo")
            l_x1 = [sem(f"loaded_x{g}") for g in range(G1, G)]
            v_ln1 = sem("v_ln1")
            v_sh1 = sem("v_sh1")
            n_x1 = sem("n_x1")

            def x_tile(g):
                return (tr, tz, hb, nn)[g - G1][:, :, :].rearrange("p k (b d) -> p (k b) d", d=D)

            def turn_banks1(g):
                return gate_banks[:, g % 2 * KC:(g % 2 + 1) * KC, :]

            UNITS = 2 * G

            def tokens(pair, g4):
                g = pair * GPP + g4
                return slice(g * GROUP, (g + 1) * GROUP)

            block = loop.enter_context(nc.Block())

            @block.sync
            def _(sp):
                for g in range(G1, G):
                    sp.dma_start(x_tile(g), xv[g]).then_inc(l_x1[g - G1], 16)

            @block.tensor
            def _(pe):
                def gru_unit(it, pair, g4, c):
                    u = it * UNITS + (pair * GPP + g4) * 2 + c
                    sl = tokens(pair, g4)
                    rows = slice((g4 // 2) * MB, (g4 // 2 + 1) * MB)
                    half = slice((g4 % 2) * GROUP, (g4 % 2 + 1) * GROUP)
                    if c == 0:
                        pe.wait_ge(s_hi, it * G + pair * GPP + g4 + 1)
                        pe.wait_ge(s_lo, it * G + pair * GPP + g4 + 1)

                    def from_slots(out, f, stop):
                        n = 0
                        for k in range(KC):
                            for w, s in ((whh_hi, slots_hi), (whh_hi, slots_lo), (whh_lo, slots_hi)):
                                n += 1
                                last = nc.tensor.matmul(out[:, :], w[:, k, f * P:(f + 1) * P], s[:, k, sl],
                                                        start=(n == 1), stop=(stop and n == 3 * KC))
                        return last

                    def from_attention(out, f, start):
                        for n, (w, a) in enumerate(((vw_hi, attn_hi), (vw_hi, attn_lo), (vw_lo, attn_hi))):
                            last = nc.tensor.matmul(out[:, :], w[rows, pair, f * P:(f + 1) * P],
                                                    a[rows, pair, half], start=(start and n == 0), stop=(n == 2))
                        return last

                    pe.wait_ge(a_r, u + 1)
                    from_slots(gate_r, c, False)
                    if c == 0:
                        pe.wait_ge(a_attn, 4 * it + 2 * pair + g4 % 2 + 1)
                        pe.wait_ge(v_alo, 4 * it + 2 * pair + g4 % 2 + 1)
                    from_attention(gate_r, c, False).then_inc(m_r, 1)
                    pe.wait_ge(a_z, u + 1)
                    from_slots(gate_z, 2 + c, False)
                    from_attention(gate_z, 2 + c, False).then_inc(m_z, 1)
                    pe.wait_ge(a_h, u + 1)
                    from_slots(gate_h, 4 + c, True).then_inc(m_h, 1)
                    pe.wait_ge(v_pre, u + 1)
                    from_attention(gate_x, 4 + c, True).then_inc(m_x, 1)

                def scores(s, pair):
                    for h in range(2):
                        n = 0
                        for b in range(2):
                            sl = tokens(pair, 2 * b + h)
                            for k in range(KC):
                                for w, x_ in ((kq_hi, slots_hi), (kq_hi, slots_lo), (kq_lo, slots_hi)):
                                    n += 1
                                    last = nc.tensor.matmul(score[:, h, :], w[:, k, 2 * pair + b, :], x_[:, k, sl],
                                                            start=(n == 1), stop=(n == 6 * KC))
                        last.then_inc(m_score, 1)

                def spread_rms(s, h):
                    if h == 0:
                        pe.wait_ge(v_diag, s + 1)
                    else:
                        pe.wait_ge(a_rms, 2 * s + 1)
                    for blk in range(BLK):
                        for b in range(2):
                            last = nc.tensor.matmul(rms_b[:, blk * P:(blk + 1) * P], ones_half[:, b, :],
                                                    diag[:, (2 * b + h) * BLK + blk, :], start=(b == 0), stop=(b == 1))
                    last.then_inc(m_rms, 1)

                def column_sums(s):
                    pe.wait_ge(v_rsum, s + 1)
                    for h in range(2):
                        nc.tensor.matmul(score[:, h, :], rsum[:, :], expo[:, h * GROUP:(h + 1) * GROUP],
                                         start=True, stop=True).then_inc(m_csum, 1)

                def half_iteration(it, pair, softmax, more):
                    s = 2 * it + pair + 1
                    first_run = G * it + GPP * pair + G
                    gru_unit(it, pair, 0, 0)
                    gru_unit(it, pair, 0, 1)
                    if softmax:
                        sum_squares(pe, first_run - 1, 1 - pair, GPP - 1, (v_ms, s))
                        pe.wait_ge(s_hi, first_run)
                        pe.wait_ge(s_lo, first_run)
                        scores(s, 1 - pair)
                    gru_unit(it, pair, 1, 0)
                    if softmax:
                        spread_rms(s, 0)
                    gru_unit(it, pair, 1, 1)
                    if softmax:
                        spread_rms(s, 1)
                    if more:
                        sum_squares(pe, first_run, pair, 0, (v_ms, s + 1))
                    gru_unit(it, pair, 2, 0)
                    gru_unit(it, pair, 2, 1)
                    if softmax:
                        column_sums(s)
                    if more:
                        sum_squares(pe, first_run + 1, pair, 1, (v_ms, s + 1))
                    gru_unit(it, pair, 3, 0)
                    gru_unit(it, pair, 3, 1)
                    if more:
                        sum_squares(pe, first_run + 2, pair, 2, (v_ms, s + 1))

                def turn_first(g):
                    pe.wait_ge(n_x1, g - G1 + 1)
                    if g >= G1 + 2:
                        pe.wait_ge(s_s0, g - 1)
                    turn_group(x_tile(g), turn_banks1(g))

                sum_squares(pe, G1 - 2, 0, G1 - 2)
                sum_squares(pe, G1 - 1, 0, G1 - 1)
                scores(0, 0)
                spread_rms(0, 0)
                spread_rms(0, 1)
                column_sums(0)
                for g in range(G1, G):
                    turn_first(g)
                for g in range(G1, G - 1):
                    sum_squares(pe, g, 1, g - G1, (v_ms, 1))
                pe.wait_ge(s_s0, G)
                with pe.Fori(0, ITERS - 1) as it:
                    half_iteration(it, 0, True, True)
                    half_iteration(it, 1, True, True)
                half_iteration(ITERS - 1, 0, True, False)
                half_iteration(ITERS - 1, 1, False, False)

            @block.scalar
            def _(act):
                def gru_unit(it, pair, g4, c, meanwhile=None):
                    u = it * UNITS + (pair * GPP + g4) * 2 + c
                    act.wait_ge(v_q, u + 2)
                    act.wait_ge(m_r, u + 1)
                    nc.scalar.activation(tr[:, c, :], gate_r[:, :], ACT.Tanh, bias=half_b_rz[:, c:c + 1],
                                         scale=0.5).then_inc(a_r, 1)
                    act.wait_ge(m_z, u + 1)
                    nc.scalar.activation(tz[:, c, :], gate_z[:, :], ACT.Tanh, bias=half_b_rz[:, 2 + c:3 + c],
                                         scale=0.5).then_inc(a_z, 1)
                    act.wait_ge(m_h, u + 1)
                    nc.scalar.activation(hb[:, c, :], gate_h[:, :], ACT.Identity, bias=half_b_hn[:, c:c + 1],
                                         scale=0.5).then_inc(a_h, 1)
                    if meanwhile is not None:
                        meanwhile()
                    act.wait_ge(v_pre, u + 2)
                    nc.scalar.activation(nn[:, c, :], pre[:, :], ACT.Tanh, bias=b_xn[:, c:c + 1]).then_inc(a_n, 1)

                def slots_high(it, pair, g4):
                    act.wait_ge(v_new, it * UNITS + (pair * GPP + g4) * 2 + 2)
                    sl = tokens(pair, g4)
                    nc.scalar.activation(slots_hi[:, :, sl], slots[:, :, sl], ACT.Copy).then_inc(s_hi, 1)

                def copy_rms(s, h):
                    act.wait_ge(m_rms, 2 * s + h + 1)
                    nc.scalar.activation(rms_c[:, h, :], rms_b[:, :], ACT.Copy).then_inc(a_rms, 1)

                def exponentials(s):
                    act.wait_ge(v_neg, s + 1)
                    nc.scalar.activation(expo[:, :], expo[:, :], ACT.Exp, bias=neg_top[:, :],
                                         accum_out=den[:, :]).then_inc(a_exp, 1)

                def copy_csum(s):
                    for h in range(2):
                        act.wait_ge(m_csum, 2 * s + h + 1)
                        nc.scalar.activation(csum_c[:, h, :], score[:, h, :], ACT.Identity,
                                             bias=attn_eps[:, :]).then_inc(a_csum, 1)

                def attention_hi(s, pair, h):
                    act.wait_ge(v_attn, 2 * s + h + 1)
                    half = slice(h * GROUP, (h + 1) * GROUP)
                    nc.scalar.activation(attn_hi[:, pair, half], expo[:, half], ACT.Copy).then_inc(a_attn, 1)

                def half_iteration(it, pair, softmax, more=True):
                    s = 2 * it + pair + 1

                    def high(p, g4):
                        return (lambda: slots_high(it, p, g4)) if more else None

                    gru_unit(it, pair, 0, 0, high(0, GPP - 1) if pair == 1 else None)
                    attention_hi(s - 1, pair, 1)
                    gru_unit(it, pair, 0, 1)
                    gru_unit(it, pair, 1, 0, high(pair, 0))
                    if softmax:
                        copy_rms(s, 0)
                    gru_unit(it, pair, 1, 1)
                    if softmax:
                        copy_rms(s, 1)
                    gru_unit(it, pair, 2, 0, high(pair, 1))
                    if softmax:
                        exponentials(s)
                    gru_unit(it, pair, 2, 1)
                    if softmax:
                        copy_csum(s)
                    gru_unit(it, pair, 3, 0, high(pair, 2))
                    if softmax:
                        attention_hi(s, 1 - pair, 0)
                    gru_unit(it, pair, 3, 1)
                    if more and pair == 1:
                        slots_high(it, pair, GPP - 1)

                for free in (a_r, a_z, a_h):
                    act.sem_inc(free, 1)
                def normalise(g):
                    act.wait_ge(v_sh1, 1)
                    for b in range(BLK):
                        t = (g - G1) * BLK + b
                        last = nc.scalar.activation(x_tile(g)[:, b, :], x_tile(g)[:, b, :], ACT.Identity,
                                                    bias=shift1[:, t:t + 1], scale=rstd1[:, t:t + 1])
                    last.then_inc(n_x1, 1)

                def first_slots(g):
                    sl = slice(g * GROUP, (g + 1) * GROUP)
                    act.wait_ge(t_x, g + 1)
                    nc.scalar.activation(slots[:, :, sl], turn_banks1(g), ACT.Copy).then_inc(s_s0, 1)

                copy_rms(0, 0)
                copy_rms(0, 1)
                exponentials(0)
                copy_csum(0)
                normalise(G1)
                normalise(G1 + 1)
                first_slots(G1)
                normalise(G1 + 2)
                first_slots(G1 + 1)
                attention_hi(0, 0, 0)
                normalise(G1 + 3)
                first_slots(G1 + 2)
                first_slots(G1 + 3)
                with act.Fori(0, ITERS - 1) as it:
                    half_iteration(it, 0, True)
                    half_iteration(it, 1, True)
                half_iteration(ITERS - 1, 0, True, more=False)
                half_iteration(ITERS - 1, 1, False, more=False)

            @block.vector
            def _(dve):
                def gru_unit(it, pair, g4, c, meanwhile=None):
                    u = it * UNITS + (pair * GPP + g4) * 2 + c
                    sl = tokens(pair, g4)
                    dve.wait_ge(a_r, u + 2)
                    dve.wait_ge(a_h, u + 2)
                    nc.vector.scalar_tensor_tensor(pre[:, :], tr[:, c, :], 1.0, hb[:, c, :], ALU.add,
                                                   ALU.mult).then_inc(v_q, 1)
                    dve.wait_ge(v_q, u + 3)
                    dve.wait_ge(m_x, u + 1)
                    nc.vector.tensor_tensor(pre[:, :], pre[:, :], gate_x[:, :], ALU.add).then_inc(v_pre, 1)
                    if meanwhile is not None:
                        meanwhile()
                    dve.wait_ge(a_n, u + 1)
                    nc.vector.tensor_tensor(dif[:, :], slots[:, c, sl], nn[:, c, :], ALU.subtract).then_inc(v_dif, 1)
                    dve.wait_ge(v_dif, u + 1)
                    dve.wait_ge(a_z, u + 2)
                    nc.vector.scalar_tensor_tensor(dif[:, :], tz[:, c, :], 1.0, dif[:, :], ALU.add,
                                                   ALU.mult).then_inc(v_mix, 1)
                    dve.wait_ge(v_mix, u + 1)
                    nc.vector.scalar_tensor_tensor(slots[:, c, sl], dif[:, :], 0.5, nn[:, c, :], ALU.mult,
                                                   ALU.add).then_inc(v_new, 1)

                def token_rms(s, pair):
                    dve.wait_ge(s_ss, GPP * (s + 1))
                    cols = slice(pair * GPP * BLK, (pair + 1) * GPP * BLK)
                    nc.vector.tensor_scalar(ms[:, :], ssq[:, cols], 1.0 / D, RMS_EPS, ALU.mult,
                                            ALU.add).then_inc(v_ms, 1)
                    dve.wait_ge(v_ms, s + 1)
                    n = [0]

                    def do(ins):
                        n[0] += 1
                        ins.then_inc(v_rms, 1)
                        dve.wait_ge(v_rms, s * 11 + n[0])

                    rsqrt_steps(nc.vector, do, rms[:, :], ms[:, :], rms_t[:, :])
                    assert n[0] == 11
                    w = GPP * BLK
                    nc.vector.tensor_tensor(
                        diag[:, :, :], ident[:, :].rearrange("p (a q) -> p a q", a=1).to_broadcast([P, w, P]),
                        rms[:, :].rearrange("p (w a) -> p w a", a=1).to_broadcast([P, w, P]),
                        ALU.mult).then_inc(v_diag, 1)

                def scale_scores(s, h):
                    dve.wait_ge(m_score, 2 * s + h + 1)
                    dve.wait_ge(a_rms, 2 * s + h + 1)
                    nc.vector.tensor_tensor(expo[:, h * GROUP:(h + 1) * GROUP], score[:, h, :], rms_c[:, h, :],
                                            ALU.mult).then_inc(v_mul, 1)

                def maximum(s):
                    dve.wait_ge(v_mul, 2 * s + 2)
                    nc.vector.reduce_max(top[:, :], expo[:, :], AX).then_inc(v_top, 1)
                    dve.wait_ge(v_top, s + 1)
                    nc.vector.tensor_scalar(neg_top[:, :], top[:, :], -1.0, None, ALU.mult).then_inc(v_neg, 1)

                def token_sum(s):
                    dve.wait_ge(a_exp, s + 1)
                    nc.vector.reciprocal(rden[:, :], den[:, :]).then_inc(v_rden, 1)
                    dve.wait_ge(v_rden, s + 1)
                    nc.vector.tensor_scalar(rsum[:, :], half_mask[:, :], rden[:, :], None, ALU.mult).then_inc(v_rsum, 1)

                def half_of(h):
                    return slice(h * GROUP, (h + 1) * GROUP)

                def csum_reciprocal(s, h):
                    dve.wait_ge(a_csum, 2 * s + h + 1)
                    nc.vector.reciprocal(csum_c[:, h, :], csum_c[:, h, :]).then_inc(v_rec, 1)

                def attention_half(s, h):
                    dve.wait_ge(v_rec, 2 * s + h + 1)
                    nc.vector.scalar_tensor_tensor(expo[:, half_of(h)], expo[:, half_of(h)], rden[:, :], csum_c[:, h, :],
                                                   ALU.mult, ALU.mult).then_inc(v_attn, 1)

                def attention_lo(s, pair, h):
                    dve.wait_ge(a_attn, 2 * s + h + 1)
                    nc.vector.tensor_tensor(attn_lo[:, pair, half_of(h)], expo[:, half_of(h)],
                                            attn_hi[:, pair, half_of(h)].bitcast(F32), ALU.subtract).then_inc(v_alo, 1)

                def half_iteration(it, pair, softmax):
                    s = 2 * it + pair + 1
                    gru_unit(it, pair, 0, 0)
                    gru_unit(it, pair, 0, 1, lambda: attention_lo(s - 1, pair, 1))
                    if softmax:
                        token_rms(s, 1 - pair)
                    gru_unit(it, pair, 1, 0)
                    if softmax:
                        scale_scores(s, 0)
                    gru_unit(it, pair, 1, 1)
                    if softmax:
                        scale_scores(s, 1)
                        maximum(s)
                    gru_unit(it, pair, 2, 0)
                    if softmax:
                        token_sum(s)
                    gru_unit(it, pair, 2, 1)
                    if softmax:
                        csum_reciprocal(s, 0)
                    gru_unit(it, pair, 3, 0, (lambda: attention_half(s, 0)) if softmax else None)
                    if softmax:
                        csum_reciprocal(s, 1)
                        attention_lo(s, 1 - pair, 0)
                    gru_unit(it, pair, 3, 1, (lambda: attention_half(s, 1)) if softmax else None)

                dve.sem_inc(v_q, 2)
                dve.sem_inc(v_pre, 1)
                token_rms(0, 0)
                ln = Steps(dve, v_ln1)
                for g in range(G1, G):
                    dve.wait_ge(l_x1[g - G1], 16)
                    for b in range(BLK):
                        ln.add(nc.vector.bn_stats(stats1[:, (g - G1) * BLK + b, :], x_tile(g)[:, b, :]))
                    if g == G1 + 1:
                        scale_scores(0, 0)
                        scale_scores(0, 1)
                        maximum(0)
                token_sum(0)
                ln.wait()
                ln_chain(dve, ln, stats1, mv1, var1[:, :], rstd1[:, :], rtmp1[:, :])
                nc.vector.scalar_tensor_tensor(shift1[:, :], mv1[:, :, 0], -1.0, rstd1[:, :], ALU.mult,
                                               ALU.mult).then_inc(v_sh1, 1)
                csum_reciprocal(0, 0)
                attention_half(0, 0)
                csum_reciprocal(0, 1)
                attention_lo(0, 0, 0)
                attention_half(0, 1)
                for g in range(G1, G):
                    sl = slice(g * GROUP, (g + 1) * GROUP)
                    dve.wait_ge(s_s0, g + 1)
                    nc.vector.tensor_copy(slots_hi[:, :, sl], slots[:, :, sl]).then_inc(s_hi, 1)
                    first_low(dve, g)
                with dve.Fori(0, ITERS - 1) as it:
                    half_iteration(it, 0, True)
                    half_iteration(it, 1, True)
                half_iteration(ITERS - 1, 0, True)
                half_iteration(ITERS - 1, 1, False)

            @block.gpsimd
            def _(pool):
                def multiply(g):
                    sl = slice(g * GROUP, (g + 1) * GROUP)
                    nc.gpsimd.tensor_tensor(square[:, g % 2, :, :], slots[:, :, sl], slots[:, :, sl],
                                            ALU.mult).then_inc(s_sqk, 1)

                for g in range(G1, G):
                    pool.wait_ge(s_s0, g + 1)
                    pool.wait_ge(s_ss, g - 1)
                    multiply(g)
                    pool.wait_ge(s_sqk, g + 1)
                    add_squares(pool, g)
                with pool.Fori(0, ITERS - 1) as it:
                    for g in range(G):
                        run = it * G + g + G
                        pool.wait_ge(v_new, it * UNITS + 2 * g + 2)
                        pool.wait_ge(s_ss, run - 1)
                        sl = slice(g * GROUP, (g + 1) * GROUP)
                        multiply(g)
                        pool.wait_ge(s_sqk, run + 1)
                        add_squares(pool, g)
                        pool.wait_ge(s_hi, run + 1)
                        nc.gpsimd.tensor_tensor(slots_lo[:, :, sl], slots[:, :, sl], slots_hi[:, :, sl].bitcast(F32),
                                                ALU.subtract).then_inc(s_lo, 1)
        attention.close()
        E = gate_t.shape[1]
        CAP = -(-T // E) * 2
        WCOL = 6 * P
        FS = w_shared.shape[1]
        FE = w_expert.shape[2]
        HALF_F = FE // 2
        LAG = 2
        G_BIS = G // 2
        ROW = D + E
        BIG = 8192.0
        HALF_T = T // 2
        AW, BW = 32, 16
        W = BLK * G
        HOT = W // (2 * FS)
        assert G * E == P and CAP == AW * BW and 2 * FS * G_BIS >= 30 and E % BLK == 0 and FS == BLK == 4
        rows = nc.dram_tensor("token_rows", (T, ROW), F32, kind="Internal").ap()
        ids = nc.dram_tensor("token_ids", (E, CAP), U32, kind="Internal").ap()
        xrows = x.rearrange("(g b p) (k q) -> g p k b q", b=BLK, p=P, k=KC)
        hrows = rows[:, 0:D].rearrange("(g b p) (k q) -> g p k b q", b=BLK, p=P, k=KC)

        def right(name, shape, dt=F32):
            return whole.enter_context(nc.sbuf_tensor(name, shape, dt, side="right"))

        raw = right("raw", [P, FE, WCOL])
        idx_all = right("idx_all", [P, E, BLK], U32)
        idx_in = right("idx_in", [P, BLK], U32)
        got = right("got", [P, BLK, ROW])
        l_w = [sem("l_w0"), sem("l_w1")]
        l_idx, p_idx, g_in_ = sem("l_idx"), sem("p_idx"), sem("gathered")

        with ExitStack() as dense:
            lsb, lps = tensors(dense)
            sg = lsb("sg", [P, GROUP])
            thr = lsb("thr", [P, 1], I32)
            same_e = lsb("same_e", [P, P])
            before = lsb("before", [P, P])
            work = lsb("work", [P, 8, GROUP])
            xg = work[:, 0:4, :].rearrange("p (s k) t -> p s k t", k=KC)
            hg = work[:, 4:8, :].rearrange("p (s k) t -> p s k t", k=KC)
            gw_f = lsb("gw_f", [P, KC, E])
            gw_hi = lsb("gw_hi", [P, KC, 2 * P - E], F32R)
            gw_lo = lsb("gw_lo", [P, KC, 2 * P - E], F32R)
            sh_hi = lsb("sh_hi", [P, FS, WCOL], F32R)
            sh_lo = lsb("sh_lo", [P, FS, WCOL], F32R)
            silu = lsb("silu", [P, 2, GROUP])
            hid = lsb("hid", [P, 2, GROUP])
            hid_hi = lsb("hid_hi", [P, FS, GROUP], F32R)
            hid_lo = lsb("hid_lo", [P, FS, GROUP], F32R)
            y = lsb("y", [P, BLK, D])
            stats2 = lsb("stats2", [P, 2 * BLK, 6])
            mv2 = lsb("mv2", [P, 2 * BLK, 2])
            var2 = lsb("var2", [P, 2 * BLK])
            rstd2 = lsb("rstd2", [P, 2, 2 * BLK])
            shift2 = lsb("shift2", [P, 2, 2 * BLK])
            rtmp2 = lsb("rtmp2", [P, 2 * BLK])
            bit = lsb("bit", [P, 1], I32)
            cand = lsb("cand", [P, 1], I32)
            keep = lsb("keep", [P, 1], I32)
            cnt = lsb("cnt", [P, 1])
            score_t = lsb("score_t", [P, GROUP])
            tots = lsb("tots", [P, 4])
            offs = lsb("offs", [P, 4])
            hi_f = lsb("hi_f", [P, GROUP], F16)
            lo_f = lsb("lo_f", [P, GROUP], F16)
            iota_i = lsb("iota_i", [P, AW], I32)
            iota_f = lsb("iota_f", [P, AW], F16)
            tok_i = lsb("tok_i", [P, W], I32)
            tok_f = lsb("tok_f", [P, W])
            ids_sb = lsb("ids_sb", [P, E // BLK, BW], U32)
            wide = lps("wide", [P, 4, 512])
            down = lps("down", [P, 2, 512])
            logit = lps("logit", [P, 512])
            small = lps("small", [P, 512])

            above = work[:, 0, :]
            tie = work[:, 1, :]
            count = work[:, 2, :]
            taken = work[:, 3, :]
            slot = work[:, 4, :]
            ones = work[:, 5, :]
            slot_i = work[:, 6, :].bitcast(I32)
            hi_i = work[:, 7, :].bitcast(I32)
            lo_i = work[:, 0, :].bitcast(I32)
            h_f = (silu, hid)
            hot_b = work[:, :, :].rearrange("p a b -> p (a b)").bitcast(F16).rearrange("p (w e b) -> p w (e b)", e=E, b=BW)
            HOT_F = HOT * E * AW // 2
            free = [got[:, :, :].rearrange("p b c -> p (b c)")]
            free += [raw[:, HALF_F:FE, :].rearrange("p f c -> p (f c)")[:, i * HOT_F:] for i in range(3)]
            free += [slots[:, k, i * HOT_F:] for k in range(KC) for i in range(G_BIS * GROUP // HOT_F)]
            hot_a = [part[:, 0:HOT_F].bitcast(F16).rearrange("p (w e a) -> p w (e a)", e=E, a=AW) for part in free]
            assert len(hot_a) * HOT == W

            l_sh, l_gw = sem("l_sh"), sem("l_gw")
            l_xg = [sem(f"l_xg{i}") for i in range(2)]
            w_rows = [sem(f"w_rows{i}") for i in range(2)]
            p2 = sem("p2")
            t_tok, t_h = sem("t_tok"), sem("t_h")
            v2 = sem("v2")
            v_x1, v_ln, a_norm = sem("v_x1"), sem("v_ln"), sem("a_norm")
            a_hf, a_hh, h_lo = sem("a_hf"), sem("a_hh"), sem("h_lo")
            v_gw, p_sh, a_sh = sem("v_gw"), sem("p_sh"), sem("a_sh")
            m_log, a_sg, t_score, a_score, w_score = (sem(n) for n in ("m_log", "a_sg", "t_score", "a_score", "w_score"))
            m_g, m_u, a_silu, v_hid, a_hid, p_lo = (sem(n) for n in ("m_g", "m_u", "a_silu", "v_hid", "a_hid", "p_lo"))
            m_dn, a_y, p_y, w_y = sem("m_dn"), sem("a_y"), sem("p_y"), sem("w_y")
            v_cnt, m_cnt, v_bis, v_bit = sem("v_cnt"), sem("m_cnt"), sem("v_bis"), sem("v_bit")
            v_tot, m_tot, v_slot, t_slot = sem("v_tot"), sem("m_tot"), sem("v_slot"), sem("t_slot")
            v_hot, a_hot, m_ids, v_ids, w_ids = (sem(n) for n in ("v_hot", "a_hot", "m_ids", "v_ids", "w_ids"))

            block = dense.enter_context(nc.Block())

            @block.sync
            def _(sp):
                def load_x(g):
                    if g >= 2:
                        sp.wait_ge(v_x1, g - 1)
                    for k in range(KC):
                        sp.dma_start(xg[:, g % 2, k, :].rearrange("p (b q) -> p b q", q=P),
                                     xrows[g, :, k]).then_inc(l_xg[g % 2], 16)

                def store_h(g):
                    sp.wait_ge(a_norm, g + 1)
                    for k in range(KC):
                        sp.dma_start(hrows[g, :, k], hg[:, g % 2, k, :].rearrange("p (b q) -> p b q", q=P))\
                            .then_inc(w_rows[g % 2], 16)

                load_x(0)
                load_x(1)
                sp.dma_start(gw_f[:, :, :], gate_t.rearrange("(k p) e -> p k e", p=P)).then_inc(l_gw, 16)
                sp.dma_start(raw[:, 0:FS, :], w_shared).then_inc(l_sh, 16)
                for g in range(2, G, 2):
                    load_x(g)
                    load_x(g + 1)
                    store_h(g - 2)
                    store_h(g - 1)
                store_h(G - 2)
                store_h(G - 1)
                sp.wait_ge(a_sh, 1)
                sp.wait_ge(p_sh, FS)
                sp.dma_start(raw[:, 0:HALF_F, :], w_expert[0, :, 0:HALF_F, :]).then_inc(l_w[0], 16)
                sp.wait_ge(a_score, 1)
                srows = rows[:, D:ROW].rearrange("(g c p) e -> c p g e", c=BLK, p=P)
                for c in range(BLK):
                    sp.dma_start(srows[c], score_t[:, c * P:(c + 1) * P].rearrange("p (g e) -> p g e", e=E))\
                        .then_inc(w_score, 16)

                def store_y(g):
                    sp.wait_ge(p_y, g + 1)
                    sp.dma_start(out[bass.ds(g * GROUP, GROUP), :].rearrange("(b p) d -> p b d", p=P),
                                 y[:, :, :]).then_inc(w_y, 16)

                with sp.Fori(0, G - 1) as g:
                    store_y(g)
                sp.wait_ge(m_ids, 1)
                sp.dma_start(raw[:, HALF_F:FE, :], w_expert[0, :, HALF_F:FE, :]).then_inc(l_w[1], 16)
                store_y(G - 1)
                sp.wait_ge(w_y, 16 * G + 1)
                sp.wait_ge(w_score, 16 * BLK)
                for i in range(2):
                    sp.wait_ge(w_rows[i], 16 * KC * G // 2)

            def plus_x1(engine, g):
                yv = y[:, :, :].rearrange("p b (k q) -> p k b q", k=KC)
                x1 = slots[:, :, bass.ds(g * GROUP, GROUP)].rearrange("p k (b q) -> p k b q", q=P)
                engine.tensor_tensor(yv, yv, x1, ALU.add).then_inc(p_y, 1)

            @block.gpsimd
            def _(pool):
                def iota_select(dst, src, op, fill, base):
                    nc.gpsimd.affine_select(out=dst[:, :], in_=src[:, :], compare_op=op, fill=fill, base=base,
                                            pattern=[[1, P]], channel_multiplier=-1).then_inc(p2, 1)

                nc.gpsimd.memset(gw_hi[:, :, :].bitcast(F32), 0.0).then_inc(p2, 1)
                nc.gpsimd.memset(gw_lo[:, :, :].bitcast(F32), 0.0).then_inc(p2, 1)
                nc.gpsimd.memset(same_e[:, :], 0.0).then_inc(p2, 1)
                for n in range(1 - G, G):
                    pool.wait_ge(p2, 3 + n + G - 1)
                    iota_select(same_e, same_e, ALU.not_equal, 1.0, -E * n)
                pool.wait_ge(p2, 3 + 2 * G - 1)
                iota_select(before, same_e, ALU.is_ge, 0.0, -1)
                nc.gpsimd.iota(iota_i[:, :], pattern=[[1, AW]], base=0, channel_multiplier=0).then_inc(p2, 1)
                nc.gpsimd.iota(tok_i[:, :], pattern=[[P, BLK], [GROUP, G]], base=-HALF_T,
                               channel_multiplier=1).then_inc(p2, 1)
                pool.wait_ge(p2, 3 + 2 * G + 2)
                nc.gpsimd.tensor_copy(iota_f[:, :], iota_i[:, :]).then_inc(p2, 1)
                nc.gpsimd.tensor_copy(tok_f[:, :], tok_i[:, :]).then_inc(p2, 1)
                for g in range(G - 2):
                    if g >= 2:
                        f = g - 2
                        pool.wait_ge(a_sh, 1)
                        nc.gpsimd.tensor_tensor(sh_lo[:, f, :], raw[:, f, :], sh_hi[:, f, :].bitcast(F32),
                                                ALU.subtract).then_inc(p_sh, 1)
                    sl = slice(g * GROUP, (g + 1) * GROUP)
                    pool.wait_ge(a_hf, g + 1)
                    pool.wait_ge(a_hh, g + 1)
                    nc.gpsimd.tensor_tensor(slots_lo[:, :, sl], h_f[g % 2][:, :, :],
                                            slots_hi[:, :, sl].bitcast(F32), ALU.subtract).then_inc(h_lo, 1)

                def hidden_lo(n, f):
                    pool.wait_ge(a_hid, n + 3)
                    nc.gpsimd.tensor_tensor(hid_lo[:, f % FS, :], hid[:, f % 2, :], hid_hi[:, f % FS, :].bitcast(F32),
                                            ALU.subtract).then_inc(p_lo, 1)

                def add_x1(g):
                    pool.wait_ge(a_y, g + 2)
                    plus_x1(nc.gpsimd, g)

                pool.sem_inc(p_lo, 2)
                for f in range(LAG):
                    hidden_lo(f, f)
                with pool.Fori(0, G - 1) as g:
                    for f in range(FS):
                        hidden_lo(g * FS + f + LAG, f + LAG)
                    add_x1(g)
                for f in range(FS - LAG):
                    hidden_lo((G - 1) * FS + f + LAG, f + LAG)
                pool.wait_ge(l_idx, 16)
                pool.wait_ge(w_score, 16 * BLK)
                for i in range(2):
                    pool.wait_ge(w_rows[i], 16 * KC * G // 2)
                nc.gpsimd.tensor_copy(idx_in[:, :], idx_all[:, 0, :]).then_inc(p_idx, 1)
                pool.wait_ge(p_idx, 1)
                for j in range(BLK):
                    pool.indirect_dma_start(got[:, j, :], None, rows,
                                            bass.IndirectOffsetOnAxis(idx_in[:, j:j + 1], 0)).then_inc(g_in_, 16)
                pool.wait_ge(g_in_, 16 * BLK)

            def turn_banks(g):
                return down if g % 2 == 0 else wide

            def count_mm():
                return nc.tensor.matmul(small[:, 0:1], same_e[:, :], cnt[:, :], start=True, stop=True)

            @block.tensor
            def _(pe):
                def turn_slots(g):
                    if g >= 2:
                        pe.wait_ge(v_x1, g - 1)
                    for b in range(BLK):
                        for k in range(KC):
                            c0 = g * GROUP + b * P
                            last = nc.tensor.transpose(turn_banks(g)[:, k, b * P:(b + 1) * P], slots[:, k, c0:c0 + P],
                                                       ident[:, :])
                    last.then_inc(t_tok, 1)

                def turn_h(g):
                    pe.wait_ge(a_norm, g + 1)
                    if g >= 1:
                        pe.wait_ge(a_hh, g)
                    if g == G - 1:
                        pe.wait_ge(h_lo, g)
                    for b in range(BLK):
                        for k in range(KC):
                            last = nc.tensor.transpose(wide[:, 2 + k, b * P:(b + 1) * P], hg[:, g % 2, k, b * P:(b + 1) * P],
                                                       ident[:, :])
                    last.then_inc(t_h, 1)

                def router(g):
                    pe.wait_ge(h_lo, g + 1)
                    sl = slice(g * GROUP, (g + 1) * GROUP)
                    c0 = P - E - g * E
                    n = 0
                    for k in range(KC):
                        for w, h in ((gw_hi, slots_hi), (gw_hi, slots_lo), (gw_lo, slots_hi)):
                            n += 1
                            last = nc.tensor.matmul(logit[:, :], w[:, k, c0:c0 + P], h[:, k, sl],
                                                    start=(g == 0 and n == 1), stop=(g == G - 1 and n == 3 * KC))
                    return last

                def into_hidden(n, g, f, between=None):
                    sl = bass.ds(g * GROUP, GROUP)
                    for bank, s_m, s_v, c in ((f % 2, m_g, a_silu, 0), (2 + f % 2, m_u, v_hid, 2)):
                        pe.wait_ge(s_v, n + 1)
                        m = 0
                        for k in range(KC):
                            if c == 2 and k == 1 and between is not None:
                                between()
                            cols = slice((c + k) * P, (c + k + 1) * P)
                            for w, h in ((sh_hi, slots_hi), (sh_hi, slots_lo), (sh_lo, slots_hi)):
                                m += 1
                                last = nc.tensor.matmul(wide[:, bank, :], w[:, f, cols], h[:, k, sl],
                                                        start=(m == 1), stop=(m == 3 * KC))
                        last.then_inc(s_m, 1)

                def out_of_hidden(n, g, f):
                    pe.wait_ge(p_lo, n + 3)
                    if f == 0:
                        pe.wait_ge(a_y, g + 1)
                    for b in range(BLK):
                        tok = slice(b * P, (b + 1) * P)
                        for m, (h, w) in enumerate(((hid_hi, sh_hi), (hid_lo, sh_hi), (hid_hi, sh_lo))):
                            last = nc.tensor.matmul(down[:, b // 2, (b % 2) * D:(b % 2 + 1) * D], h[:, f, tok],
                                                    w[:, f, 4 * P:6 * P], start=(f == 0 and m == 0 and b % 2 == 0),
                                                    stop=(f == FS - 1 and m == 2), skip_group_check=True)
                    last.then_inc(m_dn, 1)

                def body(g, f, between=None):
                    n = g * FS + f
                    into_hidden(n + LAG, g + (f + LAG) // FS, (f + LAG) % FS, between)
                    out_of_hidden(n, g, f)

                def count_product(u):
                    pe.wait_ge(v_cnt, u + 1)
                    count_mm().then_inc(m_cnt, 1)

                turn_slots(0)
                turn_slots(1)
                pe.wait_ge(v_gw, 2)
                for g in range(0, G, 2):
                    for i in range(2):
                        if g + 2 < G:
                            turn_slots(g + 2 + i)
                    for i in range(2):
                        if g >= 2:
                            router(g - 2 + i)
                    for i in range(2):
                        turn_h(g + i)
                router(G - 2)
                router(G - 1).then_inc(m_log, 1)
                pe.wait_ge(p_sh, FS)
                pe.wait_ge(p2, 3 + 2 * G)
                pe.sem_inc(m_dn, FS)
                pe.wait_ge(v_x1, G)
                pe.wait_ge(a_hh, G)
                into_hidden(0, 0, 0)
                pe.wait_ge(a_sg, 1)
                for c in range(BLK):
                    last = nc.tensor.transpose(logit[:, c * P:(c + 1) * P], sg[:, c * P:(c + 1) * P], ident[:, :])
                last.then_inc(t_score, 1)
                into_hidden(1, 0, 1)
                with pe.Fori(0, G_BIS) as g:
                    for f in range(FS):
                        u = (g * FS + f) * 2
                        body(g, f, lambda: count_product(u))
                        count_product(u + 1)
                body(G_BIS, 0)
                pe.wait_ge(v_tot, 1)
                nc.tensor.matmul(small[:, 1:2], same_e[:, :], tots[:, 0:1], start=True, stop=True)
                nc.tensor.matmul(small[:, 2:3], before[:, :], tots[:, 1:2], start=True, stop=True).then_inc(m_tot, 1)
                body(G_BIS, 1)
                pe.wait_ge(v_tot, 2)
                nc.tensor.matmul(small[:, 3:4], before[:, :], tots[:, 2:3], start=True, stop=True).then_inc(m_tot, 1)
                body(G_BIS, 2)
                pe.wait_ge(v_slot, 1)
                pe.wait_ge(a_score, 1)
                for c in range(BLK):
                    last = nc.tensor.transpose(logit[:, c * P:(c + 1) * P], slot[:, c * P:(c + 1) * P], ident[:, :])
                last.then_inc(t_slot, 1)
                body(G_BIS, 3)
                for g in range(G_BIS + 1, G - 1):
                    for f in range(FS):
                        body(g, f)
                body(G - 1, 0)
                pe.wait_ge(a_hot, W)
                for q in range(E // BLK):
                    for w in range(W):
                        last = nc.tensor.matmul(small[:, q * BLK * BW:(q + 1) * BLK * BW],
                                                hot_a[w // HOT][:, w % HOT, q * P:(q + 1) * P],
                                                hot_b[:, w, q * BLK * BW:(q + 1) * BLK * BW],
                                                start=(w == 0), stop=(w == W - 1))
                last.then_inc(m_ids, 1)
                body(G - 1, 1)
                for f in range(FS - LAG, FS):
                    out_of_hidden((G - 1) * FS + f, G - 1, f)

            @block.scalar
            def _(act):
                def normalise(g):
                    act.wait_ge(v_ln, g // 2 + 1)
                    if g >= 2:
                        act.wait_ge(w_rows[g % 2], 16 * KC * (g // 2))
                        act.wait_ge(t_h, g - 1)
                    for b in range(BLK):
                        c0 = g * GROUP + b * P
                        i, j = g // 2 % 2, g % 2 * BLK + b
                        last = nc.scalar.activation(hg[:, g % 2, :, b * P:(b + 1) * P], slots[:, :, c0:c0 + P], ACT.Identity,
                                                    bias=shift2[:, i, j:j + 1], scale=rstd2[:, i, j:j + 1])
                    last.then_inc(a_norm, 1)

                def copy_h(g):
                    act.wait_ge(t_h, g + 1)
                    sl = slice(g * GROUP, (g + 1) * GROUP)
                    if g < G - 2:
                        if g >= 2:
                            act.wait_ge(h_lo, g - 1)
                        nc.scalar.activation(h_f[g % 2][:, :, :], wide[:, 2:4, :], ACT.Copy).then_inc(a_hf, 1)
                    nc.scalar.activation(slots_hi[:, :, sl], wide[:, 2:4, :], ACT.Copy).then_inc(a_hh, 1)

                def hidden(n, f):
                    act.wait_ge(m_g, n + 1)
                    act.wait_ge(v_hid, n + 1)
                    nc.scalar.activation(silu[:, f % 2, :], wide[:, f % 2, :], ACT.Silu).then_inc(a_silu, 1)
                    act.wait_ge(v_hid, n + 3)
                    act.wait_ge(m_dn, n + 1)
                    nc.scalar.activation(hid_hi[:, f % FS, :], hid[:, f % 2, :], ACT.Copy).then_inc(a_hid, 1)

                def scale_sums(g):
                    act.wait_ge(m_dn, (g + 2) * FS)
                    act.wait_ge(w_y, 16 * g + 1)
                    nc.scalar.activation(y[:, :, :].rearrange("p b d -> p (b d)"),
                                         down[:, :, :].rearrange("p a c -> p (a c)"), ACT.Copy,
                                         scale=tanh_g[:, 1:2]).then_inc(a_y, 1)

                def token_numbers(i):
                    act.wait_ge(v_hot, 2 * (i + 1))
                    for w in range(i * HOT, (i + 1) * HOT):
                        nc.scalar.activation(hot_b[:, w, :], hot_b[:, w, :], ACT.Copy,
                                             scale=tok_f[:, w:w + 1]).then_inc(a_hot, 1)

                normalise(0)
                normalise(1)
                copy_h(0)
                act.wait_ge(l_sh, 16)
                nc.scalar.activation(sh_hi[:, :, :], raw[:, 0:FS, :], ACT.Copy).then_inc(a_sh, 1)
                copy_h(1)
                for g in range(2, G, 2):
                    normalise(g)
                    normalise(g + 1)
                    copy_h(g)
                    copy_h(g + 1)
                act.wait_ge(m_log, 1)
                nc.scalar.activation(sg[:, :], logit[:, :], ACT.Sigmoid).then_inc(a_sg, 1)
                nc.scalar.preload_act_table(ACT.Silu)
                act.sem_inc(a_silu, 2)
                act.sem_inc(a_hid, 2)
                act.sem_inc(a_y, 1)
                act.sem_inc(w_y, 1)
                hidden(0, 0)
                act.wait_ge(t_score, 1)
                nc.scalar.activation(score_t[:, :], logit[:, :], ACT.Copy).then_inc(a_score, 1)
                hidden(1, 1)
                with act.Fori(0, G_BIS + 1) as g:
                    for f in range(FS):
                        hidden(g * FS + f + LAG, f + LAG)
                    scale_sums(g)
                act.wait_ge(p2, 3 + 2 * G + 4)
                for g in range(G_BIS + 1, G - 1):
                    for f in range(FS):
                        hidden(g * FS + f + LAG, f + LAG)
                        token_numbers((g - G_BIS - 1) * FS + f)
                    scale_sums(g)
                hidden(G * FS - 2, FS - 2)
                act.wait_ge(v_ids, 1)
                idv = ids.rearrange("(q f) (a b) -> f a q b", f=BLK, b=BW)
                for f in range(BLK):
                    act.dma_start(idv[f], ids_sb[f * AW:(f + 1) * AW, :, :]).then_inc(w_ids, 16)
                hidden(G * FS - 1, FS - 1)
                act.wait_ge(w_ids, 16 * BLK)
                act.dma_start(idx_all[:, :, :], ids.rearrange("e (p j) -> p e j", j=BLK)).then_inc(l_idx, 16)
                scale_sums(G - 1)

            @block.vector
            def _(dve):
                st = Steps(dve, v2)

                def layer_norm(q):
                    for g in (2 * q, 2 * q + 1):
                        sl = slice(g * GROUP, (g + 1) * GROUP)
                        dve.wait_ge(t_tok, g + 1)
                        dve.wait_ge(l_xg[g % 2], 16 * KC * (g // 2 + 1))
                        nc.vector.scalar_tensor_tensor(slots[:, :, sl], turn_banks(g)[:, 0:2, :], tanh_g[:, 0:1],
                                                       xg[:, g % 2, :, :], ALU.mult, ALU.add).then_inc(v_x1, 1)
                    for j in range(2 * BLK):
                        if j % BLK == 0:
                            dve.wait_ge(v_x1, 2 * q + j // BLK + 1)
                        c0 = 2 * q * GROUP + j * P
                        st.add(nc.vector.bn_stats(stats2[:, j, :], slots[:, :, c0:c0 + P]))
                    st.wait()
                    for j in range(2 * BLK):
                        st.add(nc.vector.bn_aggr(mv2[:, j, :], stats2[:, j, :]))
                    st.wait()
                    if q >= 2:
                        dve.wait_ge(a_norm, 2 * q - 2)
                    st.do(nc.vector.tensor_scalar(var2[:, :], mv2[:, :, 1], LN_EPS, None, ALU.add))
                    rsqrt_steps(nc.vector, st.do, rstd2[:, q % 2, :], var2[:, :], rtmp2[:, :])
                    nc.vector.scalar_tensor_tensor(shift2[:, q % 2, :], mv2[:, :, 0], -1.0, rstd2[:, q % 2, :], ALU.mult,
                                                   ALU.mult).then_inc(v_ln, 1)
                    dve.wait_ge(v_ln, q + 1)

                layer_norm(0)
                dve.wait_ge(l_gw, 16)
                dve.wait_ge(p2, 2)
                nc.vector.tensor_copy(gw_hi[:, :, P - E:P], gw_f[:, :, :]).then_inc(v_gw, 1)
                dve.wait_ge(v_gw, 1)
                nc.vector.tensor_tensor(gw_lo[:, :, P - E:P], gw_f[:, :, :], gw_hi[:, :, P - E:P].bitcast(F32),
                                        ALU.subtract).then_inc(v_gw, 1)
                for q in range(1, G // 2):
                    layer_norm(q)
                dve.wait_ge(h_lo, G - 2)
                for g in (G - 2, G - 1):
                    sl = slice(g * GROUP, (g + 1) * GROUP)
                    dve.wait_ge(a_hh, g + 1)
                    nc.vector.tensor_tensor(slots_lo[:, :, sl], wide[:, 2:4, :], slots_hi[:, :, sl].bitcast(F32),
                                            ALU.subtract).then_inc(h_lo, 1)
                for i in range(2):
                    dve.wait_ge(w_rows[i], 16 * KC * G // 2)
                dve.wait_ge(t_h, G)
                st.add(nc.vector.memset(ones[:, :], 1.0))
                st.add(nc.vector.memset(thr[:, :], 0))
                st.do(nc.vector.memset(bit[:, :], 1 << 29))
                dve.sem_inc(v_hid, 2)
                dve.wait_ge(a_sg, 1)

                def bisect_count(u):
                    nc.vector.tensor_scalar(cand[:, :], bit[:, :], thr[:, 0:1], None, ALU.bitwise_or).then_inc(v_bis, 1)
                    dve.wait_ge(v_bis, 3 * u + 1)
                    nc.vector.tensor_scalar(slot[:, :], sg[:, :], cand[:, 0:1].bitcast(F32), 0.0, ALU.is_ge, ALU.add,
                                            accum_out=cnt[:, :]).then_inc(v_cnt, 1)

                def bisect_keep(u):
                    dve.wait_ge(m_cnt, u + 1)
                    nc.vector.tensor_scalar(keep[:, :], small[:, 0:1], float(CAP), -1.0, ALU.is_ge,
                                            ALU.mult).then_inc(v_bis, 1)
                    dve.wait_ge(v_bis, 3 * u + 2)
                    nc.vector.scalar_tensor_tensor(thr[:, :], keep[:, :], bit[:, 0:1], thr[:, :], ALU.bitwise_and,
                                                   ALU.bitwise_or).then_inc(v_bis, 1)
                    dve.wait_ge(v_bis, 3 * u + 3)
                    nc.vector.tensor_scalar(bit[:, :], bit[:, :], 1, None, ALU.logical_shift_right).then_inc(v_bit, 1)
                    dve.wait_ge(v_bit, u + 1)

                def hidden(n, f):
                    dve.wait_ge(m_u, n + 1)
                    dve.wait_ge(a_silu, n + 3)
                    dve.wait_ge(a_hid, n + 1)
                    dve.wait_ge(p_lo, n + 1)
                    nc.vector.tensor_tensor(hid[:, f % 2, :], silu[:, f % 2, :], wide[:, 2 + f % 2, :],
                                            ALU.mult).then_inc(v_hid, 1)

                hidden(0, 0)
                hidden(1, 1)
                with dve.Fori(0, G_BIS) as g:
                    for f in range(FS):
                        u = (g * FS + f) * 2
                        bisect_count(u)
                        bisect_keep(u)
                        bisect_count(u + 1)
                        hidden(g * FS + f + LAG, f + LAG)
                        bisect_keep(u + 1)

                thr_f = thr[:, 0:1].bitcast(F32)
                n = G_BIS * FS + LAG
                st.add(nc.vector.tensor_scalar(above[:, :], sg[:, :], thr_f, 0.0, ALU.is_gt, ALU.add,
                                               accum_out=tots[:, 0:1]))
                st.do(nc.vector.tensor_scalar(tie[:, :], sg[:, :], thr_f, None, ALU.is_equal))
                st.do(nc.vector.tensor_tensor_scan(count[:, :], ones[:, :], tie[:, :], 0.0, ALU.mult, ALU.add))
                st.do(nc.vector.tensor_copy(tots[:, 1:2], count[:, GROUP - 1:GROUP]))
                dve.sem_inc(v_tot, 1)
                hidden(n, 0)
                dve.wait_ge(m_tot, 1)
                st.add(nc.vector.tensor_scalar(offs[:, 0:1], small[:, 1:2], -1.0, float(CAP), ALU.mult, ALU.add))
                st.do(nc.vector.tensor_copy(offs[:, 1:2], small[:, 2:3]))
                st.do(nc.vector.tensor_scalar(taken[:, :], count[:, :], offs[:, 1:2], offs[:, 0:1], ALU.add, ALU.is_le))
                st.do(nc.vector.tensor_tensor(taken[:, :], taken[:, :], tie[:, :], ALU.mult))
                st.do(nc.vector.tensor_tensor(taken[:, :], taken[:, :], above[:, :], ALU.add))
                st.do(nc.vector.tensor_tensor_scan(count[:, :], ones[:, :], taken[:, :], 0.0, ALU.mult, ALU.add))
                st.do(nc.vector.tensor_copy(tots[:, 2:3], count[:, GROUP - 1:GROUP]))
                dve.sem_inc(v_tot, 1)
                hidden(n + 1, 1)
                dve.wait_ge(m_tot, 2)
                st.do(nc.vector.tensor_scalar(offs[:, 2:3], small[:, 3:4], -1.0 - BIG, None, ALU.add))
                st.do(nc.vector.scalar_tensor_tensor(slot[:, :], count[:, :], offs[:, 2:3], taken[:, :], ALU.add,
                                                     ALU.mult))
                nc.vector.tensor_scalar(slot[:, :], slot[:, :], BIG, None, ALU.add).then_inc(v_slot, 1)
                hidden(n + 2, 2)
                dve.wait_ge(t_slot, 1)
                st.do(nc.vector.tensor_copy(slot_i[:, :], logit[:, :]))
                st.add(nc.vector.tensor_scalar(hi_i[:, :], slot_i[:, :], 4, None, ALU.logical_shift_right))
                st.do(nc.vector.tensor_scalar(lo_i[:, :], slot_i[:, :], BW - 1, None, ALU.bitwise_and))
                st.add(nc.vector.tensor_copy(hi_f[:, :], hi_i[:, :]))
                st.do(nc.vector.tensor_copy(lo_f[:, :], lo_i[:, :]))
                hidden(n + 3, 3)
                dve.wait_ge(p2, 3 + 2 * G + 4)
                dve.wait_ge(p_y, G_BIS)
                for i in range(W // HOT):
                    ws = slice(i * HOT * E, (i + 1) * HOT * E)
                    for hot, dig, width in ((hot_b[:, i * HOT:(i + 1) * HOT, :], lo_f, BW),
                                            (hot_a[i][:, :, :], hi_f, AW)):
                        nc.vector.tensor_tensor(
                            hot.rearrange("p w (e a) -> p (w e) a", e=E),
                            dig[:, ws].rearrange("p (t a) -> p t a", a=1).to_broadcast([P, HOT * E, width]),
                            iota_f[:, 0:width].rearrange("p (a w) -> p a w", a=1).to_broadcast([P, HOT * E, width]),
                            ALU.is_equal).then_inc(v_hot, 1)
                    hidden(n + 4 + i, i % FS)
                hidden(G * FS - 2, FS - 2)
                dve.wait_ge(m_ids, 1)
                for f in range(BLK):
                    pr = slice(f * AW, (f + 1) * AW)
                    last = nc.vector.tensor_scalar(
                        ids_sb[pr, :, :], small[pr, 0:E * BW].rearrange("p (q f b) -> p q f b", f=BLK, b=BW)[:, :, f, :],
                        float(HALF_T), None, ALU.add)
                last.then_inc(v_ids, 1)
                hidden(G * FS - 1, FS - 1)
                dve.wait_ge(a_y, G + 1)
                plus_x1(nc.vector, G - 1)
        state.close()
        RING = 4
        AHEAD = 5
        with ExitStack() as experts:
            lsb, lps = tensors(experts)
            w_hi = lsb("w_hi", [P, FE, WCOL], F32R)
            w_lo = lsb("w_lo", [P, FE, WCOL], F32R)
            b_gate = lsb("b_gate", [P, E, FE])
            b_up = lsb("b_up", [P, E, FE])
            b_down = lsb("b_down", [P, E, D])
            idx_out = lsb("idx_out", [P, BLK], U32)
            xt_hi = lsb("xt_hi", [P, KC, GROUP], F32R)
            xt_lo = lsb("xt_lo", [P, KC, GROUP], F32R)
            esilu = lsb("esilu", [P, 2, GROUP])
            ehid = lsb("ehid", [P, 2, GROUP])
            eh_hi = lsb("eh_hi", [P, RING, GROUP], F32R)
            eh_lo = lsb("eh_lo", [P, RING, GROUP], F32R)
            weight = lsb("weight", [P, BLK, 1])
            yo = lsb("yo", [P, BLK, D])
            egate = lps("egate", [P, 2, 512])
            eup = lps("eup", [P, 2, 512])
            edown = lps("edown", [P, 2, 512])
            exps = lps("exps", [P, KC, 512])

            l_b = sem("l_b")
            p_out, p_step, p_sums = sem("p_out"), sem("p_step"), sem("p_sums")
            g_add = sem("scattered")
            t_xt, a_xt, v_xt, v_wt = sem("t_xt"), sem("a_xt"), sem("v_xt"), sem("v_wt")
            a_w, v_w = sem("a_w"), sem("v_w")
            k_g, k_u, k_silu, k_hid, k_hi, k_lo, k_dn = (sem(f"k_{n}") for n in ("g", "u", "silu", "hid", "hi", "lo", "dn"))
            k_out, k_yo = sem("k_out"), sem("k_yo")
            block = experts.enter_context(nc.Block())

            def half_slice(h):
                return slice(h * HALF_F, (h + 1) * HALF_F)

            @block.sync
            def _(sp):
                sp.dma_start(b_gate[:, :, :], gate_b).then_inc(l_b, 16)
                sp.dma_start(b_up[:, :, :], up_b).then_inc(l_b, 16)
                sp.dma_start(b_down[:, :, :], down_b.rearrange("(a e) d -> a e d", a=1).to_broadcast([P, E, D]))\
                    .then_inc(l_b, 16)
                with sp.Fori(0, E - 1) as e:
                    for h in range(2):
                        sp.wait_ge(a_w, e * FE + (h + 1) * HALF_F)
                        sp.wait_ge(v_w, e * FE + (h + 1) * HALF_F)
                        sp.dma_start(raw[:, half_slice(h), :],
                                     w_expert[bass.ds(e + 1, 1), :, half_slice(h), :].rearrange("a p f n -> p (a f) n"))\
                            .then_inc(l_w[h], 16)

            @block.gpsimd
            def _(pool):
                def gather(e):
                    nc.gpsimd.tensor_copy(idx_in[:, :], idx_all[:, bass.ds(e, 1), :].rearrange("p a j -> p (a j)"))\
                        .then_inc(p_idx, 1)
                    pool.wait_ge(p_idx, e + 1)
                    pool.sem_inc(p_step, 1)
                    for j in range(BLK):
                        pool.indirect_dma_start(got[:, j, :], None, rows,
                                                bass.IndirectOffsetOnAxis(idx_in[:, j:j + 1], 0)).then_inc(g_in_, 16)

                def turn_of(e, more):
                    pool.wait_ge(g_in_, 16 * BLK * (e + 1))
                    pool.sem_inc(p_step, 1)
                    nc.gpsimd.tensor_copy(idx_out[:, :], idx_in[:, :]).then_inc(p_out, 1)
                    if more:
                        pool.wait_ge(p_out, e + 1)
                        pool.wait_ge(t_xt, e + 1)
                        pool.wait_ge(v_wt, e + 1)
                        pool.sem_inc(p_step, 1)
                        gather(e + 1)
                    pool.wait_ge(k_yo, e + 1)
                    pool.wait_ge(p_out, e + 1)
                    pool.sem_inc(p_step, 1)
                    for j in range(BLK):
                        pool.indirect_dma_start(out, bass.IndirectOffsetOnAxis(idx_out[:, j:j + 1], 0), yo[:, j, :],
                                                None, compute_op=ALU.add).then_inc(g_add, 16)
                    pool.wait_ge(g_add, 16 * BLK * (e + 1))
                    pool.sem_inc(p_sums, 1)

                pool.sem_inc(p_sums, 1)
                with pool.Fori(0, E - 1) as e:
                    turn_of(e, True)
                turn_of(E - 1, False)

            @block.tensor
            def _(pe):
                def turn_rows(e):
                    pe.wait_ge(g_in_, 16 * BLK * (e + 1))
                    for k in range(KC):
                        for j in range(BLK):
                            last = nc.tensor.transpose(exps[:, k, j * P:(j + 1) * P], got[:, j, k * P:(k + 1) * P],
                                                       ident[:, :])
                    last.then_inc(t_xt, 1)

                def into_hidden(e, f):
                    n = e * FE + f
                    pe.wait_ge(a_w, n + 1)
                    pe.wait_ge(v_w, n + 1)
                    for bank, free, done, c in ((egate, k_silu, k_g, 0), (eup, k_hid, k_u, 2)):
                        pe.wait_ge(free, n + 1)
                        m = 0
                        for k in range(KC):
                            for w, x_ in ((w_hi, xt_hi), (w_hi, xt_lo), (w_lo, xt_hi)):
                                m += 1
                                last = nc.tensor.matmul(bank[:, f % 2, :], w[:, f, (c + k) * P:(c + k + 1) * P], x_[:, k, :],
                                                        start=(m == 1), stop=(m == 3 * KC))
                        last.then_inc(done, 1)

                def out_of_hidden(e, f):
                    n = e * FE + f
                    pe.wait_ge(k_lo, n + 1)
                    if f == 0:
                        pe.wait_ge(k_out, BLK * e + 1)
                    for j in range(BLK):
                        tok = slice(j * P, (j + 1) * P)
                        for m, (h, w) in enumerate(((eh_hi, w_hi), (eh_lo, w_hi), (eh_hi, w_lo))):
                            last = nc.tensor.matmul(edown[:, j // 2, (j % 2) * D:(j % 2 + 1) * D], h[:, f % RING, tok],
                                                    w[:, f, 4 * P:6 * P], start=(f == 0 and m == 0 and j % 2 == 0),
                                                    stop=(f == FE - 1 and m == 2), skip_group_check=True)
                    last.then_inc(k_dn, 1)

                def expert(e, more):
                    pe.wait_ge(a_xt, e + 1)
                    pe.wait_ge(v_xt, e + 1)
                    for f in range(FE):
                        into_hidden(e, f)
                        if f >= LAG:
                            out_of_hidden(e, f - LAG)
                    if more:
                        turn_rows(e + 1)
                    for f in range(FE - LAG, FE):
                        out_of_hidden(e, f)

                pe.sem_inc(k_dn, FE)
                turn_rows(0)
                with pe.Fori(0, E - 1) as e:
                    expert(e, True)
                expert(E - 1, False)

            @block.scalar
            def _(act):
                def split(e, f):
                    if f % HALF_F == 0:
                        act.wait_ge(l_w[f // HALF_F], 16 * (e + 1))
                    act.wait_ge(k_dn, e * FE + f + 1)
                    nc.scalar.activation(w_hi[:, f, :], raw[:, f, :], ACT.Copy).then_inc(a_w, 1)

                def rows_hi(e):
                    act.wait_ge(t_xt, e + 1)
                    nc.scalar.activation(xt_hi[:, :, :], exps[:, :, :], ACT.Copy).then_inc(a_xt, 1)

                def expert(e, more):
                    for f in range(FE):
                        n = e * FE + f
                        act.wait_ge(k_g, n + 1)
                        act.wait_ge(k_hid, n + 1)
                        nc.scalar.activation(esilu[:, f % 2, :], egate[:, f % 2, :], ACT.Silu,
                                             bias=b_gate[:, bass.ds(e, 1), f:f + 1].rearrange("p a b -> p (a b)"))\
                            .then_inc(k_silu, 1)
                        if f < FE - AHEAD:
                            split(e, f + AHEAD)
                        elif more:
                            split(e + 1, f - (FE - AHEAD))
                        act.wait_ge(k_hid, n + 3)
                        act.wait_ge(k_dn, n + 1 + FE - RING)
                        nc.scalar.activation(eh_hi[:, f % RING, :], ehid[:, f % 2, :], ACT.Copy).then_inc(k_hi, 1)
                    if more:
                        rows_hi(e + 1)

                act.sem_inc(k_silu, 2)
                act.sem_inc(k_hi, 2)
                split(0, 0)
                rows_hi(0)
                for f in range(1, AHEAD):
                    split(0, f)
                nc.scalar.preload_act_table(ACT.Silu)
                act.wait_ge(l_b, 48)
                with act.Fori(0, E - 1) as e:
                    expert(e, True)
                expert(E - 1, False)

            @block.vector
            def _(dve):
                def split(e, f):
                    dve.wait_ge(a_w, e * FE + f + 1)
                    nc.vector.tensor_tensor(w_lo[:, f, :], raw[:, f, :], w_hi[:, f, :].bitcast(F32),
                                            ALU.subtract).then_inc(v_w, 1)

                def rows_lo(e):
                    dve.wait_ge(a_xt, e + 1)
                    nc.vector.tensor_tensor(xt_lo[:, :, :], exps[:, :, :], xt_hi[:, :, :].bitcast(F32),
                                            ALU.subtract).then_inc(v_xt, 1)

                def take_scores(e, first=False):
                    if not first:
                        dve.wait_ge(k_yo, e)
                    nc.vector.tensor_scalar(weight[:, :, :], got[:, :, bass.ds(D + e, 1)], tanh_g[:, 1:2], None,
                                            ALU.mult).then_inc(v_wt, 1)

                def results(e):
                    dve.wait_ge(k_dn, (e + 2) * FE)
                    dve.wait_ge(p_sums, e + 1)
                    for j in range(BLK):
                        nc.vector.tensor_tensor(yo[:, j, :], edown[:, j // 2, (j % 2) * D:(j % 2 + 1) * D],
                                                b_down[:, bass.ds(e, 1), :].rearrange("p a d -> p (a d)"),
                                                ALU.add).then_inc(k_out, 1)
                    dve.wait_ge(k_out, BLK * (e + 1) + 1)
                    dve.wait_ge(v_wt, e + 1)
                    for j in range(BLK):
                        last = nc.vector.tensor_scalar(yo[:, j, :], yo[:, j, :], weight[:, j, :], None, ALU.mult)
                    last.then_inc(k_yo, 1)

                def expert(e, more):
                    for f in range(FE):
                        n = e * FE + f
                        dve.wait_ge(k_u, n + 1)
                        dve.wait_ge(k_silu, n + 3)
                        dve.wait_ge(k_hi, n + 1)
                        nc.vector.scalar_tensor_tensor(
                            ehid[:, f % 2, :], eup[:, f % 2, :], b_up[:, bass.ds(e, 1), f:f + 1].rearrange("p a b -> p (a b)"),
                            esilu[:, f % 2, :], ALU.add, ALU.mult).then_inc(k_hid, 1)
                        if f < FE - AHEAD:
                            split(e, f + AHEAD)
                        elif more:
                            split(e + 1, f - (FE - AHEAD))
                        dve.wait_ge(k_hi, n + 3)
                        nc.vector.tensor_tensor(eh_lo[:, f % RING, :], ehid[:, f % 2, :],
                                                eh_hi[:, f % RING, :].bitcast(F32), ALU.subtract).then_inc(k_lo, 1)
                    if more:
                        rows_lo(e + 1)
                    results(e)
                    if more:
                        take_scores(e + 1)

                dve.sem_inc(k_out, 1)
                dve.sem_inc(k_hid, 2)
                split(0, 0)
                rows_lo(0)
                for f in range(1, AHEAD):
                    split(0, f)
                take_scores(0, first=True)
                dve.wait_ge(l_b, 48)
                with dve.Fori(0, E - 1) as e:
                    expert(e, True)
                expert(E - 1, False)


V_PN = 1 + 11 + 2


def _columns(v):
    import numpy as _np
    return _np.ascontiguousarray(_np.swapaxes(v.reshape(v.shape[:-1] + (-1, P)), -1, -2))


def _ffn_layout(gate, up, down):
    import numpy as _np
    f, d = gate.shape
    blocks, chunks = f // P, d // P
    into = [w.T.reshape(chunks, P, blocks, P)[k] for w in (gate, up) for k in range(chunks)]
    return _np.concatenate(into + [down.T.reshape(blocks, P, d).transpose(1, 0, 2)], axis=-1)


def kernel(x, ctx_1024, g_xattn, g_ffn, L0_xattn_Wq, L0_xattn_Wk, L0_xattn_Wv, L0_xattn_gru_wih, L0_xattn_gru_whh,
           L0_xattn_gru_bih, L0_xattn_gru_bhh, L0_xattn_slot_norm_w, L0_xattn_input_norm_w, L0_ffn_gate_w, L0_ffn_up_w,
           L0_ffn_up_b, L0_ffn_gw, L0_ffn_gb, L0_ffn_down_w, L0_ffn_down_b, L0_ffn_sh_gate_w, L0_ffn_sh_up_w,
           L0_ffn_sh_down_w):
    import numpy as _np
    import concourse.bacc as _bacc
    from concourse.bass_utils import run_bass_kernel_spmd as _run

    x = _np.asarray(x)
    ctx_1024 = _np.asarray(ctx_1024)
    d = x.shape[-1]
    host = {
        "x": x.reshape(-1, d),
        "ctx_tok": ctx_1024.reshape(-1, d),
        "tanh_in": _np.concatenate([_np.asarray(g_xattn), _np.asarray(g_ffn)]),
        "wq": L0_xattn_Wq,
        "wk_t": _np.asarray(L0_xattn_Wk).T,
        "wv_t": _np.asarray(L0_xattn_Wv).T,
        "wih_t": _np.asarray(L0_xattn_gru_wih).T,
        "whh_t": _np.asarray(L0_xattn_gru_whh).T,
        "vectors": _np.concatenate([_columns(_np.asarray(v)) for v in (
            L0_xattn_gru_bih, L0_xattn_gru_bhh, L0_xattn_slot_norm_w, L0_xattn_input_norm_w)], axis=1),
        "gate_t": _np.asarray(L0_ffn_gate_w).T,
        "w_expert": _np.stack([_ffn_layout(*w) for w in zip(_np.asarray(L0_ffn_gw), _np.asarray(L0_ffn_up_w),
                                                            _np.asarray(L0_ffn_down_w))]),
        "gate_b": _columns(_np.asarray(L0_ffn_gb)).transpose(1, 0, 2),
        "up_b": _columns(_np.asarray(L0_ffn_up_b)).transpose(1, 0, 2),
        "down_b": L0_ffn_down_b,
        "w_shared": _ffn_layout(_np.asarray(L0_ffn_sh_gate_w), _np.asarray(L0_ffn_sh_up_w),
                                _np.asarray(L0_ffn_sh_down_w)),
    }
    nc = _bacc.Bacc("TRN2", target_bir_lowering=False, num_devices=1)
    arrays, args = {}, {}
    for name, a in host.items():
        a = _np.ascontiguousarray(a)
        arrays[f"in_{name}"] = a
        args[name] = nc.dram_tensor(f"in_{name}", a.shape, mybir.dt.from_np(a.dtype), kind="ExternalInput").ap()
    out = nc.dram_tensor("out_tokens", host["x"].shape, F32, kind="ExternalOutput").ap()
    flamingo_kernel(nc, **args, out=out)
    r = _run(nc, [arrays], core_ids=[0])
    return r.results[0]["out_tokens"].reshape(x.shape)
```

```python
import concourse.bass as bass
from concourse import mybir
from contextlib import ExitStack

F32 = mybir.dt.float32
F32R = mybir.dt.float32r
F16 = mybir.dt.float16
I32 = mybir.dt.int32
U32 = mybir.dt.uint32
ALU = mybir.AluOpType
ACT = mybir.ActivationFunctionType
AX = mybir.AxisListType.X

P = 128
GROUP = 512
BLK = GROUP // P
RSQRT_MAGIC = 0x5F3759DF


class Steps:

    def __init__(self, eng, sem, done=0):
        self.eng, self.sem, self.n = eng, sem, done

    def add(self, ins):
        ins.then_inc(self.sem, 1)
        self.n += 1

    def wait(self):
        self.eng.wait_ge(self.sem, self.n)

    def do(self, ins):
        self.add(ins)
        self.wait()


def rsqrt_steps(dve, do, y, v, t):
    do(dve.tensor_scalar(t.bitcast(I32), v.bitcast(I32), 1, None, ALU.logical_shift_right))
    do(dve.tensor_scalar(y.bitcast(I32), t.bitcast(I32), -1.0, float(RSQRT_MAGIC), ALU.mult, ALU.add))
    for _ in range(3):
        do(dve.scalar_tensor_tensor(t, y, -0.5, y, ALU.mult, ALU.mult))
        do(dve.tensor_tensor(t, t, v, ALU.mult))
        do(dve.scalar_tensor_tensor(y, t, 1.5, y, ALU.add, ALU.mult))


def flamingo_kernel(nc, x, ctx_tok, tanh_in, wq, wk_t, wv_t, wih_t, whh_t, vectors, gate_t,
                    w_expert, gate_b, up_b, down_b, w_shared, out):
    T, D = x.shape
    M = ctx_tok.shape[0]
    B = 4
    MB = M // B
    KC = D // P
    G = T // GROUP
    PAIRS = B // 2
    GPP = G // PAIRS
    ITERS = 3
    SCALE = float(D) ** -0.5
    RMS_EPS, LN_EPS, ATTN_EPS = 1e-6, 1e-5, 1e-6
    assert KC == 2 and MB == 64 and T // B == 2 * GROUP and GPP == 4

    with ExitStack() as whole:
        def tensors(stack):
            def sb(name, shape, dt=F32):
                return stack.enter_context(nc.sbuf_tensor(name, shape, dt))

            def ps(name, shape, dt=F32):
                return stack.enter_context(nc.psum_tensor(name, shape, dt))
            return sb, ps

        def sem(name):
            return whole.enter_context(nc.semaphore(name))

        sb, ps = tensors(whole)
        ident = sb("ident", [P, P])
        tanh_g = sb("tanh_g", [P, 2])

        state = ExitStack()
        ssb, _ = tensors(state)
        slots = ssb("slots", [P, KC, T])
        slots_hi = ssb("slots_hi", [P, KC, T], F32R)
        slots_lo = ssb("slots_lo", [P, KC, T], F32R)
        attention = ExitStack()
        asb, aps = tensors(attention)
        whh_hi = asb("whh_hi", [P, KC, 3 * D], F32R)
        whh_lo = asb("whh_lo", [P, KC, 3 * D], F32R)
        vw_hi = asb("vw_hi", [P, PAIRS, 2, 3 * D], F32R)
        vw_lo = asb("vw_lo", [P, PAIRS, 3 * D], F32R)
        kq_hi = asb("kq_hi", [P, KC, B, P], F32R)
        kq_lo = asb("kq_lo", [P, KC, B, P], F32R)
        square = asb("square", [P, 2, KC, GROUP])
        own_block = asb("own_block", [GPP * BLK, BLK, P])
        pick_group = asb("pick_group", [GPP * BLK, 2, P])
        half_mask = asb("half_mask", [P, P])
        ones_col = asb("ones_col", [P, 1])
        attn_eps = asb("attn_eps", [P, 1])
        half_b_rz = asb("half_b_rz", [P, 4])
        b_xn = asb("b_xn", [P, 2])
        half_b_hn = asb("half_b_hn", [P, 2])
        ssq = aps("ssq", [P, 512])

        s_hi = sem("s_hi")
        s_lo = sem("s_lo")
        s_sqk = sem("s_sqk")
        s_sq = sem("s_sq")
        s_ss = sem("s_ss")

        def rows_of(b):
            return slice(b * MB, (b + 1) * MB)

        def sum_squares(pe, run, pair, g4, wait_read=None):
            pe.wait_ge(s_sq, run + 1)
            if wait_read is not None:
                pe.wait_ge(*wait_read)
            for blk in range(BLK):
                col = (pair * GPP + g4) * BLK + blk
                last = nc.tensor.matmul(ssq[:, col:col + 1], square[:, g4 % 2, 0, blk * P:(blk + 1) * P],
                                        ones_col[:, :], start=True, stop=True)
            last.then_inc(s_ss, 1)

        def add_squares(pool, g):
            sq = square[:, g % 2, :, :]
            nc.gpsimd.tensor_tensor(sq[:, 0, :], sq[:, 0, :], sq[:, 1, :], ALU.add).then_inc(s_sq, 1)

        def ln_chain(dve, st, stats, mv, var, rstd, tmp):
            for t in range(mv.shape[1]):
                st.add(nc.vector.bn_aggr(mv[:, t, :], stats[:, t, :]))
            st.wait()
            st.do(nc.vector.tensor_scalar(var, mv[:, :, 1], LN_EPS, None, ALU.add))
            rsqrt_steps(nc.vector, st.do, rstd, var, tmp)

        G1 = GPP
        NT = G1 * BLK
        xv = x.rearrange("(g b p) d -> g p b d", b=BLK, p=P)
        t_x = sem("t_x")
        s_s0 = sem("s_s0")

        def turn_group(tile, banks):
            for blk in range(BLK):
                for k in range(KC):
                    last = nc.tensor.transpose(banks[:, k, blk * P:(blk + 1) * P], tile[:, blk, k * P:(k + 1) * P],
                                               ident[:, :])
            last.then_inc(t_x, 1)

        def first_low(dve, g):
            sl = slice(g * GROUP, (g + 1) * GROUP)
            dve.wait_ge(s_hi, g + 1)
            nc.vector.tensor_tensor(slots_lo[:, :, sl], slots[:, :, sl], slots_hi[:, :, sl].bitcast(F32),
                                    ALU.subtract).then_inc(s_lo, 1)

        with ExitStack() as setup:
            lsb, lps = tensors(setup)
            xs = lsb("xs", [P, NT, D])
            ctx_sb = lsb("ctx_sb", [P, M // P, D])
            ctx_sq = lsb("ctx_sq", [P, M // P, D])
            wq_sb = lsb("wq_sb", [P, KC, D])
            wk_sb = lsb("wk_sb", [P, KC, D])
            wv_sb = lsb("wv_sb", [P, KC, D])
            wih_sb = lsb("wih_sb", [P, KC, 3 * D])
            whh_sb = lsb("whh_sb", [P, KC, 3 * D])
            vecs = lsb("vecs", [P, 16])
            scaled_w = lsb("scaled_w", [P, 2])
            g_in = lsb("g_in", [P, 2])
            pn_t = lsb("pn_t", [P, KC, M])
            kp_t = lsb("kp_t", [P, KC, M])
            vp_t = lsb("vp_t", [P, KC, M])
            kq_f = lsb("kq_f", [P, KC, M])
            vw_f = lsb("vw_f", [P, PAIRS, 3 * D])
            stats = lsb("stats", [P, NT, 6])
            mv = lsb("mv", [P, NT, 2])
            var = lsb("var", [P, NT + 2])
            rstd = lsb("rstd", [P, NT + 2])
            rtmp = lsb("rtmp", [P, NT + 2])
            csum = lsb("csum", [P, 2])
            bank = lps("bank", [P, 3, 512])
            turn = lps("turn", [P, 2, KC, GROUP])
            W = 3 * D // 2
            vw_bank = (1, 2, 0, 1)

            l_ctx, l_wk, l_wv, l_wq, l_wih, l_whh, l_vec, l_g = (
                sem(f"loaded_{n}") for n in ("ctx", "wk", "wv", "wq", "wih", "whh", "vec", "g"))
            l_x = [sem(f"loaded_x{g}") for g in range(G1)]
            c_pool = sem("const_pool")
            c_act = sem("ctx_squares")
            v0 = sem("vector_setup")
            v_vec = sem("v_vec")
            t_pn = sem("t_pn")
            w_pn = sem("w_pn")
            m_w = sem("m_w")
            e_w = sem("e_w")
            a_whi = sem("a_whi")
            p_wlo = sem("p_wlo")
            v_wlo = sem("v_wlo")
            d_vw = sem("d_vw")
            n_x = sem("n_x")

            block = setup.enter_context(nc.Block())

            @block.sync
            def _(sp):
                sp.dma_start(ctx_sb[:, :, :], ctx_tok.rearrange("(t p) d -> p t d", p=P)).then_inc(l_ctx, 16)
                sp.dma_start(wk_sb[:, :, :], wk_t.rearrange("(k p) n -> p k n", p=P)).then_inc(l_wk, 16)
                sp.dma_start(xs[:, 0:BLK, :], xv[0]).then_inc(l_x[0], 16)
                sp.dma_start(wv_sb[:, :, :], wv_t.rearrange("(k p) n -> p k n", p=P)).then_inc(l_wv, 16)
                sp.dma_start(wq_sb[:, :, :], wq.rearrange("(k p) n -> p k n", p=P)).then_inc(l_wq, 16)
                sp.dma_start(xs[:, 2 * BLK:3 * BLK, :], xv[2]).then_inc(l_x[2], 16)
                sp.dma_start(wih_sb[:, :, :], wih_t.rearrange("(k p) n -> p k n", p=P)).then_inc(l_wih, 16)
                sp.dma_start(g_in[:, :], tanh_in.rearrange("(a n) -> a n", a=1).to_broadcast([P, 2])).then_inc(l_g, 16)
                sp.wait_ge(a_whi, 1 + B + 2)
                for b in range(2):
                    sp.dma_start(vw_hi[rows_of(1 - b), :, b, :].bitcast(F32), vw_hi[rows_of(b), :, b, :].bitcast(F32)).then_inc(d_vw, 16)
                sp.wait_ge(d_vw, 32)

            @block.scalar
            def _(act):
                act.dma_start(vecs[:, :], vectors).then_inc(l_vec, 16)
                for g in range(1, G1, 2):
                    act.dma_start(xs[:, g * BLK:(g + 1) * BLK, :], xv[g]).then_inc(l_x[g], 16)
                act.dma_start(whh_sb[:, :, :], whh_t.rearrange("(k p) n -> p k n", p=P)).then_inc(l_whh, 16)
                act.wait_ge(l_ctx, 16)
                for t in range(M // P):
                    nc.scalar.activation(ctx_sq[:, t, :], ctx_sb[:, t, :], ACT.Square,
                                         accum_out=csum[:, t:t + 1]).then_inc(c_act, 1)
                act.wait_ge(l_whh, 16)
                nc.scalar.activation(whh_hi[:, :, :], whh_sb[:, :, :], ACT.Copy).then_inc(a_whi, 1)
                for i, dst in enumerate((kp_t, vp_t)):
                    act.wait_ge(m_w, i + 1)
                    nc.scalar.activation(dst[:, :, :], bank[:, 1 + i, :], ACT.Copy).then_inc(e_w, 1)
                act.wait_ge(l_g, 16)
                nc.scalar.activation(tanh_g[:, :], g_in[:, :], ACT.Tanh).then_inc(c_act, 1)
                act.wait_ge(m_w, 3)
                act.wait_ge(v_vec, 1)
                for k in range(KC):
                    last = nc.scalar.activation(kq_f[:, k, :], bank[:, 0, k * M:(k + 1) * M], ACT.Copy,
                                                scale=scaled_w[:, k:k + 1])
                last.then_inc(e_w, 1)
                act.wait_ge(e_w, 3)
                act.wait_ge(c_pool, 11)
                for b in range(B):
                    lo = (b % 2) * MB
                    nc.scalar.activation(kq_hi[:, :, b, lo:lo + MB], kq_f[:, :, b * MB:(b + 1) * MB],
                                         ACT.Copy).then_inc(a_whi, 1)
                for n in range(2 * PAIRS):
                    act.wait_ge(m_w, 4 + n)
                    nc.scalar.activation(vw_f[:, n // 2, (n % 2) * W:(n % 2 + 1) * W], bank[:, vw_bank[n], 0:W],
                                         ACT.Copy).then_inc(e_w, 1)
                act.wait_ge(e_w, 3 + 2 * PAIRS)
                for b in range(2):
                    nc.scalar.activation(vw_hi[rows_of(b), :, b, :], vw_f[rows_of(b), :, :], ACT.Copy).then_inc(a_whi, 1)
                for g in range(G1):
                    act.wait_ge(s_s0, g + 1)
                    sl = slice(g * GROUP, (g + 1) * GROUP)
                    nc.scalar.activation(slots_hi[:, :, sl], slots[:, :, sl], ACT.Copy).then_inc(s_hi, 1)
                    if g >= 2:
                        act.wait_ge(s_ss, g - 1)
                    nc.scalar.activation(square[:, g % 2, :, :], slots[:, :, sl], ACT.Square).then_inc(s_sqk, 1)

            @block.gpsimd
            def _(pool):
                nc.gpsimd.memset(ident[:, :], 0.0).then_inc(c_pool, 1)
                nc.gpsimd.memset(own_block[:, :, :], 0.0).then_inc(c_pool, 1)
                nc.gpsimd.memset(half_mask[:, :], 0.0).then_inc(c_pool, 1)
                nc.gpsimd.memset(kq_hi[:, :, :, :].bitcast(F32), 0.0).then_inc(c_pool, 1)
                nc.gpsimd.memset(kq_lo[:, :, :, :].bitcast(F32), 0.0).then_inc(c_pool, 1)
                pool.wait_ge(c_pool, 5)
                nc.gpsimd.affine_select(out=ident[:, :], in_=ident[:, :], compare_op=ALU.not_equal, fill=1.0,
                                        base=0, pattern=[[-1, P]], channel_multiplier=1).then_inc(c_pool, 1)
                nc.gpsimd.memset(pick_group[:, :, :], 1.0).then_inc(c_pool, 1)
                nc.gpsimd.memset(half_mask[0:MB, 0:MB], 1.0).then_inc(c_pool, 1)
                nc.gpsimd.memset(ones_col[:, :], 1.0).then_inc(c_pool, 1)
                nc.gpsimd.memset(attn_eps[:, :], ATTN_EPS).then_inc(c_pool, 1)
                pool.wait_ge(c_pool, 10)
                nc.gpsimd.memset(half_mask[MB:P, MB:P], 1.0).then_inc(c_pool, 1)
                pool.wait_ge(c_pool, 11)
                n = 11
                for j in range(GPP):
                    nc.gpsimd.affine_select(out=own_block[:, :, :], in_=own_block[:, :, :], compare_op=ALU.not_equal,
                                            fill=1.0, base=-BLK * j, pattern=[[-1, BLK], [0, P]],
                                            channel_multiplier=1).then_inc(c_pool, 1)
                    n += 1
                    pool.wait_ge(c_pool, n)
                for h in range(2):
                    part = pick_group[:, h, :].rearrange("p (b m) -> p b m", b=2)
                    for sign, base in ((1, -BLK * h), (-1, BLK * h + BLK - 1)):
                        nc.gpsimd.affine_select(out=part, in_=part, compare_op=ALU.is_ge, fill=0.0, base=base,
                                                pattern=[[-sign * 2 * BLK, 2], [0, MB]],
                                                channel_multiplier=sign).then_inc(c_pool, 1)
                        n += 1
                        pool.wait_ge(c_pool, n)
                pool.wait_ge(a_whi, 1)
                nc.gpsimd.tensor_tensor(whh_lo[:, :, :], whh_sb[:, :, :], whh_hi[:, :, :].bitcast(F32),
                                        ALU.subtract).then_inc(p_wlo, 1)
                for b in range(B):
                    lo = (b % 2) * MB
                    pool.wait_ge(a_whi, 2 + b)
                    nc.gpsimd.tensor_tensor(kq_lo[:, :, b, lo:lo + MB], kq_f[:, :, b * MB:(b + 1) * MB],
                                            kq_hi[:, :, b, lo:lo + MB].bitcast(F32), ALU.subtract).then_inc(p_wlo, 1)
                for g in range(G1):
                    pool.wait_ge(s_sqk, g + 1)
                    add_squares(pool, g)

            @block.tensor
            def _(pe):
                pe.wait_ge(c_pool, 11)
                pe.wait_ge(v0, V_PN)
                for t in range(M // P):
                    for k in range(KC):
                        last = nc.tensor.transpose(bank[:, 0, k * M + t * P:k * M + (t + 1) * P],
                                                   ctx_sb[:, t, k * P:(k + 1) * P], ident[:, :])
                last.then_inc(t_pn, 1)
                pe.wait_ge(w_pn, 1)
                for w, (l, n) in enumerate(((wk_sb, l_wk), (wv_sb, l_wv))):
                    pe.wait_ge(n, 16)
                    for j in range(KC):
                        for k in range(KC):
                            last = nc.tensor.matmul(bank[:, 1 + w, j * M:(j + 1) * M], l[:, k, j * P:(j + 1) * P],
                                                    pn_t[:, k, :], start=(k == 0), stop=(k == KC - 1))
                    last.then_inc(m_w, 1)
                pe.wait_ge(e_w, 1)
                pe.wait_ge(l_wq, 16)
                for j in range(KC):
                    for k in range(KC):
                        last = nc.tensor.matmul(bank[:, 0, j * M:(j + 1) * M], wq_sb[:, k, j * P:(j + 1) * P],
                                                kp_t[:, k, :], start=(k == 0), stop=(k == KC - 1))
                last.then_inc(m_w, 1)
                pe.wait_ge(l_wih, 16)
                for n in range(2 * PAIRS):
                    pe.wait_ge(e_w, max(2 + n - (n > 0), 2))
                    for k in range(KC):
                        last = nc.tensor.matmul(bank[:, vw_bank[n], 0:W], vp_t[:, k, (n // 2) * P:(n // 2 + 1) * P],
                                                wih_sb[:, k, (n % 2) * W:(n % 2 + 1) * W],
                                                start=(k == 0), stop=(k == KC - 1))
                    last.then_inc(m_w, 1)
                for g in range(G1):
                    pe.wait_ge(n_x, (g + 1) * BLK)
                    if g >= 2:
                        pe.wait_ge(s_s0, g - 1)
                    turn_group(xs[:, g * BLK:(g + 1) * BLK, :], turn[:, g % 2, :, :])
                    if g >= 2:
                        sum_squares(pe, g - 2, 0, g - 2)

            @block.vector
            def _(dve):
                st = Steps(dve, v0)
                dve.wait_ge(c_act, 2)
                st.do(nc.vector.tensor_scalar(var[:, NT:NT + 2], csum[:, :], 1.0 / D, RMS_EPS, ALU.mult, ALU.add))
                rsqrt_steps(nc.vector, st.do, rstd[:, NT:NT + 2], var[:, NT:NT + 2], rtmp[:, NT:NT + 2])
                for t in range(M // P):
                    st.add(nc.vector.tensor_scalar(ctx_sb[:, t, :], ctx_sb[:, t, :], rstd[:, NT + t:NT + t + 1],
                                                   None, ALU.mult))
                assert st.n == V_PN
                dve.wait_ge(l_vec, 16)
                nc.vector.tensor_scalar(scaled_w[:, :], vecs[:, 12:14], SCALE, None, ALU.mult).then_inc(v_vec, 1)
                for g in range(G1):
                    dve.wait_ge(l_x[g], 16)
                    for t in range(g * BLK, (g + 1) * BLK):
                        st.add(nc.vector.bn_stats(stats[:, t, :], xs[:, t, :]))
                    if g == 0:
                        dve.wait_ge(t_pn, 1)
                        for k in range(KC):
                            last = nc.vector.tensor_scalar(pn_t[:, k, :], bank[:, 0, k * M:(k + 1) * M],
                                                           vecs[:, 14 + k:15 + k], None, ALU.mult)
                        last.then_inc(w_pn, 1)
                st.wait()
                ln_chain(dve, st, stats, mv, var[:, 0:NT], rstd[:, 0:NT], rtmp[:, 0:NT])

                def normalise(g):
                    for t in range(g * BLK, (g + 1) * BLK):
                        nc.vector.tensor_scalar(xs[:, t, :], xs[:, t, :], mv[:, t, 0:1], rstd[:, t:t + 1],
                                                ALU.subtract, ALU.mult).then_inc(n_x, 1)

                normalise(0)
                normalise(1)
                st.add(nc.vector.tensor_tensor(half_b_rz[:, :], vecs[:, 0:4], vecs[:, 6:10], ALU.add))
                st.add(nc.vector.tensor_copy(b_xn[:, :], vecs[:, 4:6]))
                st.add(nc.vector.tensor_scalar(half_b_hn[:, :], vecs[:, 10:12], 0.5, None, ALU.mult))
                st.wait()
                st.do(nc.vector.tensor_scalar(half_b_rz[:, :], half_b_rz[:, :], 0.5, None, ALU.mult))
                for g in range(G1):
                    dve.wait_ge(t_x, g + 1)
                    sl = slice(g * GROUP, (g + 1) * GROUP)
                    nc.vector.tensor_copy(slots[:, :, sl], turn[:, g % 2, :, :]).then_inc(s_s0, 1)
                    if g + 2 < G1:
                        normalise(g + 2)
                    if g >= 1:
                        first_low(dve, g - 1)
                for b in range(2):
                    dve.wait_ge(a_whi, 1 + B + b + 1)
                    nc.vector.tensor_tensor(vw_lo[rows_of(b), :, :], vw_f[rows_of(b), :, :],
                                            vw_hi[rows_of(b), :, b, :].bitcast(F32), ALU.subtract).then_inc(v_wlo, 1)
                    if b == 0:
                        first_low(dve, G1 - 1)
        with ExitStack() as loop:
            lsb, lps = tensors(loop)
            tr = lsb("tr", [P, KC, GROUP])
            tz = lsb("tz", [P, KC, GROUP])
            hb = lsb("hb", [P, KC, GROUP])
            nn = lsb("nn", [P, KC, GROUP])
            pre = lsb("pre", [P, GROUP])
            dif = lsb("dif", [P, GROUP])
            expo = lsb("expo", [P, 2 * GROUP])
            rms_c = lsb("rms_c", [P, 2, GROUP])
            csum_c = lsb("csum_c", [P, 2, GROUP])
            attn = lsb("attn", [P, PAIRS, 2, 2 * GROUP], F32R)
            attn_lo = lsb("attn_lo", [P, GROUP], F32R)
            spread = lsb("spread", [GPP * BLK, BLK, P])
            rsum = lsb("rsum", [P, P])
            ms = lsb("ms", [P, GPP * BLK])
            rms = lsb("rms", [P, GPP * BLK])
            rms_t = lsb("rms_t", [P, GPP * BLK])
            stats1 = lsb("stats1", [P, NT, 6])
            mv1 = lsb("mv1", [P, NT, 2])
            var1 = lsb("var1", [P, NT])
            rstd1 = lsb("rstd1", [P, NT])
            shift1 = lsb("shift1", [P, NT])
            rtmp1 = lsb("rtmp1", [P, NT])
            top = lsb("top", [P, 1])
            neg_top = lsb("neg_top", [P, 1])
            den = lsb("den", [P, 1])
            rden = lsb("rden", [P, 1])

            gate_banks = lps("gate_banks", [P, 4, GROUP])
            gate_r, gate_z, gate_h, gate_x = (gate_banks[:, i, :] for i in range(4))
            rms_b = lps("rms_b", [P, GROUP])
            score = lps("score", [P, 2, GROUP])

            m_r, m_z, m_h, m_x = (sem(f"m_{n}") for n in "rzhx")
            a_r, a_z, a_h, a_n = (sem(f"a_{n}") for n in "rzhn")
            v_q = sem("v_q")
            v_pre, v_dif, v_mix, v_new = (sem(f"v_{n}") for n in ("pre", "dif", "mix", "new"))
            v_ms = sem("v_ms")
            v_rms = sem("v_rms")
            v_rmsd = sem("v_rmsd")
            m_rmst = sem("m_rmst")
            v_diag = sem("v_diag")
            m_score, m_rms, m_csum = sem("m_score"), sem("m_rms"), sem("m_csum")
            a_rms, a_csum = sem("a_rms"), sem("a_csum")
            v_mul, v_top, v_neg, a_exp, v_rden, v_rsum = (sem(n) for n in
                                                          ("v_mul", "v_top", "v_neg", "a_exp", "v_rden", "v_rsum"))
            v_rec, v_attn, a_attn, v_alo = sem("v_rec"), sem("v_attn"), sem("a_attn"), sem("v_alo")
            d_alo = sem("d_alo")
            l_x1 = [sem(f"loaded_x{g}") for g in range(G1, G)]
            v_ln1 = sem("v_ln1")
            v_sh1 = sem("v_sh1")
            n_x1 = sem("n_x1")

            def x_tile(g):
                return (tr, tz, hb, nn)[g - G1][:, :, :].rearrange("p k (b d) -> p (k b) d", d=D)

            def turn_banks1(g):
                return gate_banks[:, g % 2 * KC:(g % 2 + 1) * KC, :]

            UNITS = 2 * G

            def tokens(pair, g4):
                g = pair * GPP + g4
                return slice(g * GROUP, (g + 1) * GROUP)

            block = loop.enter_context(nc.Block())

            @block.sync
            def _(sp):
                for g in range(G1, G):
                    sp.dma_start(x_tile(g), xv[g]).then_inc(l_x1[g - G1], 16)

                def move_low(s, pair, h):
                    sp.wait_ge(v_alo, 2 * s + h + 1)
                    for b in range(2):
                        sp.dma_start(attn[rows_of(1 - b), pair, b, h * GROUP:(h + 1) * GROUP].bitcast(F32),
                                     attn_lo[rows_of(b), :].bitcast(F32)).then_inc(d_alo, 16)

                with sp.Fori(0, ITERS) as it:
                    for pair in range(PAIRS):
                        for h in range(2):
                            move_low(2 * it + pair, pair, h)
                sp.wait_ge(d_alo, 32 * 2 * PAIRS * ITERS)

            @block.tensor
            def _(pe):
                def gru_unit(it, pair, g4, c, between=None):
                    u = it * UNITS + (pair * GPP + g4) * 2 + c
                    sl = tokens(pair, g4)
                    b = g4 // 2
                    half = slice((g4 % 2) * GROUP, (g4 % 2 + 1) * GROUP)
                    if c == 0:
                        pe.wait_ge(s_hi, it * G + pair * GPP + g4 + 1)
                        pe.wait_ge(s_lo, it * G + pair * GPP + g4 + 1)

                    def from_slots(out, f, stop):
                        n = 0
                        for k in range(KC):
                            for w, s in ((whh_hi, slots_hi), (whh_hi, slots_lo), (whh_lo, slots_hi)):
                                n += 1
                                last = nc.tensor.matmul(out[:, :], w[:, k, f * P:(f + 1) * P], s[:, k, sl],
                                                        start=(n == 1), stop=(stop and n == 3 * KC))
                        return last

                    def from_attention(out, f, start):
                        cols = slice(f * P, (f + 1) * P)
                        nc.tensor.matmul(out[:, :], vw_hi[:, pair, b, cols], attn[:, pair, b, half],
                                         start=start, stop=False)
                        return nc.tensor.matmul(out[:, :], vw_lo[rows_of(b), pair, cols], attn[rows_of(b), pair, b, half],
                                                start=False, stop=True)

                    def wait_attention():
                        pe.wait_ge(a_attn, 4 * it + 2 * pair + g4 % 2 + 1)
                        pe.wait_ge(d_alo, 32 * (4 * it + 2 * pair + g4 % 2 + 1))

                    pe.wait_ge(a_r, u + 1)
                    from_slots(gate_r, c, False)
                    if c == 0 and g4 == 0:
                        pe.wait_ge(a_z, u + 1)
                        from_slots(gate_z, 2 + c, False)
                        pe.wait_ge(a_h, u + 1)
                        from_slots(gate_h, 4 + c, True).then_inc(m_h, 1)
                        wait_attention()
                        from_attention(gate_r, c, False).then_inc(m_r, 1)
                        from_attention(gate_z, 2 + c, False).then_inc(m_z, 1)
                    else:
                        if c == 0:
                            wait_attention()
                        from_attention(gate_r, c, False).then_inc(m_r, 1)
                        pe.wait_ge(a_z, u + 1)
                        from_slots(gate_z, 2 + c, False)
                        from_attention(gate_z, 2 + c, False).then_inc(m_z, 1)
                        if between is not None:
                            between()
                        pe.wait_ge(a_h, u + 1)
                        from_slots(gate_h, 4 + c, True).then_inc(m_h, 1)
                    pe.wait_ge(v_pre, u + 1)
                    from_attention(gate_x, 4 + c, True).then_inc(m_x, 1)

                def scores(s, pair, split_before):
                    for h in range(2):
                        for part in (s_hi, s_lo):
                            pe.wait_ge(part, split_before + GPP - 1 + h)
                        n = 0
                        for b in range(2):
                            sl = tokens(pair, 2 * b + h)
                            for k in range(KC):
                                for w, x_ in ((kq_hi, slots_hi), (kq_hi, slots_lo), (kq_lo, slots_hi)):
                                    n += 1
                                    last = nc.tensor.matmul(score[:, h, :], w[:, k, 2 * pair + b, :], x_[:, k, sl],
                                                            start=(n == 1), stop=(n == 6 * KC))
                        last.then_inc(m_score, 1)

                def turn_rms(s):
                    pe.wait_ge(v_rmsd, s + 1)
                    nc.tensor.transpose(rms_b[0:GPP * BLK, 0:P], rms[:, :], ident[:, :]).then_inc(m_rmst, 1)

                def spread_rms(s, h):
                    if h == 0:
                        pe.wait_ge(v_diag, s + 1)
                    else:
                        pe.wait_ge(a_rms, 2 * s + 1)
                    nc.tensor.matmul(rms_b[:, :], pick_group[:, h, :], spread[:, :, :].rearrange("p b t -> p (b t)"),
                                     start=True, stop=True).then_inc(m_rms, 1)

                def column_sums(s):
                    pe.wait_ge(v_rsum, s + 1)
                    for h in range(2):
                        nc.tensor.matmul(score[:, h, :], rsum[:, :], expo[:, h * GROUP:(h + 1) * GROUP],
                                         start=True, stop=True).then_inc(m_csum, 1)

                def half_iteration(it, pair, softmax, more):
                    s = 2 * it + pair + 1
                    first_run = G * it + GPP * pair + G
                    gru_unit(it, pair, 0, 0)
                    gru_unit(it, pair, 0, 1)
                    if softmax:
                        sum_squares(pe, first_run - 1, 1 - pair, GPP - 1, (v_ms, s))
                        scores(s, 1 - pair, first_run - GPP)
                    gru_unit(it, pair, 1, 0, (lambda: turn_rms(s)) if softmax else None)
                    if softmax:
                        spread_rms(s, 0)
                    gru_unit(it, pair, 1, 1)
                    if softmax:
                        spread_rms(s, 1)
                    if more:
                        sum_squares(pe, first_run, pair, 0, (v_ms, s + 1))
                    gru_unit(it, pair, 2, 0)
                    gru_unit(it, pair, 2, 1)
                    if softmax:
                        column_sums(s)
                    if more:
                        sum_squares(pe, first_run + 1, pair, 1, (v_ms, s + 1))
                    gru_unit(it, pair, 3, 0)
                    gru_unit(it, pair, 3, 1)
                    if more:
                        sum_squares(pe, first_run + 2, pair, 2, (v_ms, s + 1))

                def turn_first(g):
                    pe.wait_ge(n_x1, g - G1 + 1)
                    if g >= G1 + 2:
                        pe.wait_ge(s_s0, g - 1)
                    turn_group(x_tile(g), turn_banks1(g))

                sum_squares(pe, G1 - 2, 0, G1 - 2)
                sum_squares(pe, G1 - 1, 0, G1 - 1)
                scores(0, 0, 0)
                turn_rms(0)
                spread_rms(0, 0)
                spread_rms(0, 1)
                column_sums(0)
                for g in range(G1, G):
                    turn_first(g)
                for g in range(G1, G - 1):
                    sum_squares(pe, g, 1, g - G1, (v_ms, 1))
                pe.wait_ge(s_s0, G)
                with pe.Fori(0, ITERS - 1) as it:
                    half_iteration(it, 0, True, True)
                    half_iteration(it, 1, True, True)
                half_iteration(ITERS - 1, 0, True, False)
                half_iteration(ITERS - 1, 1, False, False)

            @block.scalar
            def _(act):
                def gru_unit(it, pair, g4, c, meanwhile=None):
                    u = it * UNITS + (pair * GPP + g4) * 2 + c
                    act.wait_ge(v_q, u + 2)
                    act.wait_ge(m_r, u + 1)
                    nc.scalar.activation(tr[:, c, :], gate_r[:, :], ACT.Tanh, bias=half_b_rz[:, c:c + 1],
                                         scale=0.5).then_inc(a_r, 1)
                    act.wait_ge(m_z, u + 1)
                    nc.scalar.activation(tz[:, c, :], gate_z[:, :], ACT.Tanh, bias=half_b_rz[:, 2 + c:3 + c],
                                         scale=0.5).then_inc(a_z, 1)
                    act.wait_ge(m_h, u + 1)
                    nc.scalar.activation(hb[:, c, :], gate_h[:, :], ACT.Identity, bias=half_b_hn[:, c:c + 1],
                                         scale=0.5).then_inc(a_h, 1)
                    if meanwhile is not None:
                        meanwhile()
                    act.wait_ge(v_pre, u + 2)
                    nc.scalar.activation(nn[:, c, :], pre[:, :], ACT.Tanh, bias=b_xn[:, c:c + 1]).then_inc(a_n, 1)

                def slots_high(it, pair, g4):
                    act.wait_ge(v_new, it * UNITS + (pair * GPP + g4) * 2 + 3)
                    sl = tokens(pair, g4)
                    nc.scalar.activation(slots_hi[:, :, sl], slots[:, :, sl], ACT.Copy).then_inc(s_hi, 1)

                def copy_rms(s, h):
                    act.wait_ge(m_rms, 2 * s + h + 1)
                    nc.scalar.activation(rms_c[:, h, :], rms_b[:, :], ACT.Copy).then_inc(a_rms, 1)

                def exponentials(s):
                    act.wait_ge(v_neg, s + 1)
                    nc.scalar.activation(expo[:, :], expo[:, :], ACT.Exp, bias=neg_top[:, :],
                                         accum_out=den[:, :]).then_inc(a_exp, 1)

                def copy_csum(s):
                    for h in range(2):
                        act.wait_ge(m_csum, 2 * s + h + 1)
                        nc.scalar.activation(csum_c[:, h, :], score[:, h, :], ACT.Identity,
                                             bias=attn_eps[:, :]).then_inc(a_csum, 1)

                def attention_hi(s, pair, h):
                    act.wait_ge(v_attn, 2 * s + h + 1)
                    half = slice(h * GROUP, (h + 1) * GROUP)
                    for b in range(2):
                        last = nc.scalar.activation(attn[rows_of(b), pair, b, half], expo[rows_of(b), half], ACT.Copy)
                    last.then_inc(a_attn, 1)

                def half_iteration(it, pair, softmax, more=True):
                    s = 2 * it + pair + 1

                    def high(p, g4):
                        return (lambda: slots_high(it, p, g4)) if more else None

                    if not softmax:
                        attention_hi(s - 1, pair, 1)
                    if pair == 0:
                        def last_high():
                            act.wait_ge(s_lo, (it + 1) * G - 1)
                            slots_high(it - 1, 1, GPP - 1)
                        gru_unit(it, pair, 0, 0, last_high)
                    else:
                        gru_unit(it, pair, 0, 0, high(0, GPP - 1))
                    if softmax:
                        attention_hi(s - 1, pair, 1)
                    gru_unit(it, pair, 0, 1)
                    gru_unit(it, pair, 1, 0, high(pair, 0))
                    if softmax:
                        copy_rms(s, 0)
                    gru_unit(it, pair, 1, 1)
                    if softmax:
                        copy_rms(s, 1)
                    gru_unit(it, pair, 2, 0, high(pair, 1))
                    if softmax:
                        exponentials(s)
                    gru_unit(it, pair, 2, 1)
                    if softmax:
                        copy_csum(s)
                    gru_unit(it, pair, 3, 0, high(pair, 2))
                    if softmax:
                        attention_hi(s, 1 - pair, 0)
                    gru_unit(it, pair, 3, 1)

                for free in (a_r, a_z, a_h):
                    act.sem_inc(free, 1)
                def normalise(g):
                    act.wait_ge(v_sh1, 1)
                    for b in range(BLK):
                        t = (g - G1) * BLK + b
                        last = nc.scalar.activation(x_tile(g)[:, b, :], x_tile(g)[:, b, :], ACT.Identity,
                                                    bias=shift1[:, t:t + 1], scale=rstd1[:, t:t + 1])
                    last.then_inc(n_x1, 1)

                def first_slots(g):
                    sl = slice(g * GROUP, (g + 1) * GROUP)
                    act.wait_ge(t_x, g + 1)
                    nc.scalar.activation(slots[:, :, sl], turn_banks1(g), ACT.Copy).then_inc(s_s0, 1)

                copy_rms(0, 0)
                copy_rms(0, 1)
                exponentials(0)
                copy_csum(0)
                normalise(G1)
                normalise(G1 + 1)
                first_slots(G1)
                normalise(G1 + 2)
                first_slots(G1 + 1)
                attention_hi(0, 0, 0)
                normalise(G1 + 3)
                first_slots(G1 + 2)
                first_slots(G1 + 3)
                with act.Fori(0, ITERS - 1) as it:
                    half_iteration(it, 0, True)
                    half_iteration(it, 1, True)
                half_iteration(ITERS - 1, 0, True, more=False)
                half_iteration(ITERS - 1, 1, False, more=False)

            @block.vector
            def _(dve):
                def gru_unit(it, pair, g4, c, meanwhile=None):
                    u = it * UNITS + (pair * GPP + g4) * 2 + c
                    sl = tokens(pair, g4)
                    dve.wait_ge(a_r, u + 2)
                    dve.wait_ge(a_h, u + 2)
                    nc.vector.scalar_tensor_tensor(pre[:, :], tr[:, c, :], 1.0, hb[:, c, :], ALU.add,
                                                   ALU.mult).then_inc(v_q, 1)
                    dve.wait_ge(v_q, u + 3)
                    dve.wait_ge(m_x, u + 1)
                    nc.vector.tensor_tensor(pre[:, :], pre[:, :], gate_x[:, :], ALU.add).then_inc(v_pre, 1)
                    if meanwhile is not None:
                        meanwhile()
                    dve.wait_ge(a_n, u + 1)
                    nc.vector.tensor_tensor(dif[:, :], slots[:, c, sl], nn[:, c, :], ALU.subtract).then_inc(v_dif, 1)
                    dve.wait_ge(v_dif, u + 1)
                    dve.wait_ge(a_z, u + 2)
                    nc.vector.scalar_tensor_tensor(dif[:, :], tz[:, c, :], 1.0, dif[:, :], ALU.add,
                                                   ALU.mult).then_inc(v_mix, 1)
                    dve.wait_ge(v_mix, u + 1)
                    nc.vector.scalar_tensor_tensor(slots[:, c, sl], dif[:, :], 0.5, nn[:, c, :], ALU.mult,
                                                   ALU.add).then_inc(v_new, 1)

                def token_rms(s, pair):
                    dve.wait_ge(s_ss, GPP * (s + 1))
                    cols = slice(pair * GPP * BLK, (pair + 1) * GPP * BLK)
                    nc.vector.tensor_scalar(ms[:, :], ssq[:, cols], 1.0 / D, RMS_EPS, ALU.mult,
                                            ALU.add).then_inc(v_ms, 1)
                    dve.wait_ge(v_ms, s + 1)
                    n = [0]

                    def do(ins):
                        n[0] += 1
                        ins.then_inc(v_rms if n[0] < 11 else v_rmsd, 1)
                        if n[0] < 11:
                            dve.wait_ge(v_rms, s * 10 + n[0])

                    rsqrt_steps(nc.vector, do, rms[:, :], ms[:, :], rms_t[:, :])
                    assert n[0] == 11

                def spread_steps(s):
                    dve.wait_ge(m_rmst, s + 1)
                    nc.vector.tensor_tensor(
                        spread[:, :, :], own_block[:, :, :],
                        rms_b[0:GPP * BLK, 0:P].rearrange("p (a q) -> p a q", a=1).to_broadcast([GPP * BLK, BLK, P]),
                        ALU.mult).then_inc(v_diag, 1)

                def scale_scores(s, h):
                    dve.wait_ge(m_score, 2 * s + h + 1)
                    dve.wait_ge(a_rms, 2 * s + h + 1)
                    nc.vector.tensor_tensor(expo[:, h * GROUP:(h + 1) * GROUP], score[:, h, :], rms_c[:, h, :],
                                            ALU.mult).then_inc(v_mul, 1)

                def maximum(s):
                    dve.wait_ge(v_mul, 2 * s + 2)
                    nc.vector.reduce_max(top[:, :], expo[:, :], AX).then_inc(v_top, 1)
                    dve.wait_ge(v_top, s + 1)
                    nc.vector.tensor_scalar(neg_top[:, :], top[:, :], -1.0, None, ALU.mult).then_inc(v_neg, 1)

                def token_sum(s):
                    dve.wait_ge(a_exp, s + 1)
                    nc.vector.reciprocal(rden[:, :], den[:, :]).then_inc(v_rden, 1)
                    dve.wait_ge(v_rden, s + 1)
                    nc.vector.tensor_scalar(rsum[:, :], half_mask[:, :], rden[:, :], None, ALU.mult).then_inc(v_rsum, 1)

                def half_of(h):
                    return slice(h * GROUP, (h + 1) * GROUP)

                def csum_reciprocal(s, h, part):
                    dve.wait_ge(a_csum, 2 * s + h + 1)
                    cols = slice(part * GROUP // 2, (part + 1) * GROUP // 2)
                    nc.vector.reciprocal(csum_c[:, h, cols], csum_c[:, h, cols]).then_inc(v_rec, 1)

                def attention_half(s, h):
                    dve.wait_ge(v_rec, 4 * s + 2 * h + 2)
                    nc.vector.scalar_tensor_tensor(expo[:, half_of(h)], expo[:, half_of(h)], rden[:, :], csum_c[:, h, :],
                                                   ALU.mult, ALU.mult).then_inc(v_attn, 1)

                def attention_lo(s, pair, h, first=False):
                    dve.wait_ge(a_attn, 2 * s + h + 1)
                    if not first:
                        dve.wait_ge(d_alo, 32 * (2 * s + h))
                    for b in range(2):
                        last = nc.vector.tensor_tensor(attn_lo[rows_of(b), :], expo[rows_of(b), half_of(h)],
                                                       attn[rows_of(b), pair, b, half_of(h)].bitcast(F32), ALU.subtract)
                    last.then_inc(v_alo, 1)

                def half_iteration(it, pair, softmax):
                    s = 2 * it + pair + 1

                    def last_low():
                        attention_lo(s - 1, pair, 1)

                    gru_unit(it, pair, 0, 0, None if softmax else last_low)
                    gru_unit(it, pair, 0, 1, last_low if softmax else None)
                    if softmax:
                        token_rms(s, 1 - pair)
                        spread_steps(s)
                    gru_unit(it, pair, 1, 0)
                    if softmax:
                        scale_scores(s, 0)
                    gru_unit(it, pair, 1, 1)
                    if softmax:
                        scale_scores(s, 1)
                        maximum(s)
                    gru_unit(it, pair, 2, 0)
                    if softmax:
                        token_sum(s)
                    gru_unit(it, pair, 2, 1)
                    if softmax:
                        csum_reciprocal(s, 0, 0)
                        csum_reciprocal(s, 0, 1)
                    gru_unit(it, pair, 3, 0, (lambda: attention_half(s, 0)) if softmax else None)
                    if softmax:
                        attention_lo(s, 1 - pair, 0)
                        csum_reciprocal(s, 1, 0)
                    gru_unit(it, pair, 3, 1, (lambda: csum_reciprocal(s, 1, 1)) if softmax else None)
                    if softmax:
                        attention_half(s, 1)

                dve.sem_inc(v_q, 2)
                dve.sem_inc(v_pre, 1)
                dve.sem_inc(v_new, 1)
                token_rms(0, 0)
                spread_steps(0)
                ln = Steps(dve, v_ln1)
                for g in range(G1, G):
                    dve.wait_ge(l_x1[g - G1], 16)
                    for b in range(BLK):
                        ln.add(nc.vector.bn_stats(stats1[:, (g - G1) * BLK + b, :], x_tile(g)[:, b, :]))
                    if g == G1 + 1:
                        scale_scores(0, 0)
                        scale_scores(0, 1)
                        maximum(0)
                token_sum(0)
                ln.wait()
                ln_chain(dve, ln, stats1, mv1, var1[:, :], rstd1[:, :], rtmp1[:, :])
                nc.vector.scalar_tensor_tensor(shift1[:, :], mv1[:, :, 0], -1.0, rstd1[:, :], ALU.mult,
                                               ALU.mult).then_inc(v_sh1, 1)
                csum_reciprocal(0, 0, 0)
                csum_reciprocal(0, 0, 1)
                attention_half(0, 0)
                csum_reciprocal(0, 1, 0)
                csum_reciprocal(0, 1, 1)
                attention_lo(0, 0, 0, first=True)
                attention_half(0, 1)
                for g in range(G1, G):
                    sl = slice(g * GROUP, (g + 1) * GROUP)
                    dve.wait_ge(s_s0, g + 1)
                    if g < G - 1:
                        nc.vector.tensor_copy(slots_hi[:, :, sl], slots[:, :, sl]).then_inc(s_hi, 1)
                    first_low(dve, g)
                with dve.Fori(0, ITERS - 1) as it:
                    half_iteration(it, 0, True)
                    half_iteration(it, 1, True)
                half_iteration(ITERS - 1, 0, True)
                half_iteration(ITERS - 1, 1, False)

            @block.gpsimd
            def _(pool):
                def multiply(g):
                    sl = slice(g * GROUP, (g + 1) * GROUP)
                    nc.gpsimd.tensor_tensor(square[:, g % 2, :, :], slots[:, :, sl], slots[:, :, sl],
                                            ALU.mult).then_inc(s_sqk, 1)

                for g in range(G1, G):
                    pool.wait_ge(s_s0, g + 1)
                    pool.wait_ge(s_ss, g - 1)
                    multiply(g)
                    pool.wait_ge(s_sqk, g + 1)
                    add_squares(pool, g)
                with pool.Fori(0, ITERS - 1) as it:
                    for g in range(G):
                        run = it * G + g + G
                        pool.wait_ge(v_new, it * UNITS + 2 * g + 3)
                        pool.wait_ge(s_ss, run - 1)
                        sl = slice(g * GROUP, (g + 1) * GROUP)
                        multiply(g)
                        pool.wait_ge(s_sqk, run + 1)
                        add_squares(pool, g)
                        pool.wait_ge(s_hi, run + 1)
                        nc.gpsimd.tensor_tensor(slots_lo[:, :, sl], slots[:, :, sl], slots_hi[:, :, sl].bitcast(F32),
                                                ALU.subtract).then_inc(s_lo, 1)
        attention.close()
        E = gate_t.shape[1]
        CAP = -(-T // E) * 2
        WCOL = 6 * P
        FS = w_shared.shape[1]
        FE = w_expert.shape[2]
        HALF_F = FE // 2
        LAG = 2
        G_BIS = G // 2
        ROW = D + E
        BIG = 8192.0
        HALF_T = T // 2
        AW, BW = 32, 16
        W = BLK * G
        HOT = W // (2 * FS)
        assert G * E == P and CAP == AW * BW and 2 * FS * G_BIS >= 30 and E % BLK == 0 and FS == BLK == 4
        rows = nc.dram_tensor("token_rows", (T, ROW), F32, kind="Internal").ap()
        ids = nc.dram_tensor("token_ids", (E, CAP), U32, kind="Internal").ap()
        hrows = rows[:, 0:D].rearrange("(g b p) d -> g p b d", b=BLK, p=P)

        def right(name, shape, dt=F32):
            return whole.enter_context(nc.sbuf_tensor(name, shape, dt, side="right"))

        raw = right("raw", [P, FE, WCOL])
        idx_all = right("idx_all", [P, E, BLK], U32)
        idx_in = right("idx_in", [P, BLK], U32)
        got = right("got", [P, BLK, ROW])
        y = right("y", [P, BLK, D])
        l_w = [sem("l_w0"), sem("l_w1")]
        l_idx, p_idx, g_in_, w_y = sem("l_idx"), sem("p_idx"), sem("gathered"), sem("w_y")

        with ExitStack() as dense:
            lsb, lps = tensors(dense)
            sg = lsb("sg", [P, GROUP])
            thr = lsb("thr", [P, 1], I32)
            same_e = lsb("same_e", [P, P])
            before = lsb("before", [P, P])
            work = lsb("work", [P, 8, GROUP])
            x_pairs = (work[:, 0:4, :].rearrange("p a t -> p (a t)").rearrange("p (s b d) -> p s b d", b=BLK, d=D),
                       raw[:, HALF_F:, :].rearrange("p f c -> p (f c)")[:, 0:2 * BLK * D]
                       .rearrange("p (s b d) -> p s b d", b=BLK, d=D))
            hg = work[:, 4:8, :].rearrange("p a t -> p (a t)").rearrange("p (s b d) -> p s b d", b=BLK, d=D)
            gw_f = lsb("gw_f", [P, KC, E])
            gw_hi = lsb("gw_hi", [P, KC, 2 * P - E], F32R)
            gw_lo = lsb("gw_lo", [P, KC, 2 * P - E], F32R)
            sh_hi = lsb("sh_hi", [P, FS, WCOL], F32R)
            sh_lo = lsb("sh_lo", [P, FS, WCOL], F32R)
            silu = lsb("silu", [P, 2, GROUP])
            hid = lsb("hid", [P, 2, GROUP])
            hid_hi = lsb("hid_hi", [P, FS, GROUP], F32R)
            hid_lo = lsb("hid_lo", [P, FS, GROUP], F32R)
            stats2 = lsb("stats2", [P, 2 * BLK, 6])
            mv2 = lsb("mv2", [P, 2 * BLK, 2])
            var2 = lsb("var2", [P, 2 * BLK])
            rstd2 = lsb("rstd2", [P, 2, 2 * BLK])
            shift2 = lsb("shift2", [P, 2, 2 * BLK])
            rtmp2 = lsb("rtmp2", [P, 2 * BLK])
            bit = lsb("bit", [P, 1], I32)
            cand = lsb("cand", [P, 1], I32)
            keep = lsb("keep", [P, 1], I32)
            cnt = lsb("cnt", [P, 1])
            score_t = lsb("score_t", [P, GROUP])
            tots = lsb("tots", [P, 4])
            offs = lsb("offs", [P, 4])
            hi_f = lsb("hi_f", [P, GROUP], F16)
            lo_f = lsb("lo_f", [P, GROUP], F16)
            iota_i = lsb("iota_i", [P, AW], I32)
            iota_f = lsb("iota_f", [P, AW], F16)
            tok_i = lsb("tok_i", [P, W], I32)
            tok_f = lsb("tok_f", [P, W])
            ids_sb = lsb("ids_sb", [P, E // BLK, BW], U32)
            wide = lps("wide", [P, 4, 512])
            down = lps("down", [P, 2, 512])
            logit = lps("logit", [P, 512])
            small = lps("small", [P, 512])

            above = work[:, 0, :]
            tie = work[:, 1, :]
            count = work[:, 2, :]
            taken = work[:, 3, :]
            slot = work[:, 4, :]
            ones = work[:, 5, :]
            slot_i = work[:, 6, :].bitcast(I32)
            hi_i = work[:, 7, :].bitcast(I32)
            lo_i = work[:, 0, :].bitcast(I32)
            h_f = (silu, hid)
            hot_b = work[:, :, :].rearrange("p a b -> p (a b)").bitcast(F16).rearrange("p (w e b) -> p w (e b)", e=E, b=BW)
            HOT_F = HOT * E * AW // 2
            free = [got[:, :, :].rearrange("p b c -> p (b c)")]
            free += [raw[:, HALF_F:FE, :].rearrange("p f c -> p (f c)")[:, i * HOT_F:] for i in range(3)]
            free += [slots[:, k, i * HOT_F:] for k in range(KC) for i in range(G_BIS * GROUP // HOT_F)]
            hot_a = [part[:, 0:HOT_F].bitcast(F16).rearrange("p (w e a) -> p w (e a)", e=E, a=AW) for part in free]
            assert len(hot_a) * HOT == W

            l_sh, l_gw = sem("l_sh"), sem("l_gw")
            l_xg = [sem(f"l_xg{i}") for i in range(4)]
            w_rows = [sem(f"w_rows{i}") for i in range(2)]
            p2 = sem("p2")
            t_tok, t_h = sem("t_tok"), sem("t_h")
            v2 = sem("v2")
            v_x1, v_st, v_ln, a_norm, v_norm = (sem(n) for n in ("v_x1", "v_st", "v_ln", "a_norm", "v_norm"))
            a_hf, a_hh, h_lo = sem("a_hf"), sem("a_hh"), sem("h_lo")
            v_gw, p_sh, a_sh = sem("v_gw"), sem("p_sh"), sem("a_sh")
            m_log, a_sg, t_score, a_score, w_score = (sem(n) for n in ("m_log", "a_sg", "t_score", "a_score", "w_score"))
            m_g, m_u, a_silu, v_hid, a_hid, p_lo = (sem(n) for n in ("m_g", "m_u", "a_silu", "v_hid", "a_hid", "p_lo"))
            m_dn, a_y, p_y = sem("m_dn"), sem("a_y"), sem("p_y")
            v_cnt, m_cnt, v_bis, v_bit = sem("v_cnt"), sem("m_cnt"), sem("v_bis"), sem("v_bit")
            v_tot, m_tot, v_slot, t_slot = sem("v_tot"), sem("m_tot"), sem("v_slot"), sem("t_slot")
            v_hot, a_hot, m_ids, v_ids, w_ids = (sem(n) for n in ("v_hot", "a_hot", "m_ids", "v_ids", "w_ids"))

            block = dense.enter_context(nc.Block())

            def x_of(g):
                return x_pairs[g // 2 % 2][:, g % 2, :, :]

            @block.sync
            def _(sp):
                def load_x(g):
                    if g >= 4:
                        sp.wait_ge(v_x1, g - 3)
                    sp.dma_start(x_of(g), xv[g]).then_inc(l_xg[g % 4], 16)

                def store_h(g):
                    if g < G - 2:
                        sp.wait_ge(a_norm, g + 1)
                    else:
                        sp.wait_ge(v_norm, g - (G - 2) + 1)
                    sp.dma_start(hrows[g], hg[:, g % 2, :, :]).then_inc(w_rows[g % 2], 16)

                for g in range(4):
                    load_x(g)
                sp.dma_start(gw_f[:, :, :], gate_t.rearrange("(k p) e -> p k e", p=P)).then_inc(l_gw, 16)
                sp.dma_start(raw[:, 0:FS, :], w_shared).then_inc(l_sh, 16)
                for g in range(G):
                    if g + 4 < G:
                        load_x(g + 4)
                    store_h(g)
                sp.wait_ge(a_sh, 1)
                sp.wait_ge(p_sh, FS)
                sp.dma_start(raw[:, 0:HALF_F, :], w_expert[0, :, 0:HALF_F, :]).then_inc(l_w[0], 16)
                sp.wait_ge(a_score, 1)
                srows = rows[:, D:ROW].rearrange("(g c p) e -> c p g e", c=BLK, p=P)
                for c in range(BLK):
                    sp.dma_start(srows[c], score_t[:, c * P:(c + 1) * P].rearrange("p (g e) -> p g e", e=E))\
                        .then_inc(w_score, 16)

                def store_y(g):
                    sp.wait_ge(p_y, g + 1)
                    sp.dma_start(out[bass.ds(g * GROUP, GROUP), :].rearrange("(b p) d -> p b d", p=P),
                                 y[:, :, :]).then_inc(w_y, 16)

                with sp.Fori(0, G - 1) as g:
                    store_y(g)
                sp.wait_ge(v_ids, 1)
                idv = ids.rearrange("(q f) (a b) -> f a q b", f=BLK, b=BW)
                for f in range(BLK):
                    sp.dma_start(idv[f], ids_sb[f * AW:(f + 1) * AW, :, :]).then_inc(w_ids, 16)
                sp.wait_ge(w_ids, 16 * BLK)
                sp.dma_start(idx_all[:, :, :], ids.rearrange("e (p j) -> p e j", j=BLK)).then_inc(l_idx, 16)
                sp.wait_ge(m_ids, 1)
                sp.dma_start(raw[:, HALF_F:FE, :], w_expert[0, :, HALF_F:FE, :]).then_inc(l_w[1], 16)
                store_y(G - 1)
                sp.wait_ge(w_score, 16 * BLK)
                for i in range(2):
                    sp.wait_ge(w_rows[i], 16 * G // 2)

            def plus_x1(engine, g):
                yv = y[:, :, :].rearrange("p b (k q) -> p k b q", k=KC)
                x1 = slots[:, :, bass.ds(g * GROUP, GROUP)].rearrange("p k (b q) -> p k b q", q=P)
                engine.tensor_tensor(yv, yv, x1, ALU.add).then_inc(p_y, 1)

            @block.gpsimd
            def _(pool):
                def iota_select(dst, src, op, fill, base):
                    nc.gpsimd.affine_select(out=dst[:, :], in_=src[:, :], compare_op=op, fill=fill, base=base,
                                            pattern=[[1, P]], channel_multiplier=-1).then_inc(p2, 1)

                nc.gpsimd.memset(gw_hi[:, :, :].bitcast(F32), 0.0).then_inc(p2, 1)
                nc.gpsimd.memset(gw_lo[:, :, :].bitcast(F32), 0.0).then_inc(p2, 1)
                nc.gpsimd.memset(same_e[:, :], 0.0).then_inc(p2, 1)
                for n in range(1 - G, G):
                    pool.wait_ge(p2, 3 + n + G - 1)
                    iota_select(same_e, same_e, ALU.not_equal, 1.0, -E * n)
                pool.wait_ge(p2, 3 + 2 * G - 1)
                iota_select(before, same_e, ALU.is_ge, 0.0, -1)
                nc.gpsimd.iota(iota_i[:, :], pattern=[[1, AW]], base=0, channel_multiplier=0).then_inc(p2, 1)
                nc.gpsimd.iota(tok_i[:, :], pattern=[[P, BLK], [GROUP, G]], base=-HALF_T,
                               channel_multiplier=1).then_inc(p2, 1)
                pool.wait_ge(p2, 3 + 2 * G + 2)
                nc.gpsimd.tensor_copy(iota_f[:, :], iota_i[:, :]).then_inc(p2, 1)
                nc.gpsimd.tensor_copy(tok_f[:, :], tok_i[:, :]).then_inc(p2, 1)
                for g in range(G - 2):
                    if g >= 2:
                        f = g - 2
                        pool.wait_ge(a_sh, 1)
                        nc.gpsimd.tensor_tensor(sh_lo[:, f, :], raw[:, f, :], sh_hi[:, f, :].bitcast(F32),
                                                ALU.subtract).then_inc(p_sh, 1)
                    sl = slice(g * GROUP, (g + 1) * GROUP)
                    pool.wait_ge(a_hf, g + 1)
                    pool.wait_ge(a_hh, g + 1)
                    nc.gpsimd.tensor_tensor(slots_lo[:, :, sl], h_f[g % 2][:, :, :],
                                            slots_hi[:, :, sl].bitcast(F32), ALU.subtract).then_inc(h_lo, 1)

                def hidden_lo(n, f):
                    pool.wait_ge(a_hid, n + 3)
                    nc.gpsimd.tensor_tensor(hid_lo[:, f % FS, :], hid[:, f % 2, :], hid_hi[:, f % FS, :].bitcast(F32),
                                            ALU.subtract).then_inc(p_lo, 1)

                def add_x1(g):
                    pool.wait_ge(a_y, g + 2)
                    plus_x1(nc.gpsimd, g)

                pool.sem_inc(p_lo, 2)
                for f in range(LAG):
                    hidden_lo(f, f)
                with pool.Fori(0, G - 1) as g:
                    for f in range(FS):
                        hidden_lo(g * FS + f + LAG, f + LAG)
                    add_x1(g)
                for f in range(FS - LAG):
                    hidden_lo((G - 1) * FS + f + LAG, f + LAG)
                pool.wait_ge(l_idx, 16)
                pool.wait_ge(w_score, 16 * BLK)
                for i in range(2):
                    pool.wait_ge(w_rows[i], 16 * G // 2)
                nc.gpsimd.tensor_copy(idx_in[:, :], idx_all[:, 0, :]).then_inc(p_idx, 1)
                pool.wait_ge(p_idx, 1)
                for j in range(BLK):
                    pool.indirect_dma_start(got[:, j, :], None, rows,
                                            bass.IndirectOffsetOnAxis(idx_in[:, j:j + 1], 0)).then_inc(g_in_, 16)

            def turn_banks(g):
                return down if g % 2 == 0 else wide

            def h_banks(g):
                return down if g == G - 1 else wide[:, 2:4, :]

            def count_mm():
                return nc.tensor.matmul(small[:, 0:1], same_e[:, :], cnt[:, :], start=True, stop=True)

            @block.tensor
            def _(pe):
                def turn_slots(g):
                    if g >= 2:
                        pe.wait_ge(v_x1, g - 1)
                    for b in range(BLK):
                        for k in range(KC):
                            c0 = g * GROUP + b * P
                            last = nc.tensor.transpose(turn_banks(g)[:, k, b * P:(b + 1) * P], slots[:, k, c0:c0 + P],
                                                       ident[:, :])
                    last.then_inc(t_tok, 1)

                def turn_h(g):
                    if g < G - 2:
                        pe.wait_ge(a_norm, g + 1)
                    else:
                        pe.wait_ge(v_norm, g - (G - 2) + 1)
                    if g == G - 1:
                        pe.wait_ge(v_x1, g)
                    elif g >= 1:
                        pe.wait_ge(a_hh, g)
                    for b in range(BLK):
                        for k in range(KC):
                            last = nc.tensor.transpose(h_banks(g)[:, k, b * P:(b + 1) * P], hg[:, g % 2, b, k * P:(k + 1) * P],
                                                       ident[:, :])
                    last.then_inc(t_h, 1)

                def router(g):
                    pe.wait_ge(h_lo, g + 1)
                    sl = slice(g * GROUP, (g + 1) * GROUP)
                    c0 = P - E - g * E
                    n = 0
                    for k in range(KC):
                        for w, h in ((gw_hi, slots_hi), (gw_hi, slots_lo), (gw_lo, slots_hi)):
                            n += 1
                            last = nc.tensor.matmul(logit[:, :], w[:, k, c0:c0 + P], h[:, k, sl],
                                                    start=(g == 0 and n == 1), stop=(g == G - 1 and n == 3 * KC))
                    return last

                def into_hidden(n, g, f, between=None):
                    sl = bass.ds(g * GROUP, GROUP)
                    for bank, s_m, s_v, c in ((f % 2, m_g, a_silu, 0), (2 + f % 2, m_u, v_hid, 2)):
                        pe.wait_ge(s_v, n + 1)
                        m = 0
                        for k in range(KC):
                            if c == 2 and k == 1 and between is not None:
                                between()
                            cols = slice((c + k) * P, (c + k + 1) * P)
                            for w, h in ((sh_hi, slots_hi), (sh_hi, slots_lo), (sh_lo, slots_hi)):
                                m += 1
                                last = nc.tensor.matmul(wide[:, bank, :], w[:, f, cols], h[:, k, sl],
                                                        start=(m == 1), stop=(m == 3 * KC))
                        last.then_inc(s_m, 1)

                def out_of_hidden(n, g, f):
                    pe.wait_ge(p_lo, n + 3)
                    if f == 0:
                        pe.wait_ge(a_y, g + 1)
                    for b in range(BLK):
                        tok = slice(b * P, (b + 1) * P)
                        for m, (h, w) in enumerate(((hid_hi, sh_hi), (hid_lo, sh_hi), (hid_hi, sh_lo))):
                            last = nc.tensor.matmul(down[:, b // 2, (b % 2) * D:(b % 2 + 1) * D], h[:, f, tok],
                                                    w[:, f, 4 * P:6 * P], start=(f == 0 and m == 0 and b % 2 == 0),
                                                    stop=(f == FS - 1 and m == 2), skip_group_check=True)
                    last.then_inc(m_dn, 1)

                def body(g, f, between=None):
                    n = g * FS + f
                    into_hidden(n + LAG, g + (f + LAG) // FS, (f + LAG) % FS, between)
                    out_of_hidden(n, g, f)

                def count_product(u):
                    pe.wait_ge(v_cnt, u + 1)
                    count_mm().then_inc(m_cnt, 1)

                for g in range(4):
                    turn_slots(g)
                pe.wait_ge(v_gw, 2)
                for g in range(G):
                    turn_h(g)
                    if g + 4 < G:
                        turn_slots(g + 4)
                    if g >= 2 and g < G - 2:
                        router(g - 2)
                for g in range(G - 4, G - 2):
                    router(g)
                router(G - 2)
                router(G - 1).then_inc(m_log, 1)
                pe.wait_ge(p_sh, FS)
                pe.wait_ge(p2, 3 + 2 * G)
                pe.sem_inc(m_dn, FS)
                pe.wait_ge(v_x1, G)
                pe.wait_ge(a_hh, G)
                into_hidden(0, 0, 0)
                pe.wait_ge(a_sg, 1)
                for c in range(BLK):
                    last = nc.tensor.transpose(logit[:, c * P:(c + 1) * P], sg[:, c * P:(c + 1) * P], ident[:, :])
                last.then_inc(t_score, 1)
                into_hidden(1, 0, 1)
                with pe.Fori(0, G_BIS) as g:
                    for f in range(FS):
                        u = (g * FS + f) * 2
                        body(g, f, lambda: count_product(u))
                        count_product(u + 1)
                body(G_BIS, 0)
                pe.wait_ge(v_tot, 1)
                nc.tensor.matmul(small[:, 1:2], same_e[:, :], tots[:, 0:1], start=True, stop=True)
                nc.tensor.matmul(small[:, 2:3], before[:, :], tots[:, 1:2], start=True, stop=True).then_inc(m_tot, 1)
                body(G_BIS, 1)
                pe.wait_ge(v_tot, 2)
                nc.tensor.matmul(small[:, 3:4], before[:, :], tots[:, 2:3], start=True, stop=True).then_inc(m_tot, 1)
                body(G_BIS, 2)
                pe.wait_ge(v_slot, 1)
                pe.wait_ge(a_score, 1)
                for c in range(BLK):
                    last = nc.tensor.transpose(logit[:, c * P:(c + 1) * P], slot[:, c * P:(c + 1) * P], ident[:, :])
                last.then_inc(t_slot, 1)
                body(G_BIS, 3)
                for g in range(G_BIS + 1, G - 1):
                    for f in range(FS):
                        body(g, f)
                body(G - 1, 0)
                pe.wait_ge(a_hot, W)
                for q in range(E // BLK):
                    for w in range(W):
                        last = nc.tensor.matmul(small[:, q * BLK * BW:(q + 1) * BLK * BW],
                                                hot_a[w // HOT][:, w % HOT, q * P:(q + 1) * P],
                                                hot_b[:, w, q * BLK * BW:(q + 1) * BLK * BW],
                                                start=(w == 0), stop=(w == W - 1))
                last.then_inc(m_ids, 1)
                body(G - 1, 1)
                for f in range(FS - LAG, FS):
                    out_of_hidden((G - 1) * FS + f, G - 1, f)

            @block.scalar
            def _(act):
                def normalise(g):
                    act.wait_ge(v_ln, g // 2 + 1)
                    if g >= 2:
                        act.wait_ge(w_rows[g % 2], 16 * (g // 2))
                        act.wait_ge(t_h, g - 1)
                    for b in range(BLK):
                        c0 = g * GROUP + b * P
                        i, j = g // 2 % 2, g % 2 * BLK + b
                        last = nc.scalar.activation(hg[:, g % 2, b, :].rearrange("p (k q) -> p k q", k=KC), slots[:, :, c0:c0 + P], ACT.Identity,
                                                    bias=shift2[:, i, j:j + 1], scale=rstd2[:, i, j:j + 1])
                    last.then_inc(a_norm, 1)

                def copy_h(g):
                    act.wait_ge(t_h, g + 1)
                    sl = slice(g * GROUP, (g + 1) * GROUP)
                    if g < G - 2:
                        if g >= 2:
                            act.wait_ge(h_lo, g - 1)
                        nc.scalar.activation(h_f[g % 2][:, :, :], h_banks(g)[:, :, :], ACT.Copy).then_inc(a_hf, 1)
                    nc.scalar.activation(slots_hi[:, :, sl], h_banks(g)[:, :, :], ACT.Copy).then_inc(a_hh, 1)

                def hidden(n, f):
                    act.wait_ge(m_g, n + 1)
                    act.wait_ge(v_hid, n + 1)
                    nc.scalar.activation(silu[:, f % 2, :], wide[:, f % 2, :], ACT.Silu).then_inc(a_silu, 1)
                    act.wait_ge(v_hid, n + 3)
                    act.wait_ge(m_dn, n + 1)
                    nc.scalar.activation(hid_hi[:, f % FS, :], hid[:, f % 2, :], ACT.Copy).then_inc(a_hid, 1)

                def scale_sums(g):
                    act.wait_ge(m_dn, (g + 2) * FS)
                    act.wait_ge(w_y, 16 * g + 1)
                    nc.scalar.activation(y[:, :, :].rearrange("p b d -> p (b d)"),
                                         down[:, :, :].rearrange("p a c -> p (a c)"), ACT.Copy,
                                         scale=tanh_g[:, 1:2]).then_inc(a_y, 1)

                def token_numbers(i):
                    act.wait_ge(v_hot, 2 * (i + 1))
                    for w in range(i * HOT, (i + 1) * HOT):
                        nc.scalar.activation(hot_b[:, w, :], hot_b[:, w, :], ACT.Copy,
                                             scale=tok_f[:, w:w + 1]).then_inc(a_hot, 1)

                normalise(0)
                normalise(1)
                copy_h(0)
                act.wait_ge(l_sh, 16)
                nc.scalar.activation(sh_hi[:, :, :], raw[:, 0:FS, :], ACT.Copy).then_inc(a_sh, 1)
                copy_h(1)
                for g in range(2, G, 2):
                    if g < G - 2:
                        normalise(g)
                        normalise(g + 1)
                    copy_h(g)
                    copy_h(g + 1)
                act.sem_inc(a_silu, 2)
                act.sem_inc(a_hid, 2)
                act.sem_inc(a_y, 1)
                act.sem_inc(w_y, 1)
                act.wait_ge(m_log, 1)
                nc.scalar.activation(sg[:, :], logit[:, :], ACT.Sigmoid).then_inc(a_sg, 1)
                nc.scalar.preload_act_table(ACT.Silu)
                hidden(0, 0)
                act.wait_ge(t_score, 1)
                nc.scalar.activation(score_t[:, :], logit[:, :], ACT.Copy).then_inc(a_score, 1)
                hidden(1, 1)
                with act.Fori(0, G_BIS + 1) as g:
                    for f in range(FS):
                        hidden(g * FS + f + LAG, f + LAG)
                    scale_sums(g)
                act.wait_ge(p2, 3 + 2 * G + 4)
                for g in range(G_BIS + 1, G - 1):
                    for f in range(FS):
                        hidden(g * FS + f + LAG, f + LAG)
                        token_numbers((g - G_BIS - 1) * FS + f)
                    scale_sums(g)
                hidden(G * FS - 2, FS - 2)
                hidden(G * FS - 1, FS - 1)
                scale_sums(G - 1)

            @block.vector
            def _(dve):
                st = Steps(dve, v2)

                def add_x(g):
                    sl = slice(g * GROUP, (g + 1) * GROUP)
                    dve.wait_ge(t_tok, g + 1)
                    dve.wait_ge(l_xg[g % 4], 16 * (g // 4 + 1))
                    for k in range(KC):
                        last = nc.vector.scalar_tensor_tensor(
                            slots[:, k, sl].rearrange("p (b q) -> p b q", q=P),
                            turn_banks(g)[:, k, :].rearrange("p (b q) -> p b q", q=P), tanh_g[:, 0:1],
                            x_of(g)[:, :, k * P:(k + 1) * P], ALU.mult, ALU.add)
                    last.then_inc(v_x1, 1)

                def statistics(g, b):
                    if b == 0:
                        dve.wait_ge(v_x1, g + 1)
                    c0 = g * GROUP + b * P
                    nc.vector.bn_stats(stats2[:, g % 2 * BLK + b, :], slots[:, :, c0:c0 + P]).then_inc(v_st, 1)

                def chain(q):
                    dve.wait_ge(v_st, 2 * BLK * (q + 1))
                    for j in range(2 * BLK):
                        st.add(nc.vector.bn_aggr(mv2[:, j, :], stats2[:, j, :]))
                    st.wait()
                    if q >= 2:
                        dve.wait_ge(a_norm, 2 * q - 2)

                    def do(ins):
                        st.add(ins)
                        st.wait()

                    do(nc.vector.tensor_scalar(var2[:, :], mv2[:, :, 1], LN_EPS, None, ALU.add))
                    rsqrt_steps(nc.vector, do, rstd2[:, q % 2, :], var2[:, :], rtmp2[:, :])
                    nc.vector.scalar_tensor_tensor(shift2[:, q % 2, :], mv2[:, :, 0], -1.0, rstd2[:, q % 2, :], ALU.mult,
                                                   ALU.mult).then_inc(v_ln, 1)
                    dve.wait_ge(v_ln, q + 1)

                for q in range(G // 2):
                    for g in (2 * q, 2 * q + 1):
                        add_x(g)
                    for g in (2 * q, 2 * q + 1):
                        for b in range(BLK):
                            statistics(g, b)
                    chain(q)
                    if q == 0:
                        dve.wait_ge(l_gw, 16)
                        dve.wait_ge(p2, 2)
                        nc.vector.tensor_copy(gw_hi[:, :, P - E:P], gw_f[:, :, :]).then_inc(v_gw, 1)
                        dve.wait_ge(v_gw, 1)
                        nc.vector.tensor_tensor(gw_lo[:, :, P - E:P], gw_f[:, :, :], gw_hi[:, :, P - E:P].bitcast(F32),
                                                ALU.subtract).then_inc(v_gw, 1)
                for g in (G - 2, G - 1):
                    dve.wait_ge(w_rows[g % 2], 16 * (g // 2))
                    dve.wait_ge(t_h, g - 1)
                    for b in range(BLK):
                        c0 = g * GROUP + b * P
                        i, j = g // 2 % 2, g % 2 * BLK + b
                        last = nc.vector.tensor_scalar(
                            hg[:, g % 2, b, :].rearrange("p (k q) -> p k q", k=KC), slots[:, :, c0:c0 + P],
                            rstd2[:, i, j:j + 1], shift2[:, i, j:j + 1], ALU.mult, ALU.add)
                    last.then_inc(v_norm, 1)
                dve.wait_ge(h_lo, G - 2)
                for g in (G - 2, G - 1):
                    sl = slice(g * GROUP, (g + 1) * GROUP)
                    dve.wait_ge(a_hh, g + 1)
                    nc.vector.tensor_tensor(slots_lo[:, :, sl], h_banks(g)[:, :, :], slots_hi[:, :, sl].bitcast(F32),
                                            ALU.subtract).then_inc(h_lo, 1)
                for i in range(2):
                    dve.wait_ge(w_rows[i], 16 * G // 2)
                dve.wait_ge(t_h, G)
                st.add(nc.vector.memset(ones[:, :], 1.0))
                st.add(nc.vector.memset(thr[:, :], 0))
                st.do(nc.vector.memset(bit[:, :], 1 << 29))
                dve.sem_inc(v_hid, 2)
                dve.wait_ge(a_sg, 1)

                def bisect_count(u):
                    nc.vector.tensor_scalar(cand[:, :], bit[:, :], thr[:, 0:1], None, ALU.bitwise_or).then_inc(v_bis, 1)
                    dve.wait_ge(v_bis, 3 * u + 1)
                    nc.vector.tensor_scalar(slot[:, :], sg[:, :], cand[:, 0:1].bitcast(F32), 0.0, ALU.is_ge, ALU.add,
                                            accum_out=cnt[:, :]).then_inc(v_cnt, 1)

                def bisect_keep(u):
                    dve.wait_ge(m_cnt, u + 1)
                    nc.vector.tensor_scalar(keep[:, :], small[:, 0:1], float(CAP), -1.0, ALU.is_ge,
                                            ALU.mult).then_inc(v_bis, 1)
                    dve.wait_ge(v_bis, 3 * u + 2)
                    nc.vector.scalar_tensor_tensor(thr[:, :], keep[:, :], bit[:, 0:1], thr[:, :], ALU.bitwise_and,
                                                   ALU.bitwise_or).then_inc(v_bis, 1)
                    dve.wait_ge(v_bis, 3 * u + 3)
                    nc.vector.tensor_scalar(bit[:, :], bit[:, :], 1, None, ALU.logical_shift_right).then_inc(v_bit, 1)
                    dve.wait_ge(v_bit, u + 1)

                def hidden(n, f):
                    dve.wait_ge(m_u, n + 1)
                    dve.wait_ge(a_silu, n + 3)
                    dve.wait_ge(a_hid, n + 1)
                    dve.wait_ge(p_lo, n + 1)
                    nc.vector.tensor_tensor(hid[:, f % 2, :], silu[:, f % 2, :], wide[:, 2 + f % 2, :],
                                            ALU.mult).then_inc(v_hid, 1)

                hidden(0, 0)
                hidden(1, 1)
                with dve.Fori(0, G_BIS) as g:
                    for f in range(FS):
                        u = (g * FS + f) * 2
                        bisect_count(u)
                        bisect_keep(u)
                        bisect_count(u + 1)
                        hidden(g * FS + f + LAG, f + LAG)
                        bisect_keep(u + 1)

                thr_f = thr[:, 0:1].bitcast(F32)
                n = G_BIS * FS + LAG
                st.add(nc.vector.tensor_scalar(above[:, :], sg[:, :], thr_f, 0.0, ALU.is_gt, ALU.add,
                                               accum_out=tots[:, 0:1]))
                st.do(nc.vector.tensor_scalar(tie[:, :], sg[:, :], thr_f, None, ALU.is_equal))
                st.do(nc.vector.tensor_tensor_scan(count[:, :], ones[:, :], tie[:, :], 0.0, ALU.mult, ALU.add))
                st.do(nc.vector.tensor_copy(tots[:, 1:2], count[:, GROUP - 1:GROUP]))
                dve.sem_inc(v_tot, 1)
                hidden(n, 0)
                dve.wait_ge(m_tot, 1)
                st.add(nc.vector.tensor_scalar(offs[:, 0:1], small[:, 1:2], -1.0, float(CAP), ALU.mult, ALU.add))
                st.do(nc.vector.tensor_copy(offs[:, 1:2], small[:, 2:3]))
                st.do(nc.vector.tensor_scalar(taken[:, :], count[:, :], offs[:, 1:2], offs[:, 0:1], ALU.add, ALU.is_le))
                st.do(nc.vector.tensor_tensor(taken[:, :], taken[:, :], tie[:, :], ALU.mult))
                st.do(nc.vector.tensor_tensor(taken[:, :], taken[:, :], above[:, :], ALU.add))
                st.do(nc.vector.tensor_tensor_scan(count[:, :], ones[:, :], taken[:, :], 0.0, ALU.mult, ALU.add))
                st.do(nc.vector.tensor_copy(tots[:, 2:3], count[:, GROUP - 1:GROUP]))
                dve.sem_inc(v_tot, 1)
                hidden(n + 1, 1)
                dve.wait_ge(m_tot, 2)
                st.do(nc.vector.tensor_scalar(offs[:, 2:3], small[:, 3:4], -1.0 - BIG, None, ALU.add))
                st.do(nc.vector.scalar_tensor_tensor(slot[:, :], count[:, :], offs[:, 2:3], taken[:, :], ALU.add,
                                                     ALU.mult))
                nc.vector.tensor_scalar(slot[:, :], slot[:, :], BIG, None, ALU.add).then_inc(v_slot, 1)
                hidden(n + 2, 2)
                dve.wait_ge(t_slot, 1)
                st.do(nc.vector.tensor_copy(slot_i[:, :], logit[:, :]))
                st.add(nc.vector.tensor_scalar(hi_i[:, :], slot_i[:, :], 4, None, ALU.logical_shift_right))
                st.do(nc.vector.tensor_scalar(lo_i[:, :], slot_i[:, :], BW - 1, None, ALU.bitwise_and))
                st.add(nc.vector.tensor_copy(hi_f[:, :], hi_i[:, :]))
                st.do(nc.vector.tensor_copy(lo_f[:, :], lo_i[:, :]))
                hidden(n + 3, 3)
                dve.wait_ge(p2, 3 + 2 * G + 4)
                dve.wait_ge(p_y, G_BIS)
                for i in range(W // HOT):
                    ws = slice(i * HOT * E, (i + 1) * HOT * E)
                    for hot, dig, width in ((hot_b[:, i * HOT:(i + 1) * HOT, :], lo_f, BW),
                                            (hot_a[i][:, :, :], hi_f, AW)):
                        nc.vector.tensor_tensor(
                            hot.rearrange("p w (e a) -> p (w e) a", e=E),
                            dig[:, ws].rearrange("p (t a) -> p t a", a=1).to_broadcast([P, HOT * E, width]),
                            iota_f[:, 0:width].rearrange("p (a w) -> p a w", a=1).to_broadcast([P, HOT * E, width]),
                            ALU.is_equal).then_inc(v_hot, 1)
                    hidden(n + 4 + i, i % FS)
                hidden(G * FS - 2, FS - 2)
                dve.wait_ge(m_ids, 1)
                for f in range(BLK):
                    pr = slice(f * AW, (f + 1) * AW)
                    last = nc.vector.tensor_scalar(
                        ids_sb[pr, :, :], small[pr, 0:E * BW].rearrange("p (q f b) -> p q f b", f=BLK, b=BW)[:, :, f, :],
                        float(HALF_T), None, ALU.add)
                last.then_inc(v_ids, 1)
                hidden(G * FS - 1, FS - 1)
                dve.wait_ge(a_y, G + 1)
                plus_x1(nc.vector, G - 1)
        state.close()
        RING = 4
        AHEAD = 5
        with ExitStack() as experts:
            lsb, lps = tensors(experts)
            w_hi = lsb("w_hi", [P, FE, WCOL], F32R)
            w_lo = lsb("w_lo", [P, FE, WCOL], F32R)
            b_gate = lsb("b_gate", [P, E, FE])
            b_up = lsb("b_up", [P, E, FE])
            b_down = lsb("b_down", [P, E, D])
            idx_out = lsb("idx_out", [P, BLK], U32)
            xt_hi = lsb("xt_hi", [P, KC, GROUP], F32R)
            xt_lo = lsb("xt_lo", [P, KC, GROUP], F32R)
            esilu = lsb("esilu", [P, 2, GROUP])
            ehid = lsb("ehid", [P, 2, GROUP])
            eh_hi = lsb("eh_hi", [P, RING, GROUP], F32R)
            eh_lo = lsb("eh_lo", [P, RING, GROUP], F32R)
            weight = lsb("weight", [P, BLK, 1])
            yo = lsb("yo", [P, BLK, D])
            egate = lps("egate", [P, 2, 512])
            eup = lps("eup", [P, 2, 512])
            edown = lps("edown", [P, 2, 512])
            exps = lps("exps", [P, KC, 512])

            l_b = sem("l_b")
            p_out, p_step, p_sums = sem("p_out"), sem("p_step"), sem("p_sums")
            g_add = sem("scattered")
            t_xt, a_xt, v_xt, v_wt = sem("t_xt"), sem("a_xt"), sem("v_xt"), sem("v_wt")
            a_w, v_w = sem("a_w"), sem("v_w")
            k_g, k_u, k_silu, k_hid, k_hi, k_lo, k_dn = (sem(f"k_{n}") for n in ("g", "u", "silu", "hid", "hi", "lo", "dn"))
            k_out, k_yo = sem("k_out"), sem("k_yo")
            block = experts.enter_context(nc.Block())

            def half_slice(h):
                return slice(h * HALF_F, (h + 1) * HALF_F)

            @block.sync
            def _(sp):
                sp.dma_start(b_gate[:, :, :], gate_b).then_inc(l_b, 16)
                sp.dma_start(b_up[:, :, :], up_b).then_inc(l_b, 16)
                sp.dma_start(b_down[:, :, :], down_b.rearrange("(a e) d -> a e d", a=1).to_broadcast([P, E, D]))\
                    .then_inc(l_b, 16)
                with sp.Fori(0, E - 1) as e:
                    for h in range(2):
                        sp.wait_ge(a_w, e * FE + (h + 1) * HALF_F)
                        sp.wait_ge(v_w, e * FE + (h + 1) * HALF_F)
                        sp.dma_start(raw[:, half_slice(h), :],
                                     w_expert[bass.ds(e + 1, 1), :, half_slice(h), :].rearrange("a p f n -> p (a f) n"))\
                            .then_inc(l_w[h], 16)

            @block.gpsimd
            def _(pool):
                def gather(e):
                    nc.gpsimd.tensor_copy(idx_in[:, :], idx_all[:, bass.ds(e, 1), :].rearrange("p a j -> p (a j)"))\
                        .then_inc(p_idx, 1)
                    pool.wait_ge(p_idx, e + 1)
                    pool.sem_inc(p_step, 1)
                    for j in range(BLK):
                        pool.indirect_dma_start(got[:, j, :], None, rows,
                                                bass.IndirectOffsetOnAxis(idx_in[:, j:j + 1], 0)).then_inc(g_in_, 16)

                def turn_of(e, more):
                    pool.wait_ge(g_in_, 16 * BLK * (e + 1))
                    pool.sem_inc(p_step, 1)
                    nc.gpsimd.tensor_copy(idx_out[:, :], idx_in[:, :]).then_inc(p_out, 1)
                    if more:
                        pool.wait_ge(p_out, e + 1)
                        pool.wait_ge(t_xt, e + 1)
                        pool.wait_ge(v_wt, e + 1)
                        pool.sem_inc(p_step, 1)
                        gather(e + 1)
                    pool.wait_ge(k_yo, e + 1)
                    pool.wait_ge(p_out, e + 1)
                    pool.sem_inc(p_step, 1)
                    for j in range(BLK):
                        if not more and j > 0:
                            pool.wait_ge(k_yo, e + 1 + j)
                        pool.indirect_dma_start(out, bass.IndirectOffsetOnAxis(idx_out[:, j:j + 1], 0), yo[:, j, :],
                                                None, compute_op=ALU.add).then_inc(g_add, 16)
                    pool.wait_ge(g_add, 16 * BLK * (e + 1))
                    pool.sem_inc(p_sums, 1)

                pool.wait_ge(w_y, 16 * G + 1)
                pool.sem_inc(p_sums, 1)
                with pool.Fori(0, E - 1) as e:
                    turn_of(e, True)
                turn_of(E - 1, False)

            @block.tensor
            def _(pe):
                def turn_rows(e):
                    pe.wait_ge(g_in_, 16 * BLK * (e + 1))
                    for k in range(KC):
                        for j in range(BLK):
                            last = nc.tensor.transpose(exps[:, k, j * P:(j + 1) * P], got[:, j, k * P:(k + 1) * P],
                                                       ident[:, :])
                    last.then_inc(t_xt, 1)

                def into_hidden(e, f):
                    n = e * FE + f
                    pe.wait_ge(a_w, n + 1)
                    pe.wait_ge(v_w, n + 1)
                    for bank, free, done, c in ((egate, k_silu, k_g, 0), (eup, k_hid, k_u, 2)):
                        pe.wait_ge(free, n + 1)
                        m = 0
                        for k in range(KC):
                            for w, x_ in ((w_hi, xt_hi), (w_hi, xt_lo), (w_lo, xt_hi)):
                                m += 1
                                last = nc.tensor.matmul(bank[:, f % 2, :], w[:, f, (c + k) * P:(c + k + 1) * P], x_[:, k, :],
                                                        start=(m == 1), stop=(m == 3 * KC))
                        last.then_inc(done, 1)

                def out_of_hidden(e, f):
                    n = e * FE + f
                    pe.wait_ge(k_lo, n + 1)
                    if f == 0:
                        pe.wait_ge(k_out, BLK * e + 1)
                    for j in range(BLK):
                        tok = slice(j * P, (j + 1) * P)
                        for m, (h, w) in enumerate(((eh_hi, w_hi), (eh_lo, w_hi), (eh_hi, w_lo))):
                            last = nc.tensor.matmul(edown[:, j // 2, (j % 2) * D:(j % 2 + 1) * D], h[:, f % RING, tok],
                                                    w[:, f, 4 * P:6 * P], start=(f == 0 and m == 0 and j % 2 == 0),
                                                    stop=(f == FE - 1 and m == 2), skip_group_check=True)
                    last.then_inc(k_dn, 1)

                def expert(e, more):
                    pe.wait_ge(a_xt, e + 1)
                    pe.wait_ge(v_xt, e + 1)
                    for f in range(FE):
                        into_hidden(e, f)
                        if f >= LAG:
                            out_of_hidden(e, f - LAG)
                    if more:
                        turn_rows(e + 1)
                    for f in range(FE - LAG, FE):
                        out_of_hidden(e, f)

                pe.sem_inc(k_dn, FE)
                turn_rows(0)
                with pe.Fori(0, E - 1) as e:
                    expert(e, True)
                expert(E - 1, False)

            @block.scalar
            def _(act):
                def split(e, f):
                    if f % HALF_F == 0:
                        act.wait_ge(l_w[f // HALF_F], 16 * (e + 1))
                    act.wait_ge(k_dn, e * FE + f + 1)
                    nc.scalar.activation(w_hi[:, f, :], raw[:, f, :], ACT.Copy).then_inc(a_w, 1)

                def rows_hi(e):
                    act.wait_ge(t_xt, e + 1)
                    nc.scalar.activation(xt_hi[:, :, :], exps[:, :, :], ACT.Copy).then_inc(a_xt, 1)

                def expert(e, more):
                    for f in range(FE):
                        n = e * FE + f
                        act.wait_ge(k_g, n + 1)
                        act.wait_ge(k_hid, n + 1)
                        nc.scalar.activation(esilu[:, f % 2, :], egate[:, f % 2, :], ACT.Silu,
                                             bias=b_gate[:, bass.ds(e, 1), f:f + 1].rearrange("p a b -> p (a b)"))\
                            .then_inc(k_silu, 1)
                        if f < FE - AHEAD:
                            split(e, f + AHEAD)
                        elif more:
                            split(e + 1, f - (FE - AHEAD))
                        act.wait_ge(k_hid, n + 3)
                        act.wait_ge(k_dn, n + 1 + FE - RING)
                        nc.scalar.activation(eh_hi[:, f % RING, :], ehid[:, f % 2, :], ACT.Copy).then_inc(k_hi, 1)
                    if more:
                        rows_hi(e + 1)

                act.sem_inc(k_silu, 2)
                act.sem_inc(k_hi, 2)
                split(0, 0)
                rows_hi(0)
                for f in range(1, AHEAD):
                    split(0, f)
                nc.scalar.preload_act_table(ACT.Silu)
                act.wait_ge(l_b, 48)
                with act.Fori(0, E - 1) as e:
                    expert(e, True)
                expert(E - 1, False)

            @block.vector
            def _(dve):
                def split(e, f):
                    dve.wait_ge(a_w, e * FE + f + 1)
                    nc.vector.tensor_tensor(w_lo[:, f, :], raw[:, f, :], w_hi[:, f, :].bitcast(F32),
                                            ALU.subtract).then_inc(v_w, 1)

                def rows_lo(e):
                    dve.wait_ge(a_xt, e + 1)
                    nc.vector.tensor_tensor(xt_lo[:, :, :], exps[:, :, :], xt_hi[:, :, :].bitcast(F32),
                                            ALU.subtract).then_inc(v_xt, 1)

                def take_scores(e, first=False):
                    if not first:
                        dve.wait_ge(k_yo, e)
                    nc.vector.tensor_scalar(weight[:, :, :], got[:, :, bass.ds(D + e, 1)], tanh_g[:, 1:2], None,
                                            ALU.mult).then_inc(v_wt, 1)

                def results(e, more):
                    def add_bias(j):
                        nc.vector.tensor_tensor(yo[:, j, :], edown[:, j // 2, (j % 2) * D:(j % 2 + 1) * D],
                                                b_down[:, bass.ds(e, 1), :].rearrange("p a d -> p (a d)"),
                                                ALU.add).then_inc(k_out, 1)

                    def scale(j):
                        return nc.vector.tensor_scalar(yo[:, j, :], yo[:, j, :], weight[:, j, :], None, ALU.mult)

                    dve.wait_ge(k_dn, (e + 2) * FE)
                    dve.wait_ge(p_sums, e + 1)
                    dve.wait_ge(v_wt, e + 1)
                    if more:
                        for j in range(BLK):
                            add_bias(j)
                        dve.wait_ge(k_out, BLK * (e + 1) + 1)
                        for j in range(BLK):
                            last = scale(j)
                        last.then_inc(k_yo, 1)
                    else:
                        add_bias(0)
                        for j in range(BLK):
                            if j + 1 < BLK:
                                add_bias(j + 1)
                            dve.wait_ge(k_out, BLK * e + j + 2)
                            scale(j).then_inc(k_yo, 1)

                def expert(e, more):
                    for f in range(FE):
                        n = e * FE + f
                        dve.wait_ge(k_u, n + 1)
                        dve.wait_ge(k_silu, n + 3)
                        dve.wait_ge(k_hi, n + 1)
                        nc.vector.scalar_tensor_tensor(
                            ehid[:, f % 2, :], eup[:, f % 2, :], b_up[:, bass.ds(e, 1), f:f + 1].rearrange("p a b -> p (a b)"),
                            esilu[:, f % 2, :], ALU.add, ALU.mult).then_inc(k_hid, 1)
                        if f < FE - AHEAD:
                            split(e, f + AHEAD)
                        elif more:
                            split(e + 1, f - (FE - AHEAD))
                        dve.wait_ge(k_hi, n + 3)
                        nc.vector.tensor_tensor(eh_lo[:, f % RING, :], ehid[:, f % 2, :],
                                                eh_hi[:, f % RING, :].bitcast(F32), ALU.subtract).then_inc(k_lo, 1)
                    if more:
                        rows_lo(e + 1)
                    results(e, more)
                    if more:
                        take_scores(e + 1)

                dve.sem_inc(k_out, 1)
                dve.sem_inc(k_hid, 2)
                split(0, 0)
                rows_lo(0)
                for f in range(1, AHEAD):
                    split(0, f)
                take_scores(0, first=True)
                dve.wait_ge(l_b, 48)
                with dve.Fori(0, E - 1) as e:
                    expert(e, True)
                expert(E - 1, False)


V_PN = 1 + 11 + 2


def _columns(v):
    import numpy as _np
    return _np.ascontiguousarray(_np.swapaxes(v.reshape(v.shape[:-1] + (-1, P)), -1, -2))


def _ffn_layout(gate, up, down):
    import numpy as _np
    f, d = gate.shape
    blocks, chunks = f // P, d // P
    into = [w.T.reshape(chunks, P, blocks, P)[k] for w in (gate, up) for k in range(chunks)]
    return _np.concatenate(into + [down.T.reshape(blocks, P, d).transpose(1, 0, 2)], axis=-1)


def kernel(x, ctx_1024, g_xattn, g_ffn, L0_xattn_Wq, L0_xattn_Wk, L0_xattn_Wv, L0_xattn_gru_wih, L0_xattn_gru_whh,
           L0_xattn_gru_bih, L0_xattn_gru_bhh, L0_xattn_slot_norm_w, L0_xattn_input_norm_w, L0_ffn_gate_w, L0_ffn_up_w,
           L0_ffn_up_b, L0_ffn_gw, L0_ffn_gb, L0_ffn_down_w, L0_ffn_down_b, L0_ffn_sh_gate_w, L0_ffn_sh_up_w,
           L0_ffn_sh_down_w):
    import numpy as _np
    import concourse.bacc as _bacc
    from concourse.bass_utils import run_bass_kernel_spmd as _run

    x = _np.asarray(x)
    ctx_1024 = _np.asarray(ctx_1024)
    d = x.shape[-1]
    host = {
        "x": x.reshape(-1, d),
        "ctx_tok": ctx_1024.reshape(-1, d),
        "tanh_in": _np.concatenate([_np.asarray(g_xattn), _np.asarray(g_ffn)]),
        "wq": L0_xattn_Wq,
        "wk_t": _np.asarray(L0_xattn_Wk).T,
        "wv_t": _np.asarray(L0_xattn_Wv).T,
        "wih_t": _np.asarray(L0_xattn_gru_wih).T,
        "whh_t": _np.asarray(L0_xattn_gru_whh).T,
        "vectors": _np.concatenate([_columns(_np.asarray(v)) for v in (
            L0_xattn_gru_bih, L0_xattn_gru_bhh, L0_xattn_slot_norm_w, L0_xattn_input_norm_w)], axis=1),
        "gate_t": _np.asarray(L0_ffn_gate_w).T,
        "w_expert": _np.stack([_ffn_layout(*w) for w in zip(_np.asarray(L0_ffn_gw), _np.asarray(L0_ffn_up_w),
                                                            _np.asarray(L0_ffn_down_w))]),
        "gate_b": _columns(_np.asarray(L0_ffn_gb)).transpose(1, 0, 2),
        "up_b": _columns(_np.asarray(L0_ffn_up_b)).transpose(1, 0, 2),
        "down_b": L0_ffn_down_b,
        "w_shared": _ffn_layout(_np.asarray(L0_ffn_sh_gate_w), _np.asarray(L0_ffn_sh_up_w),
                                _np.asarray(L0_ffn_sh_down_w)),
    }
    nc = _bacc.Bacc("TRN2", target_bir_lowering=False, num_devices=1)
    arrays, args = {}, {}
    for name, a in host.items():
        a = _np.ascontiguousarray(a)
        arrays[f"in_{name}"] = a
        args[name] = nc.dram_tensor(f"in_{name}", a.shape, mybir.dt.from_np(a.dtype), kind="ExternalInput").ap()
    out = nc.dram_tensor("out_tokens", host["x"].shape, F32, kind="ExternalOutput").ap()
    flamingo_kernel(nc, **args, out=out)
    r = _run(nc, [arrays], core_ids=[0])
    return r.results[0]["out_tokens"].reshape(x.shape)
```
